# Optimizing a Trainium2 kernel written in Bass

```python
import numpy as np
import jax
import jax.numpy as jnp

def _softmax(x, axis=-1):
    return jax.nn.softmax(x, axis=axis)

def _gelu(x):
    return jax.nn.gelu(x, approximate=True)

def _silu(x):
    return jax.nn.silu(x)

def _sigmoid(x):
    return jax.nn.sigmoid(x)

def _layernorm(x, axis=-1, eps=1e-05):
    m = jnp.mean(x, axis=axis, keepdims=True)
    v = jnp.var(x, axis=axis, keepdims=True)
    return (x - m) / jnp.sqrt(v + eps)

def _scatter_add(tgt, idx, src, axis=0):
    return tgt.at[idx].add(src)

def _segment_sum(src, seg, n):
    return jax.ops.segment_sum(src, seg, n)
kernel_name = 'mk_decoder_postln_d2_seqx_r8_91451c'

def setup_inputs(seed: int=0):
    np.random.seed(seed)
    _w = jnp.asarray

    def _rec_inputs():
        import jax
        import jax.numpy as jnp
        _rk = jax.random.key(seed)
        x = -0.0002928 + 1 * jax.random.normal(jax.random.fold_in(_rk, 1), (8, 128, 128), jnp.float32)
        _lenS = 128 - jax.random.randint(jax.random.fold_in(_rk, 7), (8,), 0, max(1, 128 // 4) + 1, jnp.int32)
        _lenS2 = 77 - jax.random.randint(jax.random.fold_in(_rk, 8), (8,), 0, max(1, 77 // 4) + 1, jnp.int32)
        _ctx_1024P = jax.random.normal(jax.random.fold_in(_rk, 11), (8, 16, 128), jnp.float32)
        _ctx_1024c = jax.random.dirichlet(jax.random.fold_in(_rk, 511), 0.3 * jnp.ones((16,), jnp.float32), (8, 77))
        _ctx_1024t = jnp.einsum('bsk,bkd->bsd', _ctx_1024c, _ctx_1024P)
        _ctx_1024t = _ctx_1024t * jax.lax.rsqrt(jnp.mean(jnp.square(_ctx_1024t)) + 1e-12) * 0.953939
        ctx_1024 = -1.39393e-06 + 0.999914 * (_ctx_1024t + 0.3 * jax.random.normal(jax.random.fold_in(_rk, 611), (8, 77, 128), jnp.float32))
        _validS = jnp.arange(128)[None, :] < _lenS[:, None]
        _validS2 = jnp.arange(77)[None, :] < _lenS2[:, None]
        _causal = jnp.tril(jnp.ones((128, 128), dtype=bool))
        mask_1x1xSxS2_bk1 = jnp.broadcast_to(_validS2[0:1, None, None, :], (1, 1, 128, 77))
        return (x, ctx_1024, mask_1x1xSxS2_bk1)
    x, ctx_1024, mask_1x1xSxS2_bk1 = _rec_inputs()

    def _L0_attn_setup():
        import jax, jax.numpy as jnp
        import numpy as np
        D_MODEL = 128
        NUM_HEADS = 16
        HEAD_DIM = D_MODEL // NUM_HEADS
        key = jax.random.key(seed)
        ks = jax.random.split(key, 7)
        B, T, C = (4, 256, D_MODEL)
        s = 1.0 / np.sqrt(C)
        return {'x': jax.random.normal(ks[0], (B, T, C), dtype=jnp.float32), 'ln_gamma': jnp.ones((C,), dtype=jnp.float32), 'ln_beta': jnp.zeros((C,), dtype=jnp.float32), 'w_qkv': jax.random.normal(ks[1], (C, 3 * C), dtype=jnp.float32) * s, 'b_qkv': jnp.zeros((3 * C,), dtype=jnp.float32), 'w_out': jax.random.normal(ks[2], (C, C), dtype=jnp.float32) * s, 'b_out': jnp.zeros((C,), dtype=jnp.float32)}
    _L0_attn_all = _L0_attn_setup()
    _L0_attn_in = {k: v for k, v in _L0_attn_all.items() if k in ('ln_gamma', 'ln_beta', 'w_qkv', 'b_qkv', 'w_out', 'b_out')}
    del _L0_attn_all

    def _L0_xattn_setup():
        import jax, jax.numpy as jnp
        import numpy as np
        NUM_HEADS = 16
        D_MODEL = 128
        HEAD_DIM = D_MODEL // NUM_HEADS
        SCALE = float(np.sqrt(HEAD_DIM))
        EPS = 1e-05

        def layernorm(x, g, b):
            mu = jnp.mean(x, axis=-1, keepdims=True)
            var = jnp.mean(jnp.square(x - mu), axis=-1, keepdims=True)
            return (x - mu) * jax.lax.rsqrt(var + EPS) * g + b
        key = jax.random.key(seed)
        ks = jax.random.split(key, 8)
        B, Nq, Nc = (2, 256, 256)
        s = 0.02
        return {'x_query': jax.random.normal(ks[0], (B, Nq, D_MODEL), jnp.float32), 'x_context': jax.random.normal(ks[1], (B, Nc, D_MODEL), jnp.float32), 'Wq': jax.random.normal(ks[2], (D_MODEL, D_MODEL), jnp.float32) * s, 'Wkv': jax.random.normal(ks[3], (D_MODEL, 2 * D_MODEL), jnp.float32) * s, 'Wp': jax.random.normal(ks[4], (D_MODEL, D_MODEL), jnp.float32) * s, 'bp': jnp.zeros((D_MODEL,), jnp.float32), 'ln_g': jnp.ones((HEAD_DIM,), jnp.float32), 'ln_b': jnp.zeros((HEAD_DIM,), jnp.float32)}
    _L0_xattn_all = _L0_xattn_setup()
    _L0_xattn_in = {k: v for k, v in _L0_xattn_all.items() if k in ('Wq', 'Wkv', 'Wp', 'bp', 'ln_g', 'ln_b')}
    del _L0_xattn_all

    def _L0_ffn_setup():
        import jax, jax.numpy as jnp
        import numpy as np
        TOP_K = 2
        key = jax.random.key(seed)
        ks = jax.random.split(key, 6)
        B, S, D, BN, E = (32, 256, 128, 64, 8)
        return {'x': jax.random.normal(ks[0], (B, S, D), dtype=jnp.float32), 'gate_w': jax.random.normal(ks[1], (E, D), dtype=jnp.float32) * 0.02, 'down_w': jax.random.normal(ks[2], (E, BN, D), dtype=jnp.float32) * 0.02, 'down_b': jax.random.normal(ks[3], (E, BN), dtype=jnp.float32) * 0.02, 'up_w': jax.random.normal(ks[4], (E, D, BN), dtype=jnp.float32) * 0.02, 'up_b': jax.random.normal(ks[5], (E, D), dtype=jnp.float32) * 0.02}
    _L0_ffn_all = _L0_ffn_setup()
    _L0_ffn_in = {k: v for k, v in _L0_ffn_all.items() if k in ('gate_w', 'down_w', 'down_b', 'up_w', 'up_b')}
    del _L0_ffn_all

    def _L1_attn_setup():
        import jax, jax.numpy as jnp
        import numpy as np
        B, T, D = (4, 128, 128)
        H = 16
        DS, DC, EXP = (16, 4, 2)
        DIN = EXP * D
        DTR = D // 16
        TOPK_RATIO = 0.25
        EPS = 1e-05

        def _attn_core(x, Wq, bq, Wk, bk, Wv, bv, Wo, bo):
            b, L, d = x.shape
            hd = d // H
            q = (x @ Wq + bq).reshape(b, L, H, hd)
            k = (x @ Wk + bk).reshape(b, L, H, hd)
            v = (x @ Wv + bv).reshape(b, L, H, hd)
            scores = jnp.einsum('bqhd,bkhd->bhqk', q, k) / jnp.sqrt(jnp.float32(hd))
            p = jax.nn.softmax(scores, axis=-1)
            o = jnp.einsum('bhqk,bkhd->bqhd', p, v).reshape(b, L, d)
            return o @ Wo + bo

        def _ssm_core(u, in_w, conv_w, conv_b, xproj_w, dt_w, dt_b, A_log, Dp, out_w):
            b, L, _ = u.shape
            xi, z = jnp.split(u @ in_w, 2, axis=-1)
            xp = jnp.pad(xi, ((0, 0), (DC - 1, 0), (0, 0)))
            xc = conv_b + sum((xp[:, j:j + L] * conv_w[:, j] for j in range(DC)))
            xc = jax.nn.silu(xc)
            proj = xc @ xproj_w
            dtp = proj[..., :DTR]
            Bm = proj[..., DTR:DTR + DS]
            Cm = proj[..., DTR + DS:]
            delta = jax.nn.softplus(dtp @ dt_w + dt_b)
            A = -jnp.exp(A_log)
            dA = jnp.exp(delta[..., None] * A)
            dBu = (delta * xc)[..., None] * Bm[:, :, None, :]

            def step(h, inp):
                dA_t, dBu_t, C_t = inp
                h = dA_t * h + dBu_t
                return (h, jnp.einsum('bds,bs->bd', h, C_t))
            xs = (jnp.moveaxis(dA, 1, 0), jnp.moveaxis(dBu, 1, 0), jnp.moveaxis(Cm, 1, 0))
            _, ys = jax.lax.scan(step, jnp.zeros((b, DIN, DS), u.dtype), xs)
            y = jnp.moveaxis(ys, 0, 1) + xc * Dp
            y = y * jax.nn.silu(z)
            return y @ out_w
        key = jax.random.key(seed)
        ks = jax.random.split(key, 16)

        def n(k, shape, scale=0.02):
            return jax.random.normal(k, shape, jnp.float32) * scale
        return {'x': jax.random.normal(ks[0], (B, T, D), jnp.float32), 'ln_w': jnp.ones((D,), jnp.float32), 'ln_b': jnp.zeros((D,), jnp.float32), 'r_w1': n(ks[1], (D, D // 2)), 'r_b1': jnp.zeros((D // 2,), jnp.float32), 'r_w2': n(ks[2], (D // 2, 1)), 'r_b2': jnp.zeros((1,), jnp.float32), 'Wq': n(ks[3], (D, D)), 'bq': jnp.zeros((D,), jnp.float32), 'Wk': n(ks[4], (D, D)), 'bk': jnp.zeros((D,), jnp.float32), 'Wv': n(ks[5], (D, D)), 'bv': jnp.zeros((D,), jnp.float32), 'Wo': n(ks[6], (D, D)), 'bo': jnp.zeros((D,), jnp.float32), 'in_w': n(ks[7], (D, 2 * DIN)), 'conv_w': n(ks[8], (DIN, DC), 0.1), 'conv_b': jnp.zeros((DIN,), jnp.float32), 'xproj_w': n(ks[9], (DIN, DTR + 2 * DS)), 'dt_w': n(ks[10], (DTR, DIN), 0.1), 'dt_b': jnp.full((DIN,), -4.0, jnp.float32) + n(ks[11], (DIN,), 0.1), 'A_log': jnp.log(jnp.broadcast_to(jnp.arange(1, DS + 1, dtype=jnp.float32), (DIN, DS))), 'Dp': jnp.ones((DIN,), jnp.float32), 'out_w': n(ks[12], (DIN, D))}
    _L1_attn_all = _L1_attn_setup()
    _L1_attn_in = {k: v for k, v in _L1_attn_all.items() if k in ('ln_w', 'ln_b', 'r_w1', 'r_b1', 'r_w2', 'r_b2', 'Wq', 'bq', 'Wk', 'bk', 'Wv', 'bv', 'Wo', 'bo', 'in_w', 'conv_w', 'conv_b', 'xproj_w', 'dt_w', 'dt_b', 'A_log', 'Dp', 'out_w')}
    del _L1_attn_all

    def _L1_xattn_setup():
        import jax, jax.numpy as jnp
        import numpy as np
        D_MODEL = 128
        NUM_HEADS = 16
        D_K = D_MODEL // NUM_HEADS

        def _split(x):
            B, S, _ = x.shape
            return x.reshape(B, S, NUM_HEADS, D_K).transpose(0, 2, 1, 3)
        key = jax.random.key(seed)
        ks = jax.random.split(key, 8)
        B, S = (2, 256)
        query = jax.random.normal(ks[0], (B, S, D_MODEL), dtype=jnp.float32)
        k_in = jax.random.normal(ks[1], (B, S, D_MODEL), dtype=jnp.float32)
        value = jax.random.normal(ks[2], (B, S, D_MODEL), dtype=jnp.float32)
        mask = jnp.triu(jnp.ones((S, S), dtype=bool), k=1)[None, None, :, :]
        scale = 1.0 / np.sqrt(D_MODEL)
        W_q = jax.random.normal(ks[3], (D_MODEL, D_MODEL), dtype=jnp.float32) * scale
        W_k = jax.random.normal(ks[4], (D_MODEL, D_MODEL), dtype=jnp.float32) * scale
        W_v = jax.random.normal(ks[5], (D_MODEL, D_MODEL), dtype=jnp.float32) * scale
        W_o = jax.random.normal(ks[6], (D_MODEL, D_MODEL), dtype=jnp.float32) * scale
        return {'query': query, 'key': k_in, 'value': value, 'mask': mask, 'W_q': W_q, 'W_k': W_k, 'W_v': W_v, 'W_o': W_o}
    _L1_xattn_all = _L1_xattn_setup()
    _L1_xattn_in = {k: v for k, v in _L1_xattn_all.items() if k in ('W_q', 'W_k', 'W_v', 'W_o')}
    del _L1_xattn_all

    def _L1_ffn_setup():
        import jax, jax.numpy as jnp
        import numpy as np
        B, S, D = (4, 512, 128)
        E, I = (8, 256)
        CAPACITY = 2
        K = max(1, int(S / E * CAPACITY))
        key = jax.random.key(seed)
        k1, k2, k3, k4, k5 = jax.random.split(key, 5)
        x = jax.random.normal(k1, (B, S, D), dtype=jnp.float32)
        gate_w = jax.random.normal(k2, (D, E), dtype=jnp.float32) * 0.006
        Wg = jax.random.normal(k3, (E, D, I), dtype=jnp.float32) * 0.02
        Wu = jax.random.normal(k4, (E, D, I), dtype=jnp.float32) * 0.02
        Wd = jax.random.normal(k5, (E, I, D), dtype=jnp.float32) * 0.02
        return {'x': x, 'gate_w': gate_w, 'Wg': Wg, 'Wu': Wu, 'Wd': Wd}
    _L1_ffn_all = _L1_ffn_setup()
    _L1_ffn_in = {k: v for k, v in _L1_ffn_all.items() if k in ('gate_w', 'Wg', 'Wu', 'Wd')}
    del _L1_ffn_all
    return {'x': x, 'ctx_1024': ctx_1024, 'mask_1x1xSxS2_bk1': mask_1x1xSxS2_bk1, 'L0_attn_ln_gamma': _L0_attn_in['ln_gamma'], 'L0_attn_ln_beta': _L0_attn_in['ln_beta'], 'L0_attn_w_qkv': _L0_attn_in['w_qkv'], 'L0_attn_b_qkv': _L0_attn_in['b_qkv'], 'L0_attn_w_out': _L0_attn_in['w_out'], 'L0_attn_b_out': _L0_attn_in['b_out'], 'L0_xattn_Wq': _L0_xattn_in['Wq'], 'L0_xattn_Wkv': _L0_xattn_in['Wkv'], 'L0_xattn_Wp': _L0_xattn_in['Wp'], 'L0_xattn_bp': _L0_xattn_in['bp'], 'L0_xattn_ln_g': _L0_xattn_in['ln_g'], 'L0_xattn_ln_b': _L0_xattn_in['ln_b'], 'L0_ffn_gate_w': _L0_ffn_in['gate_w'], 'L0_ffn_down_w': _L0_ffn_in['down_w'], 'L0_ffn_down_b': _L0_ffn_in['down_b'], 'L0_ffn_up_w': _L0_ffn_in['up_w'], 'L0_ffn_up_b': _L0_ffn_in['up_b'], 'L1_attn_ln_w': _L1_attn_in['ln_w'], 'L1_attn_ln_b': _L1_attn_in['ln_b'], 'L1_attn_r_w1': _L1_attn_in['r_w1'], 'L1_attn_r_b1': _L1_attn_in['r_b1'], 'L1_attn_r_w2': _L1_attn_in['r_w2'], 'L1_attn_r_b2': _L1_attn_in['r_b2'], 'L1_attn_Wq': _L1_attn_in['Wq'], 'L1_attn_bq': _L1_attn_in['bq'], 'L1_attn_Wk': _L1_attn_in['Wk'], 'L1_attn_bk': _L1_attn_in['bk'], 'L1_attn_Wv': _L1_attn_in['Wv'], 'L1_attn_bv': _L1_attn_in['bv'], 'L1_attn_Wo': _L1_attn_in['Wo'], 'L1_attn_bo': _L1_attn_in['bo'], 'L1_attn_in_w': _L1_attn_in['in_w'], 'L1_attn_conv_w': _L1_attn_in['conv_w'], 'L1_attn_conv_b': _L1_attn_in['conv_b'], 'L1_attn_xproj_w': _L1_attn_in['xproj_w'], 'L1_attn_dt_w': _L1_attn_in['dt_w'], 'L1_attn_dt_b': _L1_attn_in['dt_b'], 'L1_attn_A_log': _L1_attn_in['A_log'], 'L1_attn_Dp': _L1_attn_in['Dp'], 'L1_attn_out_w': _L1_attn_in['out_w'], 'L1_xattn_W_q': _L1_xattn_in['W_q'], 'L1_xattn_W_k': _L1_xattn_in['W_k'], 'L1_xattn_W_v': _L1_xattn_in['W_v'], 'L1_xattn_W_o': _L1_xattn_in['W_o'], 'L1_ffn_gate_w': _L1_ffn_in['gate_w'], 'L1_ffn_Wg': _L1_ffn_in['Wg'], 'L1_ffn_Wu': _L1_ffn_in['Wu'], 'L1_ffn_Wd': _L1_ffn_in['Wd']}

def reference(x, ctx_1024, mask_1x1xSxS2_bk1, L0_attn_ln_gamma, L0_attn_ln_beta, L0_attn_w_qkv, L0_attn_b_qkv, L0_attn_w_out, L0_attn_b_out, L0_xattn_Wq, L0_xattn_Wkv, L0_xattn_Wp, L0_xattn_bp, L0_xattn_ln_g, L0_xattn_ln_b, L0_ffn_gate_w, L0_ffn_down_w, L0_ffn_down_b, L0_ffn_up_w, L0_ffn_up_b, L1_attn_ln_w, L1_attn_ln_b, L1_attn_r_w1, L1_attn_r_b1, L1_attn_r_w2, L1_attn_r_b2, L1_attn_Wq, L1_attn_bq, L1_attn_Wk, L1_attn_bk, L1_attn_Wv, L1_attn_bv, L1_attn_Wo, L1_attn_bo, L1_attn_in_w, L1_attn_conv_w, L1_attn_conv_b, L1_attn_xproj_w, L1_attn_dt_w, L1_attn_dt_b, L1_attn_A_log, L1_attn_Dp, L1_attn_out_w, L1_xattn_W_q, L1_xattn_W_k, L1_xattn_W_v, L1_xattn_W_o, L1_ffn_gate_w, L1_ffn_Wg, L1_ffn_Wu, L1_ffn_Wd):
    import jax
    import jax.numpy as jnp

    def _L0_attn_ref(x, ln_gamma, ln_beta, w_qkv, b_qkv, w_out, b_out):
        import jax, jax.numpy as jnp
        import numpy as np
        D_MODEL = 128
        NUM_HEADS = 16
        HEAD_DIM = D_MODEL // NUM_HEADS
        B, T, C = x.shape
        residual = x
        mu = jnp.mean(x, axis=-1, keepdims=True)
        var = jnp.var(x, axis=-1, keepdims=True)
        h = (x - mu) * jax.lax.rsqrt(var + 1e-05) * ln_gamma + ln_beta
        qkv = (h @ w_qkv + b_qkv).reshape(B, T, 3, NUM_HEADS, HEAD_DIM)
        qkv = jnp.transpose(qkv, (2, 0, 3, 1, 4))
        q, k, v = (qkv[0], qkv[1], qkv[2])
        scores = jnp.einsum('bhqd,bhkd->bhqk', q, k) / np.sqrt(HEAD_DIM)
        attn = jax.nn.softmax(scores, axis=-1)
        out = jnp.einsum('bhqk,bhkd->bhqd', attn, v)
        out = jnp.transpose(out, (0, 2, 1, 3)).reshape(B, T, C)
        out = out @ w_out + b_out
        return residual + out

    def _L0_xattn_ref(x_query, x_context, Wq, Wkv, Wp, bp, ln_g, ln_b):
        import jax, jax.numpy as jnp
        import numpy as np
        NUM_HEADS = 16
        D_MODEL = 128
        HEAD_DIM = D_MODEL // NUM_HEADS
        SCALE = float(np.sqrt(HEAD_DIM))
        EPS = 1e-05

        def layernorm(x, g, b):
            mu = jnp.mean(x, axis=-1, keepdims=True)
            var = jnp.mean(jnp.square(x - mu), axis=-1, keepdims=True)
            return (x - mu) * jax.lax.rsqrt(var + EPS) * g + b
        B, Nq, _ = x_query.shape
        Nc = x_context.shape[1]
        H, D = (NUM_HEADS, HEAD_DIM)
        q = (x_query @ Wq).reshape(B, Nq, H, D).transpose(0, 2, 1, 3)
        kv = (x_context @ Wkv).reshape(B, Nc, 2, H, D)
        k = kv[:, :, 0].transpose(0, 2, 1, 3)
        v = kv[:, :, 1].transpose(0, 2, 1, 3)
        q = layernorm(q, ln_g, ln_b)
        k = layernorm(k, ln_g, ln_b)
        q = q * SCALE
        attn = jnp.einsum('bhqd,bhkd->bhqk', q, k)
        attn = jax.nn.softmax(attn, axis=-1)
        out = jnp.einsum('bhqk,bhkd->bhqd', attn, v)
        out = out.transpose(0, 2, 1, 3).reshape(B, Nq, H * D)
        return out @ Wp + bp

    def _L0_ffn_ref(x, gate_w, down_w, down_b, up_w, up_b):
        import jax, jax.numpy as jnp
        import numpy as np
        TOP_K = 2
        pooled = x.mean(axis=1)
        gate = jax.nn.softmax(pooled @ gate_w.T, axis=-1)
        top_w, top_i = jax.lax.top_k(gate, TOP_K)
        top_w = top_w / (top_w.sum(axis=-1, keepdims=True) + 1e-08)
        Wd = down_w[top_i]
        bd = down_b[top_i]
        Wu = up_w[top_i]
        bu = up_b[top_i]
        h = jax.nn.gelu(jnp.einsum('bsd,bkcd->bksc', x, Wd) + bd[:, :, None, :], approximate=False)
        h = h * top_w[:, :, None, None]
        out = jnp.einsum('bksc,bkdc->bsd', h, Wu)
        out = out + (top_w[:, :, None] * bu).sum(axis=1)[:, None, :]
        return out

    def _L1_attn_ref(x, ln_w, ln_b, r_w1, r_b1, r_w2, r_b2, Wq, bq, Wk, bk, Wv, bv, Wo, bo, in_w, conv_w, conv_b, xproj_w, dt_w, dt_b, A_log, Dp, out_w):
        import jax, jax.numpy as jnp
        import numpy as np
        B, T, D = (4, 128, 128)
        H = 16
        DS, DC, EXP = (16, 4, 2)
        DIN = EXP * D
        DTR = D // 16
        TOPK_RATIO = 0.25
        EPS = 1e-05

        def _attn_core(x, Wq, bq, Wk, bk, Wv, bv, Wo, bo):
            b, L, d = x.shape
            hd = d // H
            q = (x @ Wq + bq).reshape(b, L, H, hd)
            k = (x @ Wk + bk).reshape(b, L, H, hd)
            v = (x @ Wv + bv).reshape(b, L, H, hd)
            scores = jnp.einsum('bqhd,bkhd->bhqk', q, k) / jnp.sqrt(jnp.float32(hd))
            p = jax.nn.softmax(scores, axis=-1)
            o = jnp.einsum('bhqk,bkhd->bqhd', p, v).reshape(b, L, d)
            return o @ Wo + bo

        def _ssm_core(u, in_w, conv_w, conv_b, xproj_w, dt_w, dt_b, A_log, Dp, out_w):
            b, L, _ = u.shape
            xi, z = jnp.split(u @ in_w, 2, axis=-1)
            xp = jnp.pad(xi, ((0, 0), (DC - 1, 0), (0, 0)))
            xc = conv_b + sum((xp[:, j:j + L] * conv_w[:, j] for j in range(DC)))
            xc = jax.nn.silu(xc)
            proj = xc @ xproj_w
            dtp = proj[..., :DTR]
            Bm = proj[..., DTR:DTR + DS]
            Cm = proj[..., DTR + DS:]
            delta = jax.nn.softplus(dtp @ dt_w + dt_b)
            A = -jnp.exp(A_log)
            dA = jnp.exp(delta[..., None] * A)
            dBu = (delta * xc)[..., None] * Bm[:, :, None, :]

            def step(h, inp):
                dA_t, dBu_t, C_t = inp
                h = dA_t * h + dBu_t
                return (h, jnp.einsum('bds,bs->bd', h, C_t))
            xs = (jnp.moveaxis(dA, 1, 0), jnp.moveaxis(dBu, 1, 0), jnp.moveaxis(Cm, 1, 0))
            _, ys = jax.lax.scan(step, jnp.zeros((b, DIN, DS), u.dtype), xs)
            y = jnp.moveaxis(ys, 0, 1) + xc * Dp
            y = y * jax.nn.silu(z)
            return y @ out_w
        b, t, d = x.shape
        k = min(max(1, int(TOPK_RATIO * t)), t)
        mu = x.mean(-1, keepdims=True)
        var = ((x - mu) ** 2).mean(-1, keepdims=True)
        xn = (x - mu) * jax.lax.rsqrt(var + EPS) * ln_w + ln_b
        scores = jnp.squeeze(jax.nn.gelu(xn @ r_w1 + r_b1) @ r_w2 + r_b2, -1)
        _, topk_idx = jax.lax.top_k(scores, k)
        bidx = jnp.arange(b)[:, None]
        mask = jnp.zeros((b, t), bool).at[bidx, topk_idx].set(True)
        order = jnp.argsort(mask.astype(jnp.int32), axis=1)
        bottom_idx = order[:, :t - k]
        x_ssm = xn[bidx, bottom_idx]
        d_ssm_tok = _ssm_core(x_ssm, in_w, conv_w, conv_b, xproj_w, dt_w, dt_b, A_log, Dp, out_w)
        delta_ssm = jnp.zeros_like(xn).at[bidx, bottom_idx].set(d_ssm_tok)
        x_attn = xn[bidx, topk_idx]
        d_attn_tok = _attn_core(x_attn, Wq, bq, Wk, bk, Wv, bv, Wo, bo)
        delta_attn = jnp.zeros_like(xn).at[bidx, topk_idx].set(d_attn_tok)
        delta = jnp.where(mask[..., None], delta_attn, delta_ssm)
        return x + delta

    def _L1_xattn_ref(query, key, value, mask, W_q, W_k, W_v, W_o):
        import jax, jax.numpy as jnp
        import numpy as np
        D_MODEL = 128
        NUM_HEADS = 16
        D_K = D_MODEL // NUM_HEADS

        def _split(x):
            B, S, _ = x.shape
            return x.reshape(B, S, NUM_HEADS, D_K).transpose(0, 2, 1, 3)
        Q = _split(query @ W_q.T)
        K = _split(key @ W_k.T)
        V = _split(value @ W_v.T)
        scores = jnp.einsum('bhqd,bhkd->bhqk', Q, K) / jnp.sqrt(jnp.float32(D_K))
        scores = jnp.where(mask, -jnp.inf, scores)
        attn_w = jax.nn.softmax(scores, axis=-1)
        attn_w = jnp.nan_to_num(attn_w, nan=0.0)
        out = jnp.einsum('bhqk,bhkd->bhqd', attn_w, V)
        B, _, Sq, _ = out.shape
        merged = out.transpose(0, 2, 1, 3).reshape(B, Sq, D_MODEL)
        return merged @ W_o.T

    def _L1_ffn_ref(x, gate_w, Wg, Wu, Wd):
        import jax, jax.numpy as jnp
        import numpy as np
        B, S, D = (4, 512, 128)
        E, I = (8, 256)
        CAPACITY = 2
        K = max(1, int(S / E * CAPACITY))
        logits = jnp.einsum('bsd,de->bse', x, gate_w)
        affinity = jax.nn.softmax(logits, axis=-1)
        affinity_T = jnp.transpose(affinity, (0, 2, 1))
        gating, index = jax.lax.top_k(affinity_T, K)
        b_idx = jnp.arange(x.shape[0])[:, None, None]
        x_sel = x[b_idx, index]
        g = jnp.einsum('bekd,edi->beki', x_sel, Wg)
        u = jnp.einsum('bekd,edi->beki', x_sel, Wu)
        h = jax.nn.silu(g) * u
        out = jnp.einsum('beki,eid->bekd', h, Wd)
        contrib = out * gating[..., None]
        x_out = jnp.zeros_like(x).at[b_idx, index].add(contrib)
        return x_out
    x = _layernorm(x + _L0_attn_ref(x, L0_attn_ln_gamma, L0_attn_ln_beta, L0_attn_w_qkv, L0_attn_b_qkv, L0_attn_w_out, L0_attn_b_out), axis=-1)
    x = _layernorm(x + _L0_xattn_ref(x, ctx_1024, L0_xattn_Wq, L0_xattn_Wkv, L0_xattn_Wp, L0_xattn_bp, L0_xattn_ln_g, L0_xattn_ln_b), axis=-1)
    x = _layernorm(x + _L0_ffn_ref(x, L0_ffn_gate_w, L0_ffn_down_w, L0_ffn_down_b, L0_ffn_up_w, L0_ffn_up_b), axis=-1)
    x = _layernorm(x + _L1_attn_ref(x, L1_attn_ln_w, L1_attn_ln_b, L1_attn_r_w1, L1_attn_r_b1, L1_attn_r_w2, L1_attn_r_b2, L1_attn_Wq, L1_attn_bq, L1_attn_Wk, L1_attn_bk, L1_attn_Wv, L1_attn_bv, L1_attn_Wo, L1_attn_bo, L1_attn_in_w, L1_attn_conv_w, L1_attn_conv_b, L1_attn_xproj_w, L1_attn_dt_w, L1_attn_dt_b, L1_attn_A_log, L1_attn_Dp, L1_attn_out_w), axis=-1)
    x = _layernorm(x + _L1_xattn_ref(x, ctx_1024, ctx_1024, mask_1x1xSxS2_bk1, L1_xattn_W_q, L1_xattn_W_k, L1_xattn_W_v, L1_xattn_W_o), axis=-1)
    x = _layernorm(x + _L1_ffn_ref(x, L1_ffn_gate_w, L1_ffn_Wg, L1_ffn_Wu, L1_ffn_Wd), axis=-1)
    return x

_drawn_inputs = setup_inputs


def setup_inputs(seed=0):
    import zlib

    import numpy as np

    out = dict(_drawn_inputs(seed))
    spreads = {'L0_attn_ln_gamma': (1.0, 0.567),
     'L0_attn_ln_beta': (0.0, 0.1),
     'L0_attn_b_qkv': (0.0, 0.1),
     'L0_attn_b_out': (0.0, 0.1),
     'L0_xattn_bp': (0.0, 0.1),
     'L0_xattn_ln_g': (1.0, 0.6),
     'L0_xattn_ln_b': (0.0, 0.8),
     'L1_attn_ln_w': (1.0, 0.6),
     'L1_attn_ln_b': (0.0, 0.8),
     'L1_attn_r_b1': (0.0, 0.8),
     'L1_attn_bq': (0.0, 0.8),
     'L1_attn_bk': (0.0, 0.8),
     'L1_attn_bv': (0.0, 0.8),
     'L1_attn_bo': (0.0, 0.403),
     'L1_attn_conv_b': (0.0, 0.8),
     'L1_attn_Dp': (1.0, 0.6)}
    factors = {'L0_ffn_gate_w': 3.703,
     'L0_ffn_down_w': 4.983,
     'L0_ffn_down_b': 8.0,
     'L0_ffn_up_w': 4.86,
     'L0_ffn_up_b': 4.732,
     'L1_attn_r_w1': 3.334,
     'L1_attn_r_w2': 3.141,
     'L1_attn_Wq': 8.0,
     'L1_attn_Wk': 8.0,
     'L1_attn_Wv': 8.0,
     'L1_attn_Wo': 8.0,
     'L1_attn_in_w': 8.0,
     'L1_attn_conv_w': 8.0,
     'L1_attn_xproj_w': 8.0,
     'L1_attn_dt_w': 8.0,
     'L1_attn_dt_b': 8.0,
     'L1_attn_A_log': 8.0,
     'L1_attn_out_w': 8.0,
     'L1_ffn_gate_w': 8.0,
     'L1_ffn_Wg': 8.0,
     'L1_ffn_Wu': 8.0,
     'L1_ffn_Wd': 8.0}
    for name, (base, spread) in spreads.items():
        noise = np.random.default_rng([zlib.crc32(name.encode()), seed]).standard_normal(out[name].shape)
        drawn = base * np.exp(spread * noise) if base else spread * noise
        out[name] = jnp.asarray(drawn.astype(out[name].dtype))
    for name, factor in factors.items():
        out[name] = (out[name] * factor).astype(out[name].dtype)
    return out
```

```python
from contextlib import ExitStack
import math

import numpy as np

import concourse.bass as bass
from concourse import mybir

F32 = mybir.dt.float32
BF16 = mybir.dt.bfloat16
U8 = mybir.dt.uint8
ALU = mybir.AluOpType
ACT = mybir.ActivationFunctionType
AX = mybir.AxisListType

B, T, D = 8, 128, 128
H, HD = 16, 8
G = 4
J = H // G
NU = B * G
NC = 77
VW = 32
HB = B // 2
E0, BN = 8, 64
KSEL = T // 4
TS = T - KSEL
DC, DS, DTR = 4, 16, 8
DIN = 2 * D
NH = DIN // 128
E1, IW = 8, 256
NI = IW // 128
EPS = 1e-5
MASKED = -1e30


class Ring:

    def __init__(self, banks, full, copied, jobs):
        self.banks, self.full, self.copied, self.jobs = banks, full, copied, jobs
        self.index = {name: n for n, name in enumerate(jobs)}
        self.filled = self.emptied = 0

    def fill(self, pe, name):
        n, size = self.filled, len(self.banks)
        assert self.jobs[n] == name, (self.jobs[n], name)
        if n >= size:
            pe.wait_ge(self.copied, n - size + 1)
        self.filled += 1
        return self.banks[n % size]

    def take(self, reader, name):
        n = self.emptied
        assert self.jobs[n] == name, (self.jobs[n], name)
        reader.wait_ge(self.full, n + 1)
        self.emptied += 1
        return self.banks[n % len(self.banks)]

    def wait_copied(self, eng, *names):
        eng.wait_ge(self.copied, max(self.index[n] for n in names) + 1)

    def drain(self, pe):
        if self.filled:
            pe.wait_ge(self.copied, self.filled)


class Count:

    def __init__(self, sem):
        self.sem, self.n = sem, 0

    def then(self, ins):
        ins.then_inc(self.sem, 1)
        self.n += 1
        return self.n


class Attention:

    def __init__(self, sem, name, nk, scale, kM, V, Wo, XB, Xout, masked=False):
        self.nk, self.scale, self.kM, self.V = nk, scale, kM, V
        self.Wo, self.XB, self.Xout, self.masked = Wo, XB, Xout, masked
        self.scores_ready = sem(f"{name}_scores_ready")
        self.max_ready = sem(f"{name}_max_ready")
        self.shifted = sem(f"{name}_shifted")
        self.exp_ready = sem(f"{name}_exp_ready")
        self.probsT_ready = sem(f"{name}_probsT_ready")
        self.probsT_copied = sem(f"{name}_probsT_copied")
        self.pv_done = sem(f"{name}_pv_done")
        self.outT_copied = sem(f"{name}_outT_copied")
        self.out_ready = sem(f"{name}_out_ready")
        self.recip_ready = sem(f"{name}_recip_ready")
        self.normed = sem(f"{name}_normed")
        self.normedT_ready = sem(f"{name}_normedT_ready")
        self.normedT_copied = sem(f"{name}_normedT_copied")
        self.proj_ready = sem(f"{name}_proj_ready")
        self.residual_ready = sem(f"{name}_residual_ready")
        self.stats_ready = sem(f"{name}_stats_ready")
        self.var_ready = sem(f"{name}_var_ready")
        self.eps_ready = sem(f"{name}_eps_ready")
        self.rstd_ready = sem(f"{name}_rstd_ready")
        self.x_ready = sem(f"{name}_x_ready")
        self.xb_ready = sem(f"{name}_xb_ready")


ACT_JOBS = (["x0T.0", "q1.0", "k1.0", "x0T.1", "q1.1", "k1.1", "ctxT.0", "ctxT.1", "W5T", "down3T", "up3T",
             "gate3T", "k5.0", "k5.1", "k2.0", "k2.1"]
            + ["x1T.0", "x1T.1", "q2T.0", "q2T.1"]
            + ["x2T.0", "x2T.1"] + [f"hid.{t}.{c}" for c in range(2) for t in range(4)]
            + ["xnT.0", "xnT.1", "router.0", "router.1", "srow.0", "srow.1", "permT.0", "permT.1", "xpT.0", "xpT.1"]
            + [f"conv.{h}.{c}" for h in range(2) for c in range(2)] + [f"z.{h}.{c}" for h in range(2) for c in range(2)]
            + ["qa", "ka", "dt.0", "dt.1"] + [f"delta.{h}.{c}" for h in range(2) for c in range(2)]
            + ["oaT"] + ["x4T.0", "x4T.1", "q5.0", "q5.1", "x5T.0", "x5T.1"])
DVE_JOBS = (["v1.0", "v1.1", "kv.0", "kv.1", "kv.2", "kv.3", "v5.0", "v5.1", "q2.0", "q2.1"]
            + ["logits8", "cT", "cexp", "up.0", "up.1"]
            + ["cumU", "va", "BC.0", "BC.1", "dposA.0", "dposA.1", "dposS.0", "dposS.1", "dl.0", "dl.1", "logits6"])


def build(nc, a, out):
    ctx = ExitStack()
    with ctx:
        _build(nc, ctx, a, out)


def _build(nc, ctx, a, out):
    def sb(name, shape, dt=F32):
        return ctx.enter_context(nc.sbuf_tensor(name, shape, dt))

    def sem(name):
        return ctx.enter_context(nc.semaphore(name))

    PS = ctx.enter_context(nc.psum_tensor("PS", [128, 8, 512], F32))

    ident = sb("ident", [128, 128])
    identb = sb("identb", [128, 128], BF16)
    before = sb("before", [128, 128])
    after = sb("after", [128, 128])
    colnum = sb("colnum", [128, 128])
    slot_base = sb("slot_base", [128, 1])
    headmask = sb("headmask", [128, J])
    part_pick = sb("part_pick", [96, 32], BF16)
    spread8 = sb("spread8", [E0, E0 * BN])
    xprojBC = sb("xprojBC", [128, NH, 3 * 2 * DS])
    earlier = sb("earlier", [8, 8, 8])
    neg_half = sb("neg_half", [128, HB])
    eps_col = sb("eps_col", [128, 1])

    gamma1 = sb("gamma1", [128, 1]); beta1 = sb("beta1", [128, 1])
    Wqkv1 = sb("Wqkv1", [128, 3 * D]); bqk1 = sb("bqk1", [128, 2]); bv1 = sb("bv1", [128, D])
    Wo1 = sb("Wo1", [128, D]); bo1 = sb("bo1", [128, D])
    Wq2 = sb("Wq2", [128, D]); Wkv2 = sb("Wkv2", [128, 2 * D]); Wp2 = sb("Wp2", [128, D]); bp2 = sb("bp2", [128, D])
    gb2 = sb("gb2", [128, 2])
    ctxN = sb("ctxN", [NC, B, D])
    W5 = sb("W5", [128, 4, D]); W5T = sb("W5T", [128, 4, D])
    mask8 = sb("mask8", [128, NC], U8); maskneg = sb("maskneg", [128, NC], BF16)
    maskf = sb("maskf", [128, NC]); nmasked = sb("nmasked", [128, 1]); anykey = sb("anykey", [128, 1])
    gate3 = sb("gate3", [E0, D]); gate3T = sb("gate3T", [128, E0])
    down3 = sb("down3", [128, 4, D]); down3T = sb("down3T", [128, 4 * 128]); downb3 = sb("downb3", [128, 4])
    up3 = sb("up3", [128, E0, BN]); up3T = sb("up3T", [128, 4, D]); upb3 = sb("upb3", [E0, D])
    lnwb4 = sb("lnwb4", [128, 2])
    rw1 = sb("rw1", [128, D // 2]); rb1 = sb("rb1", [D // 2, 1]); rw2 = sb("rw2", [D // 2, 1]); rb2 = sb("rb2", [128, 1])
    Wqkvo4 = sb("Wqkvo4", [128, 4, D]); bqk4 = sb("bqk4", [128, 2]); bv4 = sb("bv4", [128, D])
    posbias = sb("posbias", [128, D])
    inw4 = sb("inw4", [128, 2 * DIN]); convw = sb("convw", [128, DIN, DC]); convb = sb("convb", [128, NH])
    convin = sb("convin", [128, DC, DIN])
    xproj = sb("xproj", [128, NH, DTR + 2 * DS]); dtw = sb("dtw", [DTR, DIN]); dtb = sb("dtb", [128, NH])
    Alog = sb("Alog", [128, NH, DS]); Aneg = sb("Aneg", [128, NH, DS]); Dp = sb("Dp", [128, NH])
    outw4 = sb("outw4", [128, NH, D]); diagD = sb("diagD", [128, NH, 128])
    gate6 = sb("gate6", [128, E1])
    Wgu = [sb(f"Wgu{i}", [128, 2, IW]) for i in range(2)]
    Wd6 = [sb(f"Wd6_{i}", [128, NI, D]) for i in range(2)]

    X = [sb(f"X{i}", [128, B, D]) for i in range(2)]
    XH = sb("XH", [128, B, D])
    XB = sb("XB", [128, B, D])
    xT = sb("xT", [128, B, T])
    ctxT = sb("ctxT", [128, B, NC])
    qT = sb("qT", [128, B, T])
    big = sb("big", [128, J * B * T + B * H * VW])
    kM1 = big[:, 0:J * B * T].rearrange("p (j b t) -> p j b t", j=J, b=B)
    V1 = big[:, J * B * T:].rearrange("p (b h w) -> p b h w", b=B, h=H)
    kM2 = sb("kM2", [128, J, B, NC]); V2full = sb("V2", [128, B * H * VW]); V2 = V2full[0:NC].rearrange("p (b h w) -> p b h w", b=B, h=H)
    kM5 = sb("kM5", [128, J, B, NC]); V5 = sb("V5", [NC, B, H, VW])
    mb1 = sb("mb1", [128, J]); sc2 = sb("sc2", [128, J]); sh2 = sb("sh2", [128, J]); mb4 = sb("mb4", [128, J])
    qc = sb("qc", [128, B, D]); sq = sb("sq", [128, B, D])
    hss = sb("hss", [128, B * H]); hvar = sb("hvar", [128, B * H]); hr0 = sb("hr0", [128, B * H]); hr1 = sb("hr1", [128, B * H])
    wmean = sb("wmean", [128, 2, H])
    Eb = sb("Eb", [128, 3, J, 128]); PT = sb("PT", [128, 3, J, 128]); mx = sb("mx", [128, 3, J])
    outT = sb("outT", [128, G, 128]); rs = sb("rs", [128, 2, H]); oN = sb("oN", [128, 2, D]); oNT = sb("oNT", [128, 2, D])
    R = sb("R", [128, B, D]); st = sb("st", [128, B, 6]); mv = sb("mv", [128, B, 2]); ve = sb("ve", [128, B]); rstd = sb("rstd", [128, B])

    ld = {k: sem(f"loaded_{k}") for k in ("x0", "x1", "a1", "ctx", "l2", "l5", "l3", "l4", "ssm", "g6", "bc4")}
    expert_loaded = [sem("expert_loaded0"), sem("expert_loaded1")]
    stored = sem("stored")
    const_ready = sem("const_ready")
    aring = Ring([0, 1, 2, 3], sem("act_bank_full"), sem("act_bank_copied"), ACT_JOBS)
    dring = Ring([4, 5, 6, 7], sem("dve_bank_full"), sem("dve_bank_copied"), DVE_JOBS)
    dve_step, act_step, pool_step = Count(sem("dve_step")), Count(sem("act_step")), Count(sem("pool_step"))
    ln_var, ln_rstd = sem("ln_var"), sem("ln_rstd")
    ev = {}

    def event(name):
        if name not in ev:
            ev[name] = sem(name)
        return ev[name]

    at1 = Attention(sem, "at1", T, 1 / math.sqrt(HD), kM1, V1, Wo1[:], XB, X[1])
    at2 = Attention(sem, "at2", NC, math.sqrt(HD), kM2, V2, Wp2[:], XB, X[0])
    at5 = Attention(sem, "at5", NC, 1 / math.sqrt(HD), kM5, V5, W5T[:, 3, :], X[0], X[1], masked=True)

    def bank4(i, p=128):
        return PS[0:p, i, :].rearrange("p (b t) -> p b t", b=4)

    x_src = a["x"].rearrange("b t d -> t b d")

    def col(ap):
        return ap.rearrange("(p o) -> p o", o=1)

    def row(ap, p=128):
        return ap.rearrange("(o n) -> o n", o=1).to_broadcast([p, ap.shape[0]])

    loads = {
        "x0": [(X[0][:, 0:HB, :], x_src[:, 0:HB, :])],
        "x1": [(X[0][:, HB:B, :], x_src[:, HB:B, :])],
        "a1": [(gamma1[:], col(a["L0_attn_ln_gamma"])), (beta1[:], col(a["L0_attn_ln_beta"])),
               (Wqkv1[:], a["L0_attn_w_qkv"]),
               (bqk1[:], a["L0_attn_b_qkv"][0:2 * D].rearrange("(c p) -> p c", c=2)),
               (bv1[:], row(a["L0_attn_b_qkv"][2 * D:3 * D])),
               (Wo1[:], a["L0_attn_w_out"]), (bo1[:], row(a["L0_attn_b_out"]))],
        "ctx": [(ctxN[:], a["ctx_1024"].rearrange("b t d -> t b d"))],
        "l2": [(Wq2[:], a["L0_xattn_Wq"]), (Wkv2[:], a["L0_xattn_Wkv"]), (Wp2[:], a["L0_xattn_Wp"]),
               (bp2[:], row(a["L0_xattn_bp"]))]
              + [(gb2[HD * h:HD * h + HD, c:c + 1], col(a[n]))
                 for h in range(H) for c, n in enumerate(("L0_xattn_ln_g", "L0_xattn_ln_b"))],
        "l5": [(W5[:, i, :], a[f"L1_xattn_W_{n}"]) for i, n in enumerate("qkvo")]
              + [(mask8[:], a["mask_1x1xSxS2_bk1"].bitcast(U8).rearrange("(q k) -> q k", k=NC))],
        "l3": [(gate3[:], a["L0_ffn_gate_w"]),
               (down3[:], a["L0_ffn_down_w"].rearrange("(t e) c d -> (e c) t d", e=2)),
               (downb3[:], a["L0_ffn_down_b"].rearrange("(t e) c -> (e c) t", e=2)),
               (up3[:], a["L0_ffn_up_w"].rearrange("e d c -> d e c")), (upb3[:], a["L0_ffn_up_b"])],
        "l4": [(lnwb4[:, 0:1], col(a["L1_attn_ln_w"])), (lnwb4[:, 1:2], col(a["L1_attn_ln_b"])),
               (rw1[:], a["L1_attn_r_w1"]), (rb1[:], col(a["L1_attn_r_b1"])), (rw2[:], a["L1_attn_r_w2"]),
               (rb2[:], row(a["L1_attn_r_b2"])),
               (bqk4[:, 0:1], col(a["L1_attn_bq"])), (bqk4[:, 1:2], col(a["L1_attn_bk"])),
               (bv4[:], row(a["L1_attn_bv"]))]
              + [(Wqkvo4[:, i, :], a[f"L1_attn_W{n}"]) for i, n in enumerate("qkvo")],
        "bc4": [(posbias[TS:T, :], row(a["L1_attn_bo"], KSEL))],
        "ssm": [(inw4[:], a["L1_attn_in_w"]),
                (convw[:], a["L1_attn_conv_w"].rearrange("(o n) c -> o n c", o=1).to_broadcast([128, DIN, DC])),
                (convb[:], a["L1_attn_conv_b"].rearrange("(h p) -> p h", p=128)),
                (xproj[:], a["L1_attn_xproj_w"].rearrange("(h p) n -> p h n", p=128)),
                (dtw[:], a["L1_attn_dt_w"]), (dtb[:], a["L1_attn_dt_b"].rearrange("(h p) -> p h", p=128)),
                (Alog[:], a["L1_attn_A_log"].rearrange("(h p) n -> p h n", p=128)),
                (Dp[:], a["L1_attn_Dp"].rearrange("(h p) -> p h", p=128)),
                (outw4[:], a["L1_attn_out_w"].rearrange("(h p) n -> p h n", p=128))],
        "g6": [(gate6[:], a["L1_ffn_gate_w"])],
    }
    need = {k: 16 * len(v) for k, v in loads.items()}

    def loaded(eng, *keys):
        for k in keys:
            eng.wait_ge(ld[k], need[k])

    def load(eng, *keys):
        for k in keys:
            for dst, src in loads[k]:
                eng.dma_start(dst, src, allow_slow_non_contiguous=True).then_inc(ld[k], 16)

    W768 = B * TS
    du = sb("du", [128, NH, W768])
    xc = V2full[:, 0:NH * W768].rearrange("p (h n) -> p h n", h=NH)
    zs = V2full[:, NH * W768:2 * NH * W768].rearrange("p (h n) -> p h n", h=NH)
    delta = big[:, 0:2 * W768].rearrange("p (h n) -> p h n", h=NH)
    dA = [big[:, (2 + i) * W768:(3 + i) * W768] for i in range(2)]
    dBu = [big[:, (4 + i) * W768:(5 + i) * W768] for i in range(2)]
    hst = [big[:, (6 + i) * W768:(7 + i) * W768] for i in range(2)]
    hC = [big[:, (8 + i) * W768:(9 + i) * W768] for i in range(2)]
    kM2flat = kM2[:].rearrange("p j b n -> p (j b n)")
    Bsb = [kM2flat[:, i * W768:(i + 1) * W768] for i in range(2)]
    Csb = [kM2flat[:, 2 * W768:3 * W768], XH[:].rearrange("p b d -> p (b d)")[:, 0:W768]]
    sp_abs = big[:, 2 * W768:4 * W768].rearrange("p (h n) -> p h n", h=NH)
    sp_exp = big[:, 4 * W768:6 * W768].rearrange("p (h n) -> p h n", h=NH)
    sp_log = big[:, 6 * W768:8 * W768].rearrange("p (h n) -> p h n", h=NH)
    sp_relu = big[:, 8 * W768:10 * W768].rearrange("p (h n) -> p h n", h=NH)
    PADT = DC - 1 + T
    xpT = sb("xpT", [128, B, PADT])
    hrT = big[0:D // 2, 2 * B * T:3 * B * T].rearrange("p (b t) -> p b t", b=B)
    Srow = big[:, 0:B * T].rearrange("p (b t) -> p b t", b=B)
    scol = sb("scol", [128, B]); gt = big[:, B * T:2 * B * T].rearrange("p (b t) -> p b t", b=B); eq = V2full[:, 2 * NH * W768:2 * NH * W768 + B * T].rearrange("p (b t) -> p b t", b=B)
    rank = sb("rank", [128, B]); sel = sb("sel", [128, B]); unsel = sb("unsel", [128, B]); cumU = sb("cumU", [128, B])
    pos = sb("pos", [128, B]); posa = sb("posa", [128, B])
    Perm = gt; PermT = eq
    qTa = ctxT[:].rearrange("p b t -> p (b t)")[:, 0:B * KSEL].rearrange("p (b k) -> p b k", b=B); kMa = PT[:].rearrange("p a j t -> p (a j t)")[:, 0:J * B * KSEL].rearrange("p (j b k) -> p j b k", j=J, b=B); va = R[:, 0:2, :]
    Pa = convw[:].rearrange("p n c -> p (n c)").rearrange("p (n k) -> p n k", k=KSEL)
    PaT = XB[:].rearrange("p b d -> p (b d)").rearrange("p (n k) -> p n k", k=KSEL)
    mxa = sb("mxa", [128, 2 * H]); sma = sb("sma", [128, 2 * H])
    oa, oaT = R[:, 2:4, :], R[:, 4:6, :]
    dtp = qT[0:DTR].rearrange("p b t -> p (b t)")[:, 0:W768]
    Ebflat = Eb[0:96].rearrange("p a j t -> p (a j t)")
    sqb = sq[0:96].rearrange("p b d -> p (b d)").bitcast(BF16)
    BC, BC3 = Ebflat[:, 0:W768], Ebflat[:, W768:].bitcast(BF16)[:, 0:W768]
    BCh, BCm = sqb[:, 0:W768], sqb[:, W768:2 * W768]
    dpos = qc
    hid = big[:, 0:4 * B * T].rearrange("p (t n) -> p t n", t=4)
    pooledT = sb("pooledT", [128, B])
    g8 = sb("g8", [8, 8]); m8 = sb("m8", [8, 1]); c8 = sb("c8", [8, 8]); t64 = sb("t64", [8, 8, 8]); e64 = sb("e64", [8, 8, 8])
    r8 = sb("r8", [8, 8]); cT = sb("cT", [8, 8]); cexp = sb("cexp", [128, 4, B])
    aff = sb("aff", [128, B, E1]); am = sb("am", [128, B])
    hidE = [big[:, i * NI * B * T:(i + 1) * NI * B * T].rearrange("p (i n) -> p i n", i=NI) for i in range(2)]
    silu6 = [kM2flat[:, i * 512:(i + 1) * 512] for i in range(4)]

    block = ctx.enter_context(nc.Block())

    @block.sync
    def _(sp):
        load(sp, "x0", "x1", "a1", "l2", "l5", "l4", "g6")
        for e in range(E1):
            if e >= 2:
                sp.wait_ge(event("down_ready"), 2 * (e - 1))
            src = a["L1_ffn_Wg"][e], a["L1_ffn_Wu"][e]
            for i in range(2):
                sp.dma_start(Wgu[e % 2][:, i, :], src[i]).then_inc(expert_loaded[e % 2], 16)
            sp.dma_start(Wd6[e % 2][:], a["L1_ffn_Wd"][e].rearrange("(i p) d -> p i d", p=128))\
                .then_inc(expert_loaded[e % 2], 16)
        for c in range(2):
            sp.wait_ge(event("out_ready"), c + 1)
            sp.dma_start(out.rearrange("b t d -> t b d")[:, c * HB:(c + 1) * HB, :],
                         X[0][:, c * HB:(c + 1) * HB, :]).then_inc(stored, 16)
        sp.wait_ge(stored, 32)

    @block.gpsimd
    def _(pool):
        load(pool, "ctx", "l3", "ssm", "bc4")
        P_ = nc.gpsimd

        def step(ins):
            pool.wait_ge(pool_step.sem, pool_step.then(ins))

        def affine(t, op, pattern, multiplier=1):
            return P_.affine_select(out=t, in_=t, compare_op=op, fill=1.0, base=0, pattern=pattern,
                                    channel_multiplier=multiplier)

        P_.memset(ident[:], 0.0)
        P_.memset(identb[:], 0.0)
        P_.memset(before[:], 0.0)
        P_.memset(after[:], 0.0)
        P_.memset(part_pick[:], 0.0)
        P_.memset(earlier[:], 0.0)
        step(P_.memset(eps_col[:], EPS))
        affine(ident[:], ALU.not_equal, [[-1, 128]])
        affine(identb[:], ALU.not_equal, [[-1, 128]])
        affine(before[:], ALU.is_ge, [[1, 128]], -1)
        affine(after[:], ALU.is_ge, [[-1, 128]])
        affine(earlier[:], ALU.is_ge, [[-1, 8], [1, 8]], 0)
        P_.iota(colnum[:], pattern=[[1, 128]], base=0, channel_multiplier=0, allow_small_or_imprecise_dtypes=True)
        P_.iota(slot_base[:], pattern=[[0, 1]], base=TS, channel_multiplier=1, allow_small_or_imprecise_dtypes=True)
        P_.memset(xpT[:, :, 0:DC - 1], 0.0)
        step(P_.memset(spread8[:], 1.0))
        P_.tensor_tensor(out=spread8[:].rearrange("p (e c) -> p e c", e=E0), in0=spread8[:].rearrange("p (e c) -> p e c", e=E0),
                         in1=ident[0:E0, 0:E0].rearrange("p (e o) -> p e o", o=1).to_broadcast([E0, E0, BN]), op=ALU.mult)
        for k in range(3):
            step(affine(part_pick[32 * k:32 * k + 32, :], ALU.not_equal, [[-1, 32]]))
        P_.memset(neg_half[:], -0.5).then_inc(const_ready, 1)
        for v in (V1, V2, V5[:]):
            ins = P_.memset(v[:, :, :, HD:VW], 0.0)
        step(ins)
        for v in (V1, V2, V5[:]):
            ins = P_.memset(v[:, :, :, HD:HD + 1], 1.0)
        ins.then_inc(event("v_ones"), 1)

        powers = Count(ln_rstd)

        def rstds():
            for c in range(2):
                pool.wait_ge(ln_var, powers.n + 1)
                h = slice(c * HB, (c + 1) * HB)
                powers.then(P_.tensor_tensor(out=rstd[:, h], in0=ve[:, h], in1=neg_half[:], op=ALU.pow))

        def attention_rstds(at):
            for b in range(B):
                pool.wait_ge(at.eps_ready, b + 1)
                P_.tensor_tensor(out=rstd[:, b:b + 1], in0=ve[:, b:b + 1], in1=neg_half[:, 0:1], op=ALU.pow)\
                    .then_inc(at.rstd_ready, 1)

        def wide(bias):
            return bias[:].rearrange("p (o n) -> p o n", o=1).to_broadcast([128, B, D])

        rstds()
        dring.wait_copied(pool, "kv.3")
        P_.tensor_tensor(out=sq[0:NC], in0=qc[0:NC], in1=qc[0:NC], op=ALU.mult).then_inc(event("k_sq"), 1)
        loaded(pool, "x0", "x1", "a1")
        step(P_.tensor_tensor(out=XB[:], in0=X[0][:], in1=X[0][:], op=ALU.add))
        P_.tensor_tensor(out=XB[:], in0=XB[:], in1=wide(bo1), op=ALU.add).then_inc(at1.xb_ready, 1)
        attention_rstds(at1)
        dring.wait_copied(pool, "q2.1")
        P_.tensor_tensor(out=sq[:], in0=qc[:], in1=qc[:], op=ALU.mult).then_inc(event("q_sq"), 1)
        loaded(pool, "l2")
        pool.wait_ge(at1.x_ready, B)
        P_.tensor_tensor(out=XB[:], in0=X[1][:], in1=wide(bp2), op=ALU.add).then_inc(at2.xb_ready, 1)
        loaded(pool, "ssm")
        for j in range(DC):
            P_.tensor_tensor(out=convin[:, j, :], in0=inw4[:, 0:DIN], in1=convw[:, :, j], op=ALU.mult)
        for k in range(3):
            P_.tensor_copy(xprojBC[:, :, 2 * DS * k:2 * DS * (k + 1)], xproj[:, :, DTR:])
        for h in range(NH):
            ins = P_.tensor_scalar(out=diagD[:, h, :], in0=ident[:], scalar1=Dp[:, h:h + 1], scalar2=None,
                                   op0=ALU.mult)
        ins.then_inc(event("ssm_weights"), 1)
        attention_rstds(at2)
        rstds()
        rstds()
        for n in range(NH * DS):
            s = n // NH
            pool.wait_ge(event("c_copied"), s + 1)
            pool.wait_ge(event("h_ready"), n + 1)
            if n >= 2:
                pool.wait_ge(event("hC_used"), n - 1)
            P_.tensor_tensor(out=hC[n % 2], in0=hst[n % 2], in1=Csb[s % 2], op=ALU.mult)\
                .then_inc(event("hC_ready"), 1)
        rstds()
        attention_rstds(at5)
        rstds()

    @block.scalar
    def _(act):
        A_ = nc.scalar.activation

        def step(ins):
            act.wait_ge(act_step.sem, act_step.then(ins))

        def copy_out(name, dst, view, func=ACT.Identity, **kw):
            A_(dst, view(aring.take(act, name)), func, **kw).then_inc(aring.copied, 1)

        def masked_keys(name, dst, view, scale, shift):
            i = aring.take(act, name)
            for j in range(J):
                ins = A_(dst(j), view(i), ACT.Identity, scale=scale[:, j:j + 1],
                         **({"bias": shift[:, j:j + 1]} if shift is not None else {}))
            ins.then_inc(aring.copied, 1)

        def bank_full(i):
            return PS[:, i, :]

        def bank_ctx(i):
            return PS[:, i, 0:HB * NC].rearrange("p (b n) -> p b n", b=HB)

        def half(t, c):
            return t[:, c * HB:(c + 1) * HB, :]

        def attention_scalar(at):
            nk = at.nk
            for s in range(NU + 12):
                if s < NU:
                    act.wait_ge(at.shifted, s + 1)
                    A_(Eb[:, s % 3, :, 0:nk], Eb[:, s % 3, :, 0:nk], ACT.Exp, scale=at.scale).then_inc(at.exp_ready, 1)
                if 1 <= s <= NU:
                    u = s - 1
                    act.wait_ge(at.probsT_ready, u + 1)
                    if u >= 3:
                        act.wait_ge(at.pv_done, u - 2)
                    A_(PT[0:nk, u % 3, :, :], bank4(3 + u % 2, nk), ACT.Copy).then_inc(at.probsT_copied, 1)
                if s >= 5 and (s - 5) % G == 0 and (s - 5) // G < B:
                    b = (s - 5) // G
                    act.wait_ge(at.pv_done, G * b + G)
                    if b:
                        act.wait_ge(at.out_ready, b)
                    A_(outT[:], bank4(5), ACT.Copy).then_inc(at.outT_copied, 1)
                if s >= 8 and (s - 8) % G == 0 and (s - 8) // G < B:
                    b = (s - 8) // G
                    act.wait_ge(at.normedT_ready, b + 1)
                    if b >= 2:
                        act.wait_ge(at.proj_ready, b - 1)
                    A_(oNT[:, b % 2, :], PS[:, 7, 0:128], ACT.Copy).then_inc(at.normedT_copied, 1)

        def head_rstd(rows, ready, name):
            act.wait_ge(event(ready), 1)
            step(A_(hr0[0:rows], hss[0:rows], ACT.Ln, scale=1.0 / HD, bias=eps_col[0:rows]))
            A_(hr0[0:rows], hr0[0:rows], ACT.Exp, scale=-0.5).then_inc(event(name), 1)

        act.wait_ge(const_ready, 1)
        loaded(act, "a1")
        act.wait_ge(event("small1"), 1)
        for c in range(2):
            copy_out(f"x0T.{c}", half(xT, c), bank4, scale=gamma1[:], bias=beta1[:])
            copy_out(f"q1.{c}", half(qT, c), bank4, bias=bqk1[:, 0:1])
            masked_keys(f"k1.{c}", lambda j: kM1[:, j, c * HB:(c + 1) * HB, :], bank4, headmask, mb1)
        for c in range(2):
            copy_out(f"ctxT.{c}", half(ctxT, c), bank_ctx)
        copy_out("W5T", W5T[:], bank4)
        copy_out("down3T", down3T[:], bank_full)
        copy_out("up3T", up3T[:], bank4)
        copy_out("gate3T", gate3T[:], lambda i: PS[:, i, 0:E0])
        for c in range(2):
            masked_keys(f"k5.{c}", lambda j: kM5[:, j, c * HB:(c + 1) * HB, :], bank_ctx, headmask, None)
        head_rstd(NC, "k_ss", "k_rstd")
        act.wait_ge(event("small2"), 1)
        for c in range(2):
            masked_keys(f"k2.{c}", lambda j: kM2[:, j, c * HB:(c + 1) * HB, :], bank_ctx, sc2, sh2)
        attention_scalar(at1)

        for c in range(2):
            copy_out(f"x1T.{c}", half(xT, c), bank4)
        head_rstd(128, "q_ss", "q_rstd")
        for c in range(2):
            copy_out(f"q2T.{c}", half(qT, c), bank4, scale=gb2[:, 0:1], bias=gb2[:, 1:2])
        attention_scalar(at2)

        for c in range(2):
            copy_out(f"x2T.{c}", half(xT, c), bank4)
        dring.wait_copied(act, "logits8")
        A_(g8[:], g8[:], ACT.Exp).then_inc(event("gate3_exp"), 1)
        for c in range(2):
            for t in range(4):
                copy_out(f"hid.{t}.{c}", hid[:, t, c * 512:(c + 1) * 512], bank_full, ACT.Gelu, bias=downb3[:, t:t + 1])

        for c in range(2):
            copy_out(f"xnT.{c}", half(xT, c), bank4, scale=lnwb4[:, 0:1], bias=lnwb4[:, 1:2])
        for c in range(2):
            copy_out(f"router.{c}", half(hrT, c), lambda i: bank4(i, D // 2), ACT.Gelu_apprx_tanh, bias=rb1[:])
        for c in range(2):
            copy_out(f"srow.{c}", half(Srow, c), bank4, bias=rb2[:])
        for c in range(2):
            copy_out(f"permT.{c}", half(PermT, c), bank4)
        for c in range(2):
            copy_out(f"xpT.{c}", xpT[:, c * HB:(c + 1) * HB, DC - 1:], bank4, scale=lnwb4[:, 0:1], bias=lnwb4[:, 1:2])
        W384 = HB * TS
        for dst, name in ((xc, "conv"), (zs, "z")):
            for h in range(NH):
                for c in range(2):
                    kw = {"bias": convb[:, h:h + 1]} if name == "conv" else {}
                    copy_out(f"{name}.{h}.{c}", dst[:, h, c * W384:(c + 1) * W384], lambda i: PS[:, i, 0:W384],
                             ACT.Silu, **kw)
        copy_out("qa", qTa, lambda i: PS[:, i, 0:B * KSEL].rearrange("p (b k) -> p b k", b=B), bias=bqk4[:, 0:1])
        act.wait_ge(event("small4"), 1)
        masked_keys("ka", lambda j: kMa[:, j, :, :], lambda i: PS[:, i, 0:B * KSEL].rearrange("p (b k) -> p b k", b=B),
                    headmask, mb4)
        for c in range(2):
            copy_out(f"dt.{c}", dtp[:, c * W384:(c + 1) * W384], lambda i: PS[0:DTR, i, 0:W384])
        for h in range(NH):
            for c in range(2):
                i = aring.take(act, f"delta.{h}.{c}")
                w = slice(c * W384, (c + 1) * W384)
                A_(sp_abs[:, h, w], PS[:, i, 0:W384], ACT.Abs, bias=dtb[:, h:h + 1])
                A_(sp_relu[:, h, w], PS[:, i, 0:W384], ACT.Relu, bias=dtb[:, h:h + 1]).then_inc(aring.copied, 1)
        act.wait_ge(aring.copied, aring.emptied)
        step(A_(sp_exp, sp_abs, ACT.Exp, scale=-1.0))
        A_(sp_log, sp_exp, ACT.Ln, bias=1.0).then_inc(event("softplus_parts"), 1)
        loaded(act, "ssm")
        A_(Aneg[:], Alog[:], ACT.Exp).then_inc(event("a_exp"), 1)
        act.wait_ge(event("pa_shifted"), 1)
        A_(Pa, Pa, ACT.Exp, scale=1 / math.sqrt(HD)).then_inc(event("pa_exp"), 1)
        copy_out("oaT", oaT, lambda i: PS[:, i, 0:256].rearrange("p (b t) -> p b t", b=2))

        def decay(n):
            s, h = n // NH, n % NH
            if n >= 2:
                act.wait_ge(event("h_ready"), n - 1)
            A_(dA[n % 2].rearrange("p (b t) -> p b t", b=B)[:, :, 1:TS],
               delta[:, h, :].rearrange("p (b t) -> p b t", b=B)[:, :, 1:TS],
               ACT.Exp, scale=Aneg[:, h, s:s + 1]).then_inc(event("dA_ready"), 1)

        act.wait_ge(event("delta_ready"), 1)
        for s in range(DS):
            act.wait_ge(event("bc_ready"), s + 1)
            if s >= 2:
                act.wait_ge(event("dBu_ready"), NH * (s - 1))
            A_(Bsb[s % 2].rearrange("p (c n) -> p c n", c=2), PS[:, 4:6, 0:W384], ACT.Copy)\
                .then_inc(event("b_copied"), 1)
            if s >= 2:
                act.wait_ge(event("hC_ready"), NH * (s - 1))
            A_(Csb[s % 2].rearrange("p (c n) -> p c n", c=2), PS[:, 6:8, 0:W384], ACT.Copy)\
                .then_inc(event("c_copied"), 1)
            for h in range(NH):
                decay(NH * s + h)

        for c in range(2):
            copy_out(f"x4T.{c}", half(xT, c), bank4)
        for c in range(2):
            copy_out(f"q5.{c}", half(qT, c), bank4)
        attention_scalar(at5)

        for c in range(2):
            copy_out(f"x5T.{c}", half(xT, c), bank4)
        dring.wait_copied(act, "logits6")
        A_(aff[:], aff[:], ACT.Exp).then_inc(event("aff_exp"), 1)
        for k in range(E1 * NI * 2):
            act.wait_ge(event("gate_ready"), k + 1)
            if k >= 4:
                act.wait_ge(event("hidden_ready"), k - 3)
            A_(silu6[k % 4], PS[:, k % 2, :], ACT.Silu).then_inc(event("silu_ready"), 1)

    @block.vector
    def _(dve):
        V_ = nc.vector

        def step(ins):
            dve.wait_ge(dve_step.sem, dve_step.then(ins))

        def take(name):
            return dring.take(dve, name)

        def bank_full(i, p=128, n=512):
            return PS[0:p, i, 0:n]

        def half(t, c):
            return t[:, c * HB:(c + 1) * HB, :]

        var_sent = Count(ln_var)

        def norm_halves(src, dst, done, halves=(0, 1)):
            for c in halves:
                for b in range(c * HB, (c + 1) * HB):
                    ins = V_.bn_stats(st[:, b, :], src[:, b, :])
                step(ins)
                for b in range(c * HB, (c + 1) * HB):
                    ins = V_.bn_aggr(mv[:, b, :], st[:, b, :])
                step(ins)
                var_sent.then(V_.tensor_scalar(ve[:, c * HB:(c + 1) * HB], mv[:, c * HB:(c + 1) * HB, 1], EPS, None, ALU.add))
            for c in halves:
                dve.wait_ge(ln_rstd, var_sent.n - len(halves) + halves.index(c) + 1)
                for b in range(c * HB, (c + 1) * HB):
                    ins = V_.tensor_scalar(dst[:, b, :], src[:, b, :], mv[:, b, 0:1], rstd[:, b:b + 1],
                                           ALU.subtract, ALU.mult)
                ins.then_inc(event(done), 1)

        def centre(W, k):
            w = W.rearrange("p (h d) -> p h d", h=H)
            step(V_.tensor_reduce(wmean[:, k, :], w, axis=AX.X, op=ALU.add))
            step(V_.tensor_scalar(wmean[:, k, :], wmean[:, k, :], 1.0 / HD, None, ALU.mult))
            return V_.tensor_tensor(w, w, wmean[:, k, :].rearrange("p (h o) -> p h o", o=1).to_broadcast([128, H, HD]),
                                    ALU.subtract)

        def head_norm(rows, squares, sums, first, done):
            dve.wait_ge(event(squares), 1)
            V_.tensor_reduce(hss[0:rows], sq[0:rows].rearrange("p b (h d) -> p (b h) d", d=HD), axis=AX.X,
                             op=ALU.add).then_inc(event(sums), 1)
            dve.wait_ge(event(sums), 1)
            step(V_.tensor_scalar(hvar[0:rows], hss[0:rows], 1.0 / HD, EPS, ALU.mult, ALU.add))
            dve.wait_ge(event(first), 1)
            step(V_.tensor_tensor(hr1[0:rows], hr0[0:rows], hr0[0:rows], ALU.mult))
            step(V_.tensor_tensor(hr1[0:rows], hr1[0:rows], hvar[0:rows], ALU.mult))
            step(V_.tensor_scalar(hr1[0:rows], hr1[0:rows], -0.5, 1.5, ALU.mult, ALU.add))
            step(V_.tensor_tensor(hr1[0:rows], hr1[0:rows], hr0[0:rows], ALU.mult))
            V_.tensor_tensor(sq[0:rows].rearrange("p b (h d) -> p (b h) d", d=HD),
                             qc[0:rows].rearrange("p b (h d) -> p (b h) d", d=HD),
                             hr1[0:rows].rearrange("p (n o) -> p n o", o=1).to_broadcast([rows, B * H, HD]),
                             ALU.mult).then_inc(event(done), 1)

        def attention_vector(at):
            nk = at.nk

            def scores(u):
                return PS[:, u % 3, 0:J * nk].rearrange("p (j k) -> p j k", j=J)

            for s in range(-1, NU + 16):
                if s + 1 < NU:
                    u = s + 1
                    dve.wait_ge(at.scores_ready, u + 1)
                    if u >= 3:
                        dve.wait_ge(at.shifted, u - 2)
                    V_.tensor_reduce(mx[:, u % 3, :], scores(u), axis=AX.X, op=ALU.max).then_inc(at.max_ready, 1)
                if 0 <= s < NU:
                    dve.wait_ge(at.max_ready, s + 1)
                    if s >= 3:
                        dve.wait_ge(at.probsT_ready, s - 2)
                    V_.tensor_tensor(Eb[:, s % 3, :, 0:nk], scores(s),
                                     mx[:, s % 3, :].rearrange("p (j o) -> p j o", o=1).to_broadcast([128, J, nk]),
                                     ALU.subtract).then_inc(at.shifted, 1)

                def row_of(lag):
                    b = (s - lag) // G
                    return b if s >= lag and (s - lag) % G == 0 and b < B else None

                if (b := row_of(6)) is not None:
                    dve.wait_ge(at.out_ready, b + 1)
                    if b >= 2:
                        dve.wait_ge(at.normed, b - 1)
                    o = PS[:, 6, :].rearrange("p (h w) -> p h w", h=H)
                    ins = V_.reciprocal(rs[:, b % 2, :].rearrange("p (h o) -> p h o", o=1), o[:, :, HD:HD + 1])
                    if at.masked:
                        step(ins)
                        ins = V_.tensor_scalar(rs[:, b % 2, :], rs[:, b % 2, :], anykey[:], None, ALU.mult)
                    ins.then_inc(at.recip_ready, 1)
                if (b := row_of(7)) is not None:
                    dve.wait_ge(at.recip_ready, b + 1)
                    if b >= 2:
                        dve.wait_ge(at.normedT_ready, b - 1)
                    o = PS[:, 6, :].rearrange("p (h w) -> p h w", h=H)
                    V_.tensor_tensor(oN[:, b % 2, :].rearrange("p (h d) -> p h d", h=H), o[:, :, 0:HD],
                                     rs[:, b % 2, :].rearrange("p (h o) -> p h o", o=1).to_broadcast([128, H, HD]),
                                     ALU.mult).then_inc(at.normed, 1)
                if (b := row_of(10)) is not None:
                    dve.wait_ge(at.proj_ready, b + 1)
                    V_.tensor_tensor(R[:, b, :], at.XB[:, b, :], PS[:, 7, 128:256], ALU.add)\
                        .then_inc(at.residual_ready, 1)
                if (b := row_of(11)) is not None:
                    dve.wait_ge(at.residual_ready, b + 1)
                    V_.bn_stats(st[:, b, :], R[:, b, :]).then_inc(at.stats_ready, 1)
                if (b := row_of(12)) is not None:
                    dve.wait_ge(at.stats_ready, b + 1)
                    V_.bn_aggr(mv[:, b, :], st[:, b, :]).then_inc(at.var_ready, 1)
                if (b := row_of(13)) is not None:
                    dve.wait_ge(at.var_ready, b + 1)
                    V_.tensor_scalar(ve[:, b:b + 1], mv[:, b, 1:2], EPS, None, ALU.add).then_inc(at.eps_ready, 1)
                if (b := row_of(15)) is not None:
                    dve.wait_ge(at.rstd_ready, b + 1)
                    V_.tensor_scalar(at.Xout[:, b, :], R[:, b, :], mv[:, b, 0:1], rstd[:, b:b + 1],
                                     ALU.subtract, ALU.mult).then_inc(at.x_ready, 1)

        def wide(v, shape):
            return v.rearrange("p (b o) -> p b o", o=1).to_broadcast(shape)

        dve.wait_ge(const_ready, 1)
        step(V_.tensor_reduce(headmask[:], ident[:].rearrange("p (g j d) -> p j g d", g=G, j=J), axis=AX.XY, op=ALU.add))
        loaded(dve, "a1")
        V_.tensor_scalar(mb1[:], headmask[:], bqk1[:, 1:2], None, ALU.mult).then_inc(event("small1"), 1)
        loaded(dve, "x0")
        norm_halves(X[0], XH, "xh1", (0,))
        loaded(dve, "x1")
        norm_halves(X[0], XH, "xh1", (1,))
        loaded(dve, "l2")
        centre(Wkv2[:, 0:D], 0).then_inc(event("w2_centred"), 1)
        centre(Wq2[:], 1).then_inc(event("w2_centred"), 1)
        V_.tensor_scalar(sc2[:], headmask[:], gb2[:, 0:1], None, ALU.mult)
        V_.tensor_scalar(sh2[:], headmask[:], gb2[:, 1:2], None, ALU.mult).then_inc(event("small2"), 1)
        for c in range(2):
            i = take(f"v1.{c}")
            V_.tensor_tensor(V1[:, c * HB:(c + 1) * HB, :, 0:HD],
                             bank4(i).rearrange("p b (h d) -> p b h d", h=H),
                             bv1[:].rearrange("p (o h d) -> p o h d", o=1, h=H).to_broadcast([128, HB, H, HD]),
                             ALU.add).then_inc(dring.copied, 1)
        for p in range(4):
            kv = PS[0:NC, take(f"kv.{p}"), :].rearrange("p (b n) -> p b n", b=2)
            V_.tensor_copy(qc[0:NC, 2 * p:2 * p + 2, :], kv[:, :, 0:D])
            V_.tensor_copy(V2[:, 2 * p:2 * p + 2, :, 0:HD], kv[:, :, D:2 * D].rearrange("p b (h d) -> p b h d", h=H))\
                .then_inc(dring.copied, 1)
        loaded(dve, "l5")
        V_.tensor_scalar(maskneg[:], mask8[:], MASKED, None, ALU.mult)
        step(V_.tensor_reduce(nmasked[:], mask8[:], axis=AX.X, op=ALU.add))
        step(V_.tensor_scalar(anykey[:], nmasked[:], float(NC), None, ALU.is_lt))
        for c in range(2):
            V_.tensor_copy(V5[:, c * HB:(c + 1) * HB, :, 0:HD],
                           bank4(take(f"v5.{c}"), NC).rearrange("p b (h d) -> p b h d", h=H)).then_inc(dring.copied, 1)
        head_norm(NC, "k_sq", "k_ss", "k_rstd", "kn_ready")
        dve.wait_ge(at1.xb_ready, 1)
        attention_vector(at1)

        for c in range(2):
            ins = V_.tensor_copy(half(qc, c), bank4(take(f"q2.{c}")))
            ins.then_inc(dring.copied, 1)
        head_norm(128, "q_sq", "q_ss", "q_rstd", "qn_ready")
        dve.wait_ge(at2.xb_ready, 1)
        attention_vector(at2)

        aring.wait_copied(dve, "x2T.1")
        step(V_.tensor_reduce(pooledT[:], xT[:], axis=AX.X, op=ALU.add))
        V_.tensor_scalar(pooledT[:], pooledT[:], 1.0 / T, None, ALU.mult).then_inc(event("pooled"), 1)
        i = take("logits8")
        step(V_.tensor_reduce(m8[:], PS[0:8, i, 0:8], axis=AX.X, op=ALU.max))
        V_.tensor_scalar(g8[:], PS[0:8, i, 0:8], m8[:], None, ALU.subtract).then_inc(dring.copied, 1)
        dve.wait_ge(event("gate3_exp"), 1)
        step(V_.tensor_reduce(m8[:], g8[:], axis=AX.X, op=ALU.add))
        step(V_.reciprocal(m8[:], m8[:]))
        step(V_.tensor_scalar(g8[:], g8[:], m8[:], None, ALU.mult))
        other = g8[:].rearrange("p (o f) -> p o f", o=1).to_broadcast([8, 8, 8])
        own = g8[:].rearrange("p (e o) -> p e o", o=1).to_broadcast([8, 8, 8])
        V_.tensor_tensor(t64[:], other, own, ALU.is_gt)
        step(V_.tensor_tensor(e64[:], other, own, ALU.is_equal))
        step(V_.tensor_tensor(e64[:], e64[:], earlier[:], ALU.mult))
        step(V_.tensor_tensor(t64[:], t64[:], e64[:], ALU.add))
        step(V_.tensor_reduce(r8[:], t64[:], axis=AX.X, op=ALU.add))
        step(V_.tensor_scalar(r8[:], r8[:], 2.0, None, ALU.is_lt))
        step(V_.tensor_tensor(c8[:], r8[:], g8[:], ALU.mult))
        step(V_.tensor_reduce(m8[:], c8[:], axis=AX.X, op=ALU.add))
        step(V_.tensor_scalar(m8[:], m8[:], 1e-8, None, ALU.add))
        step(V_.reciprocal(m8[:], m8[:]))
        V_.tensor_scalar(c8[:], c8[:], m8[:], None, ALU.mult).then_inc(event("c8_ready"), 1)
        V_.tensor_copy(cT[:], PS[0:8, take("cT"), 0:8]).then_inc(dring.copied, 1)
        V_.tensor_copy(cexp[:], PS[:, take("cexp"), 0:4 * B].rearrange("p (t b) -> p t b", t=4)).then_inc(dring.copied, 1)
        dve.wait_ge(dring.copied, dring.emptied)
        for c in range(2):
            for t in range(4):
                aring.wait_copied(dve, f"hid.{t}.{c}")
                v = hid[:, t, c * 512:(c + 1) * 512].rearrange("p (b n) -> p b n", b=HB)
                V_.tensor_tensor(v, v, wide(cexp[:, t, c * HB:(c + 1) * HB], [128, HB, T]), ALU.mult)\
                    .then_inc(event("hid_scaled"), 1)
        for c in range(2):
            V_.tensor_tensor(half(R, c), half(X[0], c), bank4(take(f"up.{c}")), ALU.add).then_inc(dring.copied, 1)
        dve.wait_ge(dring.copied, dring.emptied)
        norm_halves(R, X[1], "x3")

        dve.wait_ge(event("x3"), 2)
        norm_halves(X[1], XH, "xh4")
        aring.wait_copied(dve, "srow.1")
        step(V_.tensor_tensor(gt, Srow, ident[:].rearrange("p (o t) -> p o t", o=1).to_broadcast([128, B, T]), ALU.mult))
        step(V_.tensor_reduce(scol[:], gt, axis=AX.X, op=ALU.add))
        V_.tensor_tensor(gt, Srow, wide(scol[:], [128, B, T]), ALU.is_gt)
        step(V_.tensor_tensor(eq, Srow, wide(scol[:], [128, B, T]), ALU.is_equal))
        step(V_.tensor_tensor(eq, eq, before[:].rearrange("p (o t) -> p o t", o=1).to_broadcast([128, B, T]), ALU.mult))
        step(V_.tensor_tensor(gt, gt, eq, ALU.add))
        step(V_.tensor_reduce(rank[:], gt, axis=AX.X, op=ALU.add))
        step(V_.tensor_scalar(sel[:], rank[:], float(KSEL), None, ALU.is_lt))
        V_.tensor_scalar(unsel[:], sel[:], -1.0, 1.0, ALU.mult, ALU.add).then_inc(event("unsel"), 1)
        V_.tensor_copy(cumU[:], PS[:, take("cumU"), 0:B]).then_inc(dring.copied, 1)
        dve.wait_ge(dring.copied, dring.emptied)
        step(V_.tensor_scalar(posa[:], cumU[:], -1.0, slot_base[:], ALU.mult, ALU.add))
        step(V_.tensor_tensor(posa[:], posa[:], sel[:], ALU.mult))
        step(V_.tensor_tensor(pos[:], cumU[:], unsel[:], ALU.mult))
        step(V_.tensor_tensor(pos[:], pos[:], posa[:], ALU.add))
        V_.tensor_tensor(Perm, colnum[:].rearrange("p (o t) -> p o t", o=1).to_broadcast([128, B, T]),
                         wide(pos[:], [128, B, T]), ALU.is_equal).then_inc(event("perm"), 1)
        loaded(dve, "l4", "ssm")
        V_.tensor_scalar(mb4[:], headmask[:], bqk4[:, 1:2], None, ALU.mult).then_inc(event("small4"), 1)
        V_.tensor_tensor(va, PS[:, take("va"), 0:256].rearrange("p (b n) -> p b n", b=2),
                         bv4[:].rearrange("p (o n) -> p o n", o=1).to_broadcast([128, 2, D]), ALU.add)\
            .then_inc(dring.copied, 1)
        W384 = HB * TS
        for c in range(2):
            V_.tensor_copy(BC[:, c * W384:(c + 1) * W384], PS[0:96, take(f"BC.{c}"), 0:W384]).then_inc(dring.copied, 1)
        dve.wait_ge(dring.copied, dring.emptied)
        step(V_.tensor_copy(BCh, BC))
        V_.tensor_copy(BC3[0:32], BCh[0:32])
        step(V_.tensor_tensor(BC, BC, BCh, ALU.subtract))
        step(V_.tensor_copy(BCm, BC))
        V_.tensor_copy(BC3[32:64], BCm[32:64])
        V_.tensor_tensor(BC3[64:96], BC[64:96], BCm[64:96], ALU.subtract).then_inc(event("bc_parts"), 1)
        dve.wait_ge(event("sa_ready"), 1)
        Sa = PS[:, 0:4, 0:256].rearrange("p g (n k) -> p g n k", k=KSEL)
        step(V_.tensor_reduce(mxa[:].rearrange("p (g n) -> p g n", g=G), Sa, axis=AX.X, op=ALU.max))
        for g in range(G):
            ins = V_.tensor_tensor(Pa[:, 8 * g:8 * g + 8, :], Sa[:, g], wide(mxa[:, 8 * g:8 * g + 8], [128, 8, KSEL]),
                                   ALU.subtract)
        ins.then_inc(event("pa_shifted"), 1)
        dve.wait_ge(event("softplus_parts"), 1)
        step(V_.tensor_scalar(sp_abs, sp_exp, 1.0, -1.0, ALU.add, ALU.add))
        step(V_.tensor_tensor(sp_abs, sp_exp, sp_abs, ALU.subtract))
        step(V_.tensor_tensor(sp_abs, sp_abs, sp_log, ALU.add))
        step(V_.tensor_tensor(delta, sp_abs, sp_relu, ALU.add))
        dve.wait_ge(event("a_exp"), 1)
        V_.tensor_scalar(Aneg[:], Aneg[:], -1.0, None, ALU.mult)
        for i in range(2):
            V_.memset(dA[i].rearrange("p (b t) -> p b t", b=B)[:, :, 0:1], 0.0)
        V_.tensor_tensor(du[:], delta, xc, ALU.mult).then_inc(event("delta_ready"), 1)
        dve.wait_ge(event("delta_ready"), 1)
        dve.wait_ge(event("pa_exp"), 1)
        step(V_.tensor_reduce(sma[:], Pa, axis=AX.X, op=ALU.add))
        step(V_.reciprocal(sma[:], sma[:]))
        step(V_.tensor_tensor(Pa, Pa, wide(sma[:], [128, 2 * H, KSEL]), ALU.mult))
        V_.transpose(PaT.rearrange("p n k -> p (n k)"), Pa.rearrange("p n k -> p (n k)")).then_inc(event("paT"), 1)
        dve.wait_ge(event("oa_ready"), 1)
        for c in range(4):
            ins = V_.tensor_copy(oa[32 * c:32 * c + 32, :, :],
                                 PS[32 * c:32 * c + 32, 4 + c, 0:256].rearrange("p (b n) -> p b n", b=2))
        ins.then_inc(event("oa_copied"), 1)
        loaded(dve, "bc4")
        for c in range(2):
            V_.tensor_tensor(dpos[TS:T, c * HB:(c + 1) * HB, :],
                             PS[TS:T, take(f"dposA.{c}"), :].rearrange("p (b n) -> p b n", b=HB),
                             posbias[TS:T, :].rearrange("p (o n) -> p o n", o=1).to_broadcast([KSEL, HB, D]),
                             ALU.add).then_inc(dring.copied, 1)
        for n in range(NH * DS):
            s, h = n // NH, n % NH
            dve.wait_ge(event("b_copied"), s + 1)
            if n >= 2:
                dve.wait_ge(event("h_ready"), n - 1)
            V_.tensor_tensor(dBu[n % 2], du[:, h, :], Bsb[s % 2], ALU.mult).then_inc(event("dBu_ready"), 1)
            if n >= 1:
                m = n - 1
                dve.wait_ge(event("dBu_ready"), m + 1)
                dve.wait_ge(event("dA_ready"), m + 1)
                if m >= 2:
                    dve.wait_ge(event("hC_ready"), m - 1)
                V_.tensor_tensor_scan(hst[m % 2], dA[m % 2], dBu[m % 2], 0.0, ALU.mult, ALU.add)\
                    .then_inc(event("h_ready"), 1)
        m = NH * DS - 1
        dve.wait_ge(event("dBu_ready"), m + 1)
        dve.wait_ge(event("dA_ready"), m + 1)
        dve.wait_ge(event("hC_ready"), m - 1)
        V_.tensor_tensor_scan(hst[m % 2], dA[m % 2], dBu[m % 2], 0.0, ALU.mult, ALU.add).then_inc(event("h_ready"), 1)
        dve.wait_ge(event("hC_used"), NH * DS)
        for h in range(NH):
            ins = V_.tensor_tensor(xc[:, h, :].rearrange("p (c n) -> p c n", c=2), PS[:, 2 * h:2 * h + 2, 0:W384],
                                   zs[:, h, :].rearrange("p (c n) -> p c n", c=2), ALU.mult)
        ins.then_inc(event("y_gated"), 1)
        for c in range(2):
            V_.tensor_copy(dpos[0:TS, c * HB:(c + 1) * HB, :],
                           PS[0:TS, take(f"dposS.{c}"), :].rearrange("p (b n) -> p b n", b=HB)).then_inc(dring.copied, 1)
        for c in range(2):
            i = take(f"dl.{c}")
            V_.scalar_tensor_tensor(half(R, c), half(X[1], c), 2.0, bank4(i), ALU.mult, ALU.add).then_inc(dring.copied, 1)
        dve.wait_ge(dring.copied, dring.emptied)
        norm_halves(R, X[0], "x4")
        dve.wait_ge(event("x4"), 2)
        attention_vector(at5)

        i = take("logits6")
        lg = PS[:, i, 0:B * E1].rearrange("p (b e) -> p b e", b=B)
        step(V_.tensor_reduce(am[:], lg, axis=AX.X, op=ALU.max))
        V_.tensor_tensor(aff[:], lg, wide(am[:], [128, B, E1]), ALU.subtract).then_inc(dring.copied, 1)
        dve.wait_ge(dring.copied, dring.emptied)
        dve.wait_ge(event("aff_exp"), 1)
        step(V_.tensor_reduce(am[:], aff[:], axis=AX.X, op=ALU.add))
        step(V_.reciprocal(am[:], am[:]))
        step(V_.tensor_tensor(aff[:], aff[:], wide(am[:], [128, B, E1]), ALU.mult))
        dve.wait_ge(at5.x_ready, B)
        for e in range(E1 + 1):
            if e < E1:
                for k in range(NI * 2):
                    n = e * NI * 2 + k
                    i, c = k // 2, k % 2
                    dve.wait_ge(event("up_ready"), n + 1)
                    dve.wait_ge(event("silu_ready"), n + 1)
                    if e >= 2:
                        dve.wait_ge(event("down_ready"), 2 * (e - 1))
                    V_.tensor_tensor(hidE[e % 2][:, i, c * 512:(c + 1) * 512], silu6[n % 4], PS[:, 2 + n % 2, :],
                                     ALU.mult).then_inc(event("hidden_ready"), 1)
            if e >= 1:
                p = e - 1
                for c in range(2):
                    dve.wait_ge(event("down_ready"), 2 * p + c + 1)
                    for b4 in range(HB):
                        b = c * HB + b4
                        if p >= 1:
                            dve.wait_ge(event("summed"), B * (p - 1) + b + 1)
                        V_.scalar_tensor_tensor(R[:, b, :], PS[:, 4 + (2 * p + c) % 4, b4 * D:(b4 + 1) * D],
                                                aff[:, b, p:p + 1], (R if p else X[1])[:, b, :],
                                                ALU.mult, ALU.add).then_inc(event("summed"), 1)
        dve.wait_ge(event("summed"), B * E1)
        norm_halves(R, X[0], "out_ready")

    @block.tensor
    def _(pe):
        M_ = nc.tensor.matmul

        def fill(ring, name):
            return ring.fill(pe, name)

        def half(t, c):
            return t[:, c * HB:(c + 1) * HB, :]

        def flat(ap):
            return ap.rearrange("p b t -> p (b t)")

        def transposes(name, srcs, rows, cols):
            i = fill(aring, name)
            for k, src in enumerate(srcs):
                ins = nc.tensor.transpose(PS[0:cols, i, k * rows:(k + 1) * rows], src, ident[0:rows, 0:rows])
            ins.then_inc(aring.full, 1)

        def product(ring, name, lhsT, rhs, rows=128, cols=512):
            i = fill(ring, name)
            M_(PS[0:rows, i, 0:cols], lhsT, rhs, start=True, stop=True).then_inc(ring.full, 1)

        def row_products(ring, name, lhsTs, rhs, rows=128, width=D):
            i = fill(ring, name)
            for k, lhsT in enumerate(lhsTs):
                ins = M_(PS[0:rows, i, k * width:(k + 1) * width], lhsT, rhs, start=True, stop=True)
            ins.then_inc(ring.full, 1)

        def x_transposed(stage, X_, ready, per_half):
            for c in range(2):
                pe.wait_ge(ready, per_half * (c + 1))
                transposes(f"{stage}.{c}", [X_[:, b, :] for b in range(c * HB, (c + 1) * HB)], 128, 128)

        def attention_tensor(at):
            nk = at.nk
            aring.drain(pe)
            dring.drain(pe)
            for s in range(-2, NU + 12):
                if s + 2 < NU:
                    u = s + 2
                    b, g = u // G, u % G
                    if u >= 3:
                        pe.wait_ge(at.shifted, u - 2)
                    r = slice(32 * g, 32 * g + 32)
                    dst = PS[:, u % 3, 0:J * nk].rearrange("p (j k) -> p j k", j=J)
                    ins = M_(dst, qT[r, b, :], at.kM[r, :, b, :], start=True, stop=not at.masked)
                    if at.masked:
                        ins = M_(dst, identb[:], maskneg[:].rearrange("p (o k) -> p o k", o=1).to_broadcast([128, J, nk]),
                                 start=False, stop=True)
                    ins.then_inc(at.scores_ready, 1)
                if 0 <= s < NU:
                    pe.wait_ge(at.exp_ready, s + 1)
                    if s >= 2:
                        pe.wait_ge(at.probsT_copied, s - 1)
                    for j in range(J):
                        ins = nc.tensor.transpose(PS[0:nk, 3 + s % 2, 128 * j:128 * j + 128], Eb[:, s % 3, j, 0:nk], ident[:])
                    ins.then_inc(at.probsT_ready, 1)
                if 1 <= s <= NU:
                    u = s - 1
                    b, g = u // G, u % G
                    pe.wait_ge(at.probsT_copied, u + 1)
                    if g == 0 and b:
                        pe.wait_ge(at.outT_copied, b)
                    for j in range(J):
                        ins = M_(PS[32 * j:32 * j + 32, 5, 128 * g:128 * g + 128], at.V[0:nk, b, J * g + j, :],
                                 PT[0:nk, u % 3, j, :], start=True, stop=True)
                    ins.then_inc(at.pv_done, 1)

                def row_of(lag):
                    b = (s - lag) // G
                    return b if s >= lag and (s - lag) % G == 0 and b < B else None

                if (b := row_of(6)) is not None:
                    pe.wait_ge(at.outT_copied, b + 1)
                    if b:
                        pe.wait_ge(at.normed, b)
                    for g in range(G):
                        ins = nc.tensor.transpose(PS[:, 6, 128 * g:128 * g + 128], outT[:, g, :], ident[:])
                    ins.then_inc(at.out_ready, 1)
                if (b := row_of(8)) is not None:
                    pe.wait_ge(at.normed, b + 1)
                    if b:
                        pe.wait_ge(at.normedT_copied, b)
                    nc.tensor.transpose(PS[:, 7, 0:128], oN[:, b % 2, :], ident[:]).then_inc(at.normedT_ready, 1)
                if (b := row_of(9)) is not None:
                    pe.wait_ge(at.normedT_copied, b + 1)
                    if b:
                        pe.wait_ge(at.residual_ready, b)
                    M_(PS[:, 7, 128:256], oNT[:, b % 2, :], at.Wo, start=True, stop=True).then_inc(at.proj_ready, 1)
            pe.wait_ge(at.residual_ready, B)

        pe.wait_ge(const_ready, 1)
        loaded(pe, "a1")
        for c in range(2):
            pe.wait_ge(event("xh1"), c + 1)
            transposes(f"x0T.{c}", [XH[:, b, :] for b in range(c * HB, (c + 1) * HB)], 128, 128)
            aring.wait_copied(pe, f"x0T.{c}")
            product(aring, f"q1.{c}", Wqkv1[:, 0:D], half(xT, c))
            product(aring, f"k1.{c}", Wqkv1[:, D:2 * D], half(xT, c))
            row_products(dring, f"v1.{c}", [xT[:, b, :] for b in range(c * HB, (c + 1) * HB)], Wqkv1[:, 2 * D:3 * D])
        loaded(pe, "ctx")
        for c in range(2):
            transposes(f"ctxT.{c}", [ctxN[:, b, :] for b in range(c * HB, (c + 1) * HB)], NC, 128)
        loaded(pe, "l5", "l3", "l2")
        transposes("W5T", [W5[:, k, :] for k in range(4)], 128, 128)
        transposes("down3T", [down3[:, k, :] for k in range(4)], 128, 128)
        transposes("up3T", [up3[:, 2 * k:2 * k + 2, :].rearrange("p e c -> p (e c)") for k in range(4)], 128, 128)
        transposes("gate3T", [gate3[:]], E0, 128)
        aring.wait_copied(pe, "ctxT.1")
        pe.wait_ge(event("w2_centred"), 1)
        for p in range(4):
            row_products(dring, f"kv.{p}", [ctxT[:, b, :] for b in (2 * p, 2 * p + 1)], Wkv2[:], NC, 2 * D)
        aring.wait_copied(pe, "W5T")
        for c in range(2):
            product(aring, f"k5.{c}", W5T[:, 1, :], half(ctxT, c), cols=HB * NC)
        for c in range(2):
            row_products(dring, f"v5.{c}", [ctxT[:, b, :] for b in range(c * HB, (c + 1) * HB)], W5T[:, 2, :], NC)
        pe.wait_ge(event("kn_ready"), 1)
        for c in range(2):
            transposes(f"k2.{c}", [sq[0:NC, b, :] for b in range(c * HB, (c + 1) * HB)], NC, 128)
        pe.wait_ge(event("v_ones"), 1)
        attention_tensor(at1)

        x_transposed("x1T", X[1], at1.x_ready, HB)
        pe.wait_ge(event("w2_centred"), 2)
        for c in range(2):
            aring.wait_copied(pe, f"x1T.{c}")
            row_products(dring, f"q2.{c}", [xT[:, b, :] for b in range(c * HB, (c + 1) * HB)], Wq2[:])
        pe.wait_ge(event("qn_ready"), 1)
        for c in range(2):
            transposes(f"q2T.{c}", [sq[:, b, :] for b in range(c * HB, (c + 1) * HB)], 128, 128)
        attention_tensor(at2)

        x_transposed("x2T", X[0], at2.x_ready, HB)
        pe.wait_ge(event("pooled"), 1)
        product(dring, "logits8", pooledT[:], gate3T[:], 8, 8)
        for c in range(2):
            for t in range(4):
                product(aring, f"hid.{t}.{c}", down3T[:, t * 128:(t + 1) * 128], half(xT, c))
        pe.wait_ge(event("c8_ready"), 1)
        i = fill(dring, "cT")
        nc.tensor.transpose(PS[0:8, i, 0:8], c8[:], ident[0:8, 0:8]).then_inc(dring.full, 1)
        dring.wait_copied(pe, "cT")
        i = fill(dring, "cexp")
        for t in range(4):
            ins = M_(PS[:, i, t * B:(t + 1) * B], spread8[:, t * 128:(t + 1) * 128], cT[:], start=True, stop=True)
        ins.then_inc(dring.full, 1)
        for c in range(2):
            pe.wait_ge(event("hid_scaled"), 4 * (c + 1))
            i = fill(dring, f"up.{c}")
            for b4 in range(HB):
                b = c * HB + b4
                dst = PS[:, i, b4 * D:(b4 + 1) * D]
                for t in range(4):
                    M_(dst, hid[:, t, b * T:(b + 1) * T], up3T[:, t, :], start=(t == 0), stop=False)
                ins = M_(dst, cT[:, b:b + 1].to_broadcast([8, 128]), upb3[:], start=False, stop=True)
            ins.then_inc(dring.full, 1)

        loaded(pe, "l4")
        x_transposed("xnT", XH, event("xh4"), 1)
        for c in range(2):
            aring.wait_copied(pe, f"xnT.{c}")
            product(aring, f"router.{c}", rw1[:], half(xT, c), rows=D // 2)
        for c in range(2):
            aring.wait_copied(pe, f"router.{c}")
            product(aring, f"srow.{c}", rw2[:].to_broadcast([D // 2, 128]), half(hrT, c))
        pe.wait_ge(event("unsel"), 1)
        product(dring, "cumU", after[:], unsel[:], cols=B)
        pe.wait_ge(event("perm"), 1)
        for c in range(2):
            transposes(f"permT.{c}", [Perm[:, b, :] for b in range(c * HB, (c + 1) * HB)], 128, 128)
        for c in range(2):
            i = fill(aring, f"xpT.{c}")
            for b4 in range(HB):
                ins = M_(PS[:, i, b4 * T:(b4 + 1) * T], XH[:, c * HB + b4, :], Perm[:, c * HB + b4, :], start=True, stop=True)
            ins.then_inc(aring.full, 1)
        loaded(pe, "ssm")
        pe.wait_ge(event("ssm_weights"), 1)
        aring.wait_copied(pe, "xpT.1")
        W384 = HB * TS
        for h in range(NH):
            for c in range(2):
                i = fill(aring, f"conv.{h}.{c}")
                for j in range(DC):
                    ins = M_(PS[:, i, 0:W384], convin[:, j, 128 * h:128 * h + 128],
                             xpT[:, c * HB:(c + 1) * HB, j:j + TS], start=(j == 0), stop=(j == DC - 1))
                ins.then_inc(aring.full, 1)
        for h in range(NH):
            for c in range(2):
                product(aring, f"z.{h}.{c}", inw4[:, DIN + 128 * h:DIN + 128 * h + 128],
                        xpT[:, c * HB:(c + 1) * HB, DC - 1:DC - 1 + TS], cols=W384)
        chosen = xpT[:, :, DC - 1 + TS:]
        product(aring, "qa", Wqkvo4[:, 0, :], chosen, cols=B * KSEL)
        product(aring, "ka", Wqkvo4[:, 1, :], chosen, cols=B * KSEL)
        i = fill(dring, "va")
        for b in range(B):
            n, c = b // 4, b % 4
            ins = M_(PS[32 * c:32 * c + 32, i, n * D:(n + 1) * D], chosen[:, b, :], Wqkvo4[:, 2, :], start=True, stop=True)
        ins.then_inc(dring.full, 1)
        aring.wait_copied(pe, "conv.1.1")
        for c in range(2):
            w = slice(c * W384, (c + 1) * W384)
            i = fill(aring, f"dt.{c}")
            for h in range(NH):
                ins = M_(PS[0:DTR, i, 0:W384], xproj[:, h, 0:DTR], xc[:, h, w], start=(h == 0), stop=(h == NH - 1))
            ins.then_inc(aring.full, 1)
        for c in range(2):
            w = slice(c * W384, (c + 1) * W384)
            i = fill(dring, f"BC.{c}")
            for h in range(NH):
                ins = M_(PS[0:96, i, 0:W384], xprojBC[:, h, :], xc[:, h, w], start=(h == 0), stop=(h == NH - 1))
            ins.then_inc(dring.full, 1)
        aring.wait_copied(pe, "dt.1")
        for h in range(NH):
            for c in range(2):
                product(aring, f"delta.{h}.{c}", dtw[:, 128 * h:128 * h + 128], dtp[:, c * W384:(c + 1) * W384], cols=W384)
        aring.drain(pe)
        for g in range(G):
            for b in range(B):
                n, c = b // 4, b % 4
                ins = M_(PS[32 * c:32 * c + 32, g, n * 128:(n + 1) * 128].rearrange("p (j k) -> p j k", j=J),
                         qTa[32 * g:32 * g + 32, b, :], kMa[32 * g:32 * g + 32, :, b, :], start=True, stop=True)
        ins.then_inc(event("sa_ready"), 1)
        pe.wait_ge(event("paT"), 1)
        dring.drain(pe)
        for c in range(4):
            r = slice(32 * c, 32 * c + 32)
            for n in range(2):
                for hh in range(H):
                    g, j = hh // J, hh % J
                    ins = M_(PS[r, 4 + c, n * D + hh * HD:n * D + (hh + 1) * HD], PaT[r, 8 * g + 4 * n + j, :],
                             va[r, n, hh * HD:(hh + 1) * HD], start=True, stop=True)
        ins.then_inc(event("oa_ready"), 1)
        pe.wait_ge(event("oa_copied"), 1)
        transposes("oaT", [oa[:, n, :] for n in range(2)], 128, 128)
        aring.wait_copied(pe, "oaT")
        for c in range(2):
            i = fill(dring, f"dposA.{c}")
            for b4 in range(HB):
                ins = M_(PS[TS:T, i, b4 * D:(b4 + 1) * D], oaT[:, c, 32 * b4:32 * b4 + 32], Wqkvo4[:, 3, :],
                         start=True, stop=True)
            ins.then_inc(dring.full, 1)
        aring.drain(pe)
        for h in range(NH):
            for c in range(2):
                M_(PS[:, 2 * h + c, 0:W384], diagD[:, h, :], xc[:, h, c * W384:(c + 1) * W384], start=True, stop=False)
        dring.drain(pe)
        pe.wait_ge(event("bc_parts"), 1)

        def spread(s):
            if s:
                pe.wait_ge(event("b_copied"), s)
                pe.wait_ge(event("c_copied"), s)
            for k in range(2):
                for c in range(2):
                    ins = M_(PS[:, 4 + 2 * k + c, 0:W384], part_pick[:, DS * k + s:DS * k + s + 1].to_broadcast([96, 128]),
                             BC3[:, c * W384:(c + 1) * W384], start=True, stop=True)
            ins.then_inc(event("bc_ready"), 1)

        spread(0)
        for s in range(DS):
            if s + 1 < DS:
                spread(s + 1)
            for h in range(NH):
                n = NH * s + h
                pe.wait_ge(event("hC_ready"), n + 1)
                for c in range(2):
                    ins = M_(PS[:, 2 * h + c, 0:W384], ident[:], hC[n % 2][:, c * W384:(c + 1) * W384], start=False,
                             stop=(s == DS - 1))
                ins.then_inc(event("hC_used"), 1)
        pe.wait_ge(event("y_gated"), 1)
        for c in range(2):
            i = fill(dring, f"dposS.{c}")
            for b4 in range(HB):
                b = c * HB + b4
                for h in range(NH):
                    ins = M_(PS[0:TS, i, b4 * D:(b4 + 1) * D], xc[:, h, b * TS:(b + 1) * TS], outw4[:, h, :],
                             start=(h == 0), stop=(h == NH - 1))
            ins.then_inc(dring.full, 1)
        for c in range(2):
            dring.wait_copied(pe, f"dposS.{c}")
            i = fill(dring, f"dl.{c}")
            for b4 in range(HB):
                b = c * HB + b4
                ins = M_(PS[:, i, b4 * D:(b4 + 1) * D], PermT[:, b, :], dpos[:, b, :], start=True, stop=True)
            ins.then_inc(dring.full, 1)

        x_transposed("x4T", X[0], event("x4"), 1)
        for c in range(2):
            aring.wait_copied(pe, f"x4T.{c}")
            product(aring, f"q5.{c}", W5T[:, 0, :], half(xT, c))
        attention_tensor(at5)

        loaded(pe, "g6")
        x_transposed("x5T", X[1], at5.x_ready, HB)
        aring.wait_copied(pe, "x5T.1")
        row_products(dring, "logits6", [xT[:, b, :] for b in range(B)], gate6[:], width=E1)
        dring.drain(pe)

        def down(e):
            w = Wd6[e % 2]
            for c in range(2):
                if 2 * e + c >= 4:
                    pe.wait_ge(event("summed"), B * (e - 2) + HB * (c + 1))
                pe.wait_ge(event("hidden_ready"), NI * 2 * (e + 1))
                for b4 in range(HB):
                    b = c * HB + b4
                    for i in range(NI):
                        ins = M_(PS[:, 4 + (2 * e + c) % 4, b4 * D:(b4 + 1) * D], hidE[e % 2][:, i, b * T:(b + 1) * T],
                                 w[:, i, :], start=(i == 0), stop=(i == NI - 1))
                ins.then_inc(event("down_ready"), 1)

        for e in range(E1):
            pe.wait_ge(expert_loaded[e % 2], 48 * (e // 2 + 1))
            for i in range(NI):
                for c in range(2):
                    n = e * NI * 2 + 2 * i + c
                    if n >= 2:
                        pe.wait_ge(event("silu_ready"), n - 1)
                    M_(PS[:, n % 2, :], Wgu[e % 2][:, 0, i * 128:(i + 1) * 128], half(xT, c), start=True, stop=True)\
                        .then_inc(event("gate_ready"), 1)
                    if n >= 2:
                        pe.wait_ge(event("hidden_ready"), n - 1)
                    M_(PS[:, 2 + n % 2, :], Wgu[e % 2][:, 1, i * 128:(i + 1) * 128], half(xT, c), start=True, stop=True)\
                        .then_inc(event("up_ready"), 1)
            if e:
                down(e - 1)
        down(E1 - 1)


_INS = [
    'x', 'ctx_1024', 'mask_1x1xSxS2_bk1', 'L0_attn_ln_gamma', 'L0_attn_ln_beta', 'L0_attn_w_qkv', 'L0_attn_b_qkv',
    'L0_attn_w_out', 'L0_attn_b_out', 'L0_xattn_Wq', 'L0_xattn_Wkv', 'L0_xattn_Wp', 'L0_xattn_bp',
    'L0_xattn_ln_g', 'L0_xattn_ln_b', 'L0_ffn_gate_w', 'L0_ffn_down_w', 'L0_ffn_down_b', 'L0_ffn_up_w',
    'L0_ffn_up_b', 'L1_attn_ln_w', 'L1_attn_ln_b', 'L1_attn_r_w1', 'L1_attn_r_b1', 'L1_attn_r_w2', 'L1_attn_r_b2',
    'L1_attn_Wq', 'L1_attn_bq', 'L1_attn_Wk', 'L1_attn_bk', 'L1_attn_Wv', 'L1_attn_bv', 'L1_attn_Wo',
    'L1_attn_bo', 'L1_attn_in_w', 'L1_attn_conv_w', 'L1_attn_conv_b', 'L1_attn_xproj_w', 'L1_attn_dt_w',
    'L1_attn_dt_b', 'L1_attn_A_log', 'L1_attn_Dp', 'L1_attn_out_w', 'L1_xattn_W_q', 'L1_xattn_W_k',
    'L1_xattn_W_v', 'L1_xattn_W_o', 'L1_ffn_gate_w', 'L1_ffn_Wg', 'L1_ffn_Wu', 'L1_ffn_Wd',
]
_SHAPE = (B, T, D)


def kernel(**inputs):
    import concourse.bacc as _bacc
    from concourse.bass_utils import run_bass_kernel_spmd as _run

    nc = _bacc.Bacc("TRN2", target_bir_lowering=False, num_devices=1)
    arrays, args = {}, {}
    for name in _INS:
        x = np.ascontiguousarray(inputs[name])
        if x.dtype.kind == "b":
            x = x.reshape(-1).view(np.int32)
        arrays[f"in_{name}"] = x
        args[name] = nc.dram_tensor(f"in_{name}", x.shape, mybir.dt.from_np(x.dtype), kind="ExternalInput").ap()
    out = nc.dram_tensor("out_x", _SHAPE, F32, kind="ExternalOutput").ap()
    build(nc, args, out)
    return _run(nc, [arrays], core_ids=[0]).results[0]["out_x"]
```

```python
from contextlib import ExitStack
import math

import numpy as np

import concourse.bass as bass
from concourse import mybir

F32 = mybir.dt.float32
BF16 = mybir.dt.bfloat16
U8 = mybir.dt.uint8
ALU = mybir.AluOpType
ACT = mybir.ActivationFunctionType
AX = mybir.AxisListType

B, T, D = 8, 128, 128
H, HD = 16, 8
G = 4
J = H // G
NU = B * G
NC = 77
VW = 32
HB = B // 2
E0, BN = 8, 64
KSEL = T // 4
TS = T - KSEL
DC, DS, DTR = 4, 16, 8
DIN = 2 * D
NH = DIN // 128
E1, IW = 8, 256
NI = IW // 128
EPS = 1e-5
MASKED = -1e30


class Ring:

    def __init__(self, banks, full, copied, jobs):
        self.banks, self.full, self.copied, self.jobs = banks, full, copied, jobs
        self.index = {name: n for n, name in enumerate(jobs)}
        self.filled = self.emptied = 0

    def fill(self, pe, name):
        n, size = self.filled, len(self.banks)
        assert self.jobs[n] == name, (self.jobs[n], name)
        if n >= size:
            pe.wait_ge(self.copied, n - size + 1)
        self.filled += 1
        return self.banks[n % size]

    def take(self, reader, name):
        n = self.emptied
        assert self.jobs[n] == name, (self.jobs[n], name)
        reader.wait_ge(self.full, n + 1)
        self.emptied += 1
        return self.banks[n % len(self.banks)]

    def wait_copied(self, eng, *names):
        eng.wait_ge(self.copied, max(self.index[n] for n in names) + 1)

    def drain(self, pe):
        if self.filled:
            pe.wait_ge(self.copied, self.filled)


class Count:

    def __init__(self, sem):
        self.sem, self.n = sem, 0

    def then(self, ins):
        ins.then_inc(self.sem, 1)
        self.n += 1
        return self.n


class Attention:

    def __init__(self, sem, name, nk, scale, kM, V, Wo, XB, Xout, masked=False):
        self.nk, self.scale, self.kM, self.V = nk, scale, kM, V
        self.Wo, self.XB, self.Xout, self.masked = Wo, XB, Xout, masked
        self.queries_ready = sem(f"{name}_queries_ready")
        self.scores_ready = sem(f"{name}_scores_ready")
        self.max_ready = sem(f"{name}_max_ready")
        self.shifted = sem(f"{name}_shifted")
        self.exp_ready = sem(f"{name}_exp_ready")
        self.probsT_ready = sem(f"{name}_probsT_ready")
        self.probsT_copied = sem(f"{name}_probsT_copied")
        self.pv_done = sem(f"{name}_pv_done")
        self.outT_copied = sem(f"{name}_outT_copied")
        self.out_ready = sem(f"{name}_out_ready")
        self.recip_ready = sem(f"{name}_recip_ready")
        self.normed = sem(f"{name}_normed")
        self.normedT_ready = sem(f"{name}_normedT_ready")
        self.normedT_copied = sem(f"{name}_normedT_copied")
        self.proj_ready = sem(f"{name}_proj_ready")
        self.residual_ready = sem(f"{name}_residual_ready")
        self.stats_ready = sem(f"{name}_stats_ready")
        self.var_ready = sem(f"{name}_var_ready")
        self.eps_ready = sem(f"{name}_eps_ready")
        self.rstd_ready = sem(f"{name}_rstd_ready")
        self.x_ready = sem(f"{name}_x_ready")
        self.xb_ready = sem(f"{name}_xb_ready")


ACT_JOBS = (["ctxT.0", "ctxT.1", "W5T", "k5.0", "k5.1", "x0T.0", "x0T.1", "q1.0", "k1.0", "q1.1", "k1.1"]
            + ["x1T.0", "x1T.1", "k2.0", "k2.1", "down3T", "up3T", "gate3T", "q2T.0", "q2T.1"]
            + ["x2T.0", "x2T.1"] + [f"hid.{t}.{c}" for c in range(2) for t in range(4)]
            + ["xnT.0", "xnT.1", "router.0", "router.1", "srow.0", "srow.1", "permT.0", "permT.1", "xpT.0", "xpT.1"]
            + [f"conv.{h}.{c}" for h in range(2) for c in range(2)] + [f"z.{h}.{c}" for h in range(2) for c in range(2)]
            + ["qa", "ka", "dt.0", "dt.1"] + [f"delta.{h}.{c}" for h in range(2) for c in range(2)]
            + ["oaT"] + ["x4T.0", "x4T.1", "q5.0", "q5.1", "x5T.0", "x5T.1"])
DVE_JOBS = (["kv.0", "kv.1", "kv.2", "kv.3", "v5.0", "v5.1", "v1.0", "v1.1", "q2.0", "q2.1"]
            + ["logits8", "cT", "cexp", "up.0", "up.1"]
            + ["cumU", "va", "BC.0", "BC.1", "dposA.0", "dposA.1", "dposS.0", "dposS.1", "dl.0", "dl.1", "logits6"])


def build(nc, a, out):
    ctx = ExitStack()
    with ctx:
        _build(nc, ctx, a, out)


def _build(nc, ctx, a, out):
    def sb(name, shape, dt=F32):
        return ctx.enter_context(nc.sbuf_tensor(name, shape, dt))

    def sem(name):
        return ctx.enter_context(nc.semaphore(name))

    PS = ctx.enter_context(nc.psum_tensor("PS", [128, 8, 512], F32))

    ident = sb("ident", [128, 128])
    identb = sb("identb", [128, 128], BF16)
    before = sb("before", [128, 128])
    after = sb("after", [128, 128])
    colnum = sb("colnum", [128, 128])
    slot_base = sb("slot_base", [128, 1])
    groupmask = sb("groupmask", [128, G])
    headmask = sb("headmask", [128, J])
    part_pick = sb("part_pick", [96, 32], BF16)
    spread8 = sb("spread8", [E0, E0 * BN])
    xprojBC = sb("xprojBC", [128, NH, 3 * 2 * DS])
    earlier = sb("earlier", [8, 8, 8])
    neg_half = sb("neg_half", [128, HB])
    eps_col = sb("eps_col", [128, 1])

    gamma1 = sb("gamma1", [128, 1]); beta1 = sb("beta1", [128, 1])
    Wqkv1 = sb("Wqkv1", [128, 3 * D]); bqk1 = sb("bqk1", [128, 2]); bv1 = sb("bv1", [128, D])
    Wo1 = sb("Wo1", [128, D]); bo1 = sb("bo1", [128, D])
    Wq2 = sb("Wq2", [128, D]); Wkv2 = sb("Wkv2", [128, 2 * D]); Wp2 = sb("Wp2", [128, D]); bp2 = sb("bp2", [128, D])
    gbrow2 = sb("gbrow2", [128, 2, HD])
    dmask = sb("dmask", [128, HD])
    gbpick = sb("gbpick", [128, 2, HD])
    gb2 = sb("gb2", [128, 2])
    ctxN = sb("ctxN", [128, B, D])
    untransposed = sb("untransposed", [128, 12 * D])
    W5 = untransposed[:, 0:4 * D].rearrange("p (i n) -> p i n", i=4)
    W5T = sb("W5T", [128, 4, D])
    mask8 = sb("mask8", [128, NC], U8); maskneg = sb("maskneg", [128, NC], BF16)
    maskf = sb("maskf", [128, NC]); nmasked = sb("nmasked", [128, 1]); anykey = sb("anykey", [128, 1])
    gate3 = sb("gate3", [E0, D]); gate3T = sb("gate3T", [128, E0])
    down3 = untransposed[:, 4 * D:8 * D].rearrange("p (i n) -> p i n", i=4)
    down3T = sb("down3T", [128, 4 * 128]); downb3 = sb("downb3", [128, 4])
    up3 = untransposed[:, 8 * D:12 * D].rearrange("p (e c) -> p e c", e=E0)
    up3T = sb("up3T", [128, 4, D]); upb3 = sb("upb3", [E0, D])
    lnwb4 = sb("lnwb4", [128, 2])
    rw1 = sb("rw1", [128, D // 2]); rb1 = sb("rb1", [D // 2, 1]); rw2 = sb("rw2", [D // 2, 1]); rb2 = sb("rb2", [128, 1])
    Wqkvo4 = sb("Wqkvo4", [128, 4, D]); bqk4 = sb("bqk4", [128, 2]); bv4 = sb("bv4", [128, D])
    posbias = sb("posbias", [128, D])
    inw4 = sb("inw4", [128, 2 * DIN]); convw = sb("convw", [128, DIN, DC]); convb = sb("convb", [128, NH])
    convin = sb("convin", [128, DC, DIN])
    xproj = sb("xproj", [128, NH, DTR + 2 * DS]); dtw = sb("dtw", [DTR, DIN]); dtb = sb("dtb", [128, NH])
    Alog = sb("Alog", [128, NH, DS]); Aneg = sb("Aneg", [128, NH, DS]); Dp = sb("Dp", [128, NH])
    outw4 = sb("outw4", [128, NH, D]); diagD = sb("diagD", [128, NH, 128])
    gate6 = sb("gate6", [128, E1])

    X = [sb(f"X{i}", [128, B, D]) for i in range(2)]
    XH = sb("XH", [128, B, D])
    XB = sb("XB", [128, B, D])
    xT = sb("xT", [128, B, T])
    ctxT = sb("ctxT", [128, B, NC])
    qT = sb("qT", [128, B, T])
    qG = sb("qG", [128, 2, G, T])
    big = sb("big", [128, J * B * T + B * H * VW])
    kM1 = big[:, 0:J * B * T].rearrange("p (j b t) -> p j b t", j=J, b=B)
    V1 = big[:, J * B * T:].rearrange("p (b h w) -> p b h w", b=B, h=H)
    kM2 = sb("kM2", [128, J, B, NC]); V2full = sb("V2", [128, B * H * VW]); V2 = V2full[0:NC].rearrange("p (b h w) -> p b h w", b=B, h=H)
    kM5 = sb("kM5", [128, J, B, NC]); V5 = sb("V5", [NC, B, H, VW])
    mb1 = sb("mb1", [128, J]); sc2 = sb("sc2", [128, J]); sh2 = sb("sh2", [128, J]); mb4 = sb("mb4", [128, J])
    qc = sb("qc", [128, B, D]); sq = sb("sq", [128, B, D])
    hss = sb("hss", [128, B * H]); hvar = sb("hvar", [128, B * H]); hr0 = sb("hr0", [128, B * H]); hr1 = sb("hr1", [128, B * H])
    wmean = sb("wmean", [128, 2, H])
    Eb = sb("Eb", [128, 3, J, 128]); PT = sb("PT", [128, 3, J, 128]); mx = sb("mx", [128, 3, J])
    outT = sb("outT", [128, G, 128]); rs = sb("rs", [128, 2, H]); oN = sb("oN", [128, 2, D]); oNT = sb("oNT", [128, 2, D])
    R = sb("R", [128, B, D]); st = sb("st", [128, B, 6]); mv = sb("mv", [128, B, 2]); ve = sb("ve", [128, B]); rstd = sb("rstd", [128, B])

    ld = {k: sem(f"loaded_{k}") for k in ("x0", "x1", "a1", "ctx", "l2", "l5", "l3", "l4", "ssm", "g6", "bc4")}
    experts_loaded = sem("experts_loaded")
    stored = sem("stored")
    const_ready = sem("const_ready")
    aring = Ring([0, 1, 2, 3], sem("act_bank_full"), sem("act_bank_copied"), ACT_JOBS)
    dring = Ring([4, 5, 6, 7], sem("dve_bank_full"), sem("dve_bank_copied"), DVE_JOBS)
    dve_step, act_step, pool_step = Count(sem("dve_step")), Count(sem("act_step")), Count(sem("pool_step"))
    ln_var, ln_rstd = sem("ln_var"), sem("ln_rstd")
    ev = {}

    def event(name):
        if name not in ev:
            ev[name] = sem(name)
        return ev[name]

    at1 = Attention(sem, "at1", T, 1 / math.sqrt(HD), kM1, V1, Wo1[:], XB, X[1])
    at2 = Attention(sem, "at2", NC, math.sqrt(HD), kM2, V2, Wp2[:], XB, X[0])
    at5 = Attention(sem, "at5", NC, 1 / math.sqrt(HD), kM5, V5, W5T[:, 3, :], X[0], X[1], masked=True)

    def bank4(i, p=128):
        return PS[0:p, i, :].rearrange("p (b t) -> p b t", b=4)

    x_src = a["x"].rearrange("b t d -> t b d")

    def col(ap):
        return ap.rearrange("(p o) -> p o", o=1)

    def row(ap, p=128):
        return ap.rearrange("(o n) -> o n", o=1).to_broadcast([p, ap.shape[0]])

    loads = {
        "x0": [(X[0][:, 0:HB, :], x_src[:, 0:HB, :])],
        "x1": [(X[0][:, HB:B, :], x_src[:, HB:B, :])],
        "a1": [(gamma1[:], col(a["L0_attn_ln_gamma"])), (beta1[:], col(a["L0_attn_ln_beta"])),
               (Wqkv1[:], a["L0_attn_w_qkv"]),
               (bqk1[:], a["L0_attn_b_qkv"][0:2 * D].rearrange("(c p) -> p c", c=2)),
               (bv1[:], row(a["L0_attn_b_qkv"][2 * D:3 * D])),
               (Wo1[:], a["L0_attn_w_out"]), (bo1[:], row(a["L0_attn_b_out"]))],
        "ctx": [(ctxN[0:NC], a["ctx_1024"].rearrange("b t d -> t b d"))],
        "l2": [(Wq2[:], a["L0_xattn_Wq"]), (Wkv2[:], a["L0_xattn_Wkv"]), (Wp2[:], a["L0_xattn_Wp"]),
               (bp2[:], row(a["L0_xattn_bp"]))]
              + [(gbrow2[:, c, :], row(a[n])) for c, n in enumerate(("L0_xattn_ln_g", "L0_xattn_ln_b"))],
        "l5": [(W5[:, i, :], a[f"L1_xattn_W_{n}"]) for i, n in enumerate("qkvo")]
              + [(mask8[:], a["mask_1x1xSxS2_bk1"].bitcast(U8).rearrange("(q k) -> q k", k=NC))],
        "l3": [(gate3[:], a["L0_ffn_gate_w"]),
               (down3, a["L0_ffn_down_w"].rearrange("(t e) c d -> (e c) t d", e=2)),
               (downb3[:], a["L0_ffn_down_b"].rearrange("(t e) c -> (e c) t", e=2)),
               (up3, a["L0_ffn_up_w"].rearrange("e d c -> d e c")), (upb3[:], a["L0_ffn_up_b"])],
        "l4": [(lnwb4[:, 0:1], col(a["L1_attn_ln_w"])), (lnwb4[:, 1:2], col(a["L1_attn_ln_b"])),
               (rw1[:], a["L1_attn_r_w1"]), (rb1[:], col(a["L1_attn_r_b1"])), (rw2[:], a["L1_attn_r_w2"]),
               (rb2[:], row(a["L1_attn_r_b2"])),
               (bqk4[:, 0:1], col(a["L1_attn_bq"])), (bqk4[:, 1:2], col(a["L1_attn_bk"])),
               (bv4[:], row(a["L1_attn_bv"]))]
              + [(Wqkvo4[:, i, :], a[f"L1_attn_W{n}"]) for i, n in enumerate("qkvo")],
        "bc4": [(posbias[TS:T, :], row(a["L1_attn_bo"], KSEL))],
        "ssm": [(inw4[:], a["L1_attn_in_w"]),
                (convw[:], a["L1_attn_conv_w"].rearrange("(o n) c -> o n c", o=1).to_broadcast([128, DIN, DC])),
                (convb[:], a["L1_attn_conv_b"].rearrange("(h p) -> p h", p=128)),
                (xproj[:], a["L1_attn_xproj_w"].rearrange("(h p) n -> p h n", p=128)),
                (dtw[:], a["L1_attn_dt_w"]), (dtb[:], a["L1_attn_dt_b"].rearrange("(h p) -> p h", p=128)),
                (Alog[:], a["L1_attn_A_log"].rearrange("(h p) n -> p h n", p=128)),
                (Dp[:], a["L1_attn_Dp"].rearrange("(h p) -> p h", p=128)),
                (outw4[:], a["L1_attn_out_w"].rearrange("(h p) n -> p h n", p=128))],
        "g6": [(gate6[:], a["L1_ffn_gate_w"])],
    }
    need = {k: 16 * len(v) for k, v in loads.items()}

    def loaded(eng, *keys):
        for k in keys:
            eng.wait_ge(ld[k], need[k])

    def load(eng, *keys):
        for k in keys:
            for dst, src in loads[k]:
                eng.dma_start(dst, src, allow_slow_non_contiguous=True).then_inc(ld[k], 16)

    W768 = B * TS
    du = untransposed[:].rearrange("p (h n) -> p h n", h=NH)
    xc = V2full[:, 0:NH * W768].rearrange("p (h n) -> p h n", h=NH)
    zs = V2full[:, NH * W768:2 * NH * W768].rearrange("p (h n) -> p h n", h=NH)
    delta = big[:, 0:2 * W768].rearrange("p (h n) -> p h n", h=NH)

    def spare(t):
        return t[:].rearrange("p b d -> p (b d)")[:, 0:W768]

    dA = [big[:, (2 + i) * W768:(3 + i) * W768] for i in range(2)] + [spare(X[0])]
    dBu = [big[:, (4 + i) * W768:(5 + i) * W768] for i in range(2)] + [spare(xT)]
    hst = [big[:, (6 + i) * W768:(7 + i) * W768] for i in range(2)] + [spare(sq)]
    hC = [big[:, (8 + i) * W768:(9 + i) * W768] for i in range(2)] + [spare(XB), spare(ctxN)]
    NDA, NDB, NHS, NHC = len(dA), len(dBu), len(hst), len(hC)
    kM2flat = kM2[:].rearrange("p j b n -> p (j b n)")
    Bsb = [kM2flat[:, i * W768:(i + 1) * W768] for i in range(2)]
    Csb = [kM2flat[:, 2 * W768:3 * W768], spare(XH)]
    sp_abs = big[:, 2 * W768:4 * W768].rearrange("p (h n) -> p h n", h=NH)
    sp_exp = big[:, 4 * W768:6 * W768].rearrange("p (h n) -> p h n", h=NH)
    sp_log = big[:, 6 * W768:8 * W768].rearrange("p (h n) -> p h n", h=NH)
    sp_relu = big[:, 8 * W768:10 * W768].rearrange("p (h n) -> p h n", h=NH)
    PADT = DC - 1 + T
    xpT = sb("xpT", [128, B, PADT])
    hrT = big[0:D // 2, 2 * B * T:3 * B * T].rearrange("p (b t) -> p b t", b=B)
    Srow = big[:, 0:B * T].rearrange("p (b t) -> p b t", b=B)
    scol = sb("scol", [128, B]); gt = big[:, B * T:2 * B * T].rearrange("p (b t) -> p b t", b=B); eq = V2full[:, 2 * NH * W768:2 * NH * W768 + B * T].rearrange("p (b t) -> p b t", b=B)
    rank = sb("rank", [128, B]); sel = sb("sel", [128, B]); unsel = sb("unsel", [128, B]); cumU = sb("cumU", [128, B])
    pos = sb("pos", [128, B]); posa = sb("posa", [128, B])
    Perm = gt; PermT = eq
    qTa = ctxT[:].rearrange("p b t -> p (b t)")[:, 0:B * KSEL].rearrange("p (b k) -> p b k", b=B); kMa = PT[:].rearrange("p a j t -> p (a j t)")[:, 0:J * B * KSEL].rearrange("p (j b k) -> p j b k", j=J, b=B); va = R[:, 0:2, :]
    Pa = convw[:].rearrange("p n c -> p (n c)").rearrange("p (n k) -> p n k", k=KSEL)
    PaT = XB[:].rearrange("p b d -> p (b d)").rearrange("p (n k) -> p n k", k=KSEL)
    mxa = sb("mxa", [128, 2 * H]); sma = sb("sma", [128, 2 * H])
    oa, oaT = R[:, 2:4, :], R[:, 4:6, :]
    dtp = qT[0:DTR].rearrange("p b t -> p (b t)")[:, 0:W768]
    Ebflat = Eb[0:96].rearrange("p a j t -> p (a j t)")
    sqb = sq[0:96].rearrange("p b d -> p (b d)").bitcast(BF16)
    BC, BC3 = Ebflat[:, 0:W768], Ebflat[:, W768:].bitcast(BF16)[:, 0:W768]
    BCh, BCm = sqb[:, 0:W768], sqb[:, W768:2 * W768]
    dpos = qc
    hid = big[:, 0:4 * B * T].rearrange("p (t n) -> p t n", t=4)
    pooledT = sb("pooledT", [128, B])
    g8 = sb("g8", [8, 8]); m8 = sb("m8", [8, 1]); c8 = sb("c8", [8, 8]); t64 = sb("t64", [8, 8, 8]); e64 = sb("e64", [8, 8, 8])
    r8 = sb("r8", [8, 8]); cT = sb("cT", [8, 8]); cexp = sb("cexp", [128, 4, B])
    aff = sb("aff", [128, B, E1]); am = sb("am", [128, B])
    hidE = [big[:, i * NI * B * T:(i + 1) * NI * B * T].rearrange("p (i n) -> p i n", i=NI) for i in range(2)]
    Wg6 = V2full[:, 0:E1 * IW].rearrange("p (e n) -> p e n", e=E1)
    Wu6 = V2full[:, E1 * IW:2 * E1 * IW].rearrange("p (e n) -> p e n", e=E1)
    Wd6 = big[:, 2 * NI * B * T:2 * NI * B * T + E1 * NI * D].rearrange("p (e n) -> p e n", e=E1 * NI)
    silu6 = [kM2flat[:, i * 512:(i + 1) * 512] for i in range(4)]

    block = ctx.enter_context(nc.Block())

    @block.sync
    def _(sp):
        load(sp, "x0", "x1", "a1", "l3", "l4", "ssm", "bc4", "g6")
        sp.wait_ge(dring.full, dring.index["dl.1"] + 1)
        sp.dma_start(Wg6, a["L1_ffn_Wg"].rearrange("e d n -> d e n")).then_inc(experts_loaded, 16)
        sp.dma_start(Wu6, a["L1_ffn_Wu"].rearrange("e d n -> d e n")).then_inc(experts_loaded, 16)
        sp.dma_start(Wd6, a["L1_ffn_Wd"].rearrange("e (i p) d -> p (e i) d", p=128)).then_inc(experts_loaded, 16)
        for c in range(2):
            sp.wait_ge(event("out_ready"), c + 1)
            sp.dma_start(out.rearrange("b t d -> t b d")[:, c * HB:(c + 1) * HB, :],
                         X[0][:, c * HB:(c + 1) * HB, :]).then_inc(stored, 16)
        sp.wait_ge(stored, 32)

    @block.gpsimd
    def _(pool):
        P_ = nc.gpsimd

        def step(ins):
            pool.wait_ge(pool_step.sem, pool_step.then(ins))

        def affine(t, op, pattern, multiplier=1):
            return P_.affine_select(out=t, in_=t, compare_op=op, fill=1.0, base=0, pattern=pattern,
                                    channel_multiplier=multiplier)

        P_.memset(ident[:], 0.0)
        P_.memset(neg_half[:], -0.5)
        step(P_.memset(eps_col[:], EPS))
        affine(ident[:], ALU.not_equal, [[-1, 128]]).then_inc(const_ready, 1)
        pool.wait_ge(const_ready, 1)
        P_.memset(identb[:], 0.0)
        P_.memset(before[:], 0.0)
        P_.memset(after[:], 0.0)
        P_.memset(part_pick[:], 0.0)
        P_.memset(earlier[:], 0.0)
        step(P_.memset(spread8[:], 1.0))
        affine(identb[:], ALU.not_equal, [[-1, 128]])
        affine(before[:], ALU.is_ge, [[1, 128]], -1)
        affine(after[:], ALU.is_ge, [[-1, 128]])
        affine(earlier[:], ALU.is_ge, [[-1, 8], [1, 8]], 0)
        P_.iota(colnum[:], pattern=[[1, 128]], base=0, channel_multiplier=0, allow_small_or_imprecise_dtypes=True)
        P_.iota(slot_base[:], pattern=[[0, 1]], base=TS, channel_multiplier=1, allow_small_or_imprecise_dtypes=True)
        P_.memset(xpT[:, :, 0:DC - 1], 0.0)
        P_.tensor_tensor(out=spread8[:].rearrange("p (e c) -> p e c", e=E0), in0=spread8[:].rearrange("p (e c) -> p e c", e=E0),
                         in1=ident[0:E0, 0:E0].rearrange("p (e o) -> p e o", o=1).to_broadcast([E0, E0, BN]), op=ALU.mult)
        for k in range(3):
            step(affine(part_pick[32 * k:32 * k + 32, :], ALU.not_equal, [[-1, 32]]))

        def value_ones(*values):
            for v in values:
                ins = P_.memset(v[:, :, :, HD:VW], 0.0)
            step(ins)
            for v in values:
                ins = P_.memset(v[:, :, :, HD:HD + 1], 1.0)
            ins.then_inc(event("v_ones"), 1)

        powers = Count(ln_rstd)

        def rstds():
            for c in range(2):
                pool.wait_ge(ln_var, powers.n + 1)
                h = slice(c * HB, (c + 1) * HB)
                powers.then(P_.tensor_tensor(out=rstd[:, h], in0=ve[:, h], in1=neg_half[:], op=ALU.pow))

        def attention_pool(at, query_jobs, meanwhile=()):
            def queries(b):
                aring.wait_copied(pool, query_jobs[b // HB])
                if b >= 2:
                    pool.wait_ge(at.scores_ready, G * (b - 1))
                P_.tensor_tensor(out=qG[:, b % 2], in0=qT[:, b, :].rearrange("p (o t) -> p o t", o=1).to_broadcast([128, G, T]),
                                 in1=groupmask[:].rearrange("p (g o) -> p g o", o=1).to_broadcast([128, G, T]), op=ALU.mult)\
                    .then_inc(at.queries_ready, 1)

            ahead = 5
            for b in range(ahead):
                queries(b)
                if b == 1:
                    for work in meanwhile:
                        work()
            for b in range(B):
                pool.wait_ge(at.eps_ready, b + 1)
                P_.tensor_tensor(out=rstd[:, b:b + 1], in0=ve[:, b:b + 1], in1=neg_half[:, 0:1], op=ALU.pow)\
                    .then_inc(at.rstd_ready, 1)
                if b + ahead < B:
                    queries(b + ahead)

        def wide(bias):
            return bias[:].rearrange("p (o n) -> p o n", o=1).to_broadcast([128, B, D])

        rstds()
        value_ones(V1)
        dring.wait_copied(pool, "kv.3")
        P_.tensor_tensor(out=sq[0:NC], in0=qc[0:NC], in1=qc[0:NC], op=ALU.mult).then_inc(event("k_sq"), 1)

        def residual1():
            loaded(pool, "x0", "x1", "a1")
            step(P_.tensor_tensor(out=XB[:], in0=X[0][:], in1=X[0][:], op=ALU.add))
            P_.tensor_tensor(out=XB[:], in0=XB[:], in1=wide(bo1), op=ALU.add).then_inc(at1.xb_ready, 1)

        def residual2():
            loaded(pool, "l2")
            P_.tensor_tensor(out=XB[:], in0=X[1][:], in1=wide(bp2), op=ALU.add).then_inc(at2.xb_ready, 1)

        pool.wait_ge(event("groupmask"), 1)
        attention_pool(at1, ("q1.0", "q1.1"), (residual1, lambda: value_ones(V2, V5[:])))
        dring.wait_copied(pool, "q2.0")
        pool.wait_ge(aring.full, aring.index["k2.1"] + 1)
        P_.tensor_tensor(out=sq[:, 0:HB], in0=qc[:, 0:HB], in1=qc[:, 0:HB], op=ALU.mult).then_inc(event("q_sq"), 1)
        pool.wait_ge(at1.x_ready, B)
        attention_pool(at2, ("q2T.0", "q2T.1"), (residual2,))
        loaded(pool, "ssm")
        for j in range(DC):
            P_.tensor_tensor(out=convin[:, j, :], in0=inw4[:, 0:DIN], in1=convw[:, :, j], op=ALU.mult)
        for k in range(3):
            P_.tensor_copy(xprojBC[:, :, 2 * DS * k:2 * DS * (k + 1)], xproj[:, :, DTR:])
        for h in range(NH):
            ins = P_.tensor_scalar(out=diagD[:, h, :], in0=ident[:], scalar1=Dp[:, h:h + 1], scalar2=None,
                                   op0=ALU.mult)
        ins.then_inc(event("ssm_weights"), 1)
        rstds()
        rstds()
        for n in range(NH * DS):
            s = n // NH
            pool.wait_ge(event("c_copied"), s + 1)
            pool.wait_ge(event("h_ready"), n + 1)
            if n >= NHC:
                pool.wait_ge(event("hC_used"), n - NHC + 1)
            P_.tensor_tensor(out=hC[n % NHC], in0=hst[n % NHS], in1=Csb[s % 2], op=ALU.mult)\
                .then_inc(event("hC_ready"), 1)
        rstds()
        attention_pool(at5, ("q5.0", "q5.1"))
        rstds()

    @block.scalar
    def _(act):
        A_ = nc.scalar.activation

        def step(ins):
            act.wait_ge(act_step.sem, act_step.then(ins))

        def copy_out(name, dst, view, func=ACT.Identity, **kw):
            A_(dst, view(aring.take(act, name)), func, **kw).then_inc(aring.copied, 1)

        def masked(name, dst, view, scale, shift):
            i = aring.take(act, name)
            for j in range(J):
                ins = A_(dst(j), view(i), ACT.Identity, scale=scale[:, j:j + 1],
                         **({"bias": shift[:, j:j + 1]} if shift is not None else {}))
            ins.then_inc(aring.copied, 1)

        def bank_full(i):
            return PS[:, i, :]

        def bank_ctx(i):
            return PS[:, i, 0:HB * NC].rearrange("p (b n) -> p b n", b=HB)

        def half(t, c):
            return t[:, c * HB:(c + 1) * HB, :]

        def attention_scalar(at):
            nk = at.nk
            for s in range(NU + 15):
                if s < NU:
                    act.wait_ge(at.shifted, s + 1)
                    A_(Eb[:, s % 3, :, 0:nk], Eb[:, s % 3, :, 0:nk], ACT.Exp, scale=at.scale).then_inc(at.exp_ready, 1)
                if 1 <= s <= NU:
                    u = s - 1
                    act.wait_ge(at.probsT_ready, u + 1)
                    if u >= 3:
                        act.wait_ge(at.pv_done, u - 2)
                    A_(PT[0:nk, u % 3, :, :], bank4(3 + u % 2, nk), ACT.Copy).then_inc(at.probsT_copied, 1)
                if s >= 5 and (s - 5) % G == 0 and (s - 5) // G < B:
                    b = (s - 5) // G
                    act.wait_ge(at.pv_done, G * b + G)
                    if b:
                        act.wait_ge(at.out_ready, b)
                    A_(outT[:], bank4(5 + b % 2), ACT.Copy).then_inc(at.outT_copied, 1)
                if s >= 11 and (s - 11) % G == 0 and (s - 11) // G < B:
                    b = (s - 11) // G
                    act.wait_ge(at.normedT_ready, b + 1)
                    if b >= 2:
                        act.wait_ge(at.proj_ready, b - 1)
                    A_(oNT[:, b % 2, :], PS[:, 7, 0:128], ACT.Copy).then_inc(at.normedT_copied, 1)

        def head_rstd(rows, ready, name):
            act.wait_ge(event(ready), 1)
            step(A_(hr0[0:rows], hss[0:rows], ACT.Ln, scale=1.0 / HD, bias=eps_col[0:rows]))
            A_(hr0[0:rows], hr0[0:rows], ACT.Exp, scale=-0.5).then_inc(event(name), 1)

        load(act, "ctx", "l2", "l5")
        for c in range(2):
            copy_out(f"ctxT.{c}", half(ctxT, c), bank_ctx)
        copy_out("W5T", W5T[:], bank4)
        loaded(act, "a1")
        act.wait_ge(event("small1"), 1)
        for c in range(2):
            masked(f"k5.{c}", lambda j: kM5[:, j, c * HB:(c + 1) * HB, :], bank_ctx, headmask, None)
        for c in range(2):
            copy_out(f"x0T.{c}", half(xT, c), bank4, scale=gamma1[:], bias=beta1[:])
        for c in range(2):
            copy_out(f"q1.{c}", half(qT, c), bank4, bias=bqk1[:, 0:1])
            masked(f"k1.{c}", lambda j: kM1[:, j, c * HB:(c + 1) * HB, :], bank4, headmask, mb1)
        head_rstd(NC, "k_ss", "k_rstd")
        attention_scalar(at1)

        for c in range(2):
            copy_out(f"x1T.{c}", half(xT, c), bank4)
        act.wait_ge(event("small2"), 1)
        for c in range(2):
            masked(f"k2.{c}", lambda j: kM2[:, j, c * HB:(c + 1) * HB, :], bank_ctx, sc2, sh2)
        copy_out("down3T", down3T[:], bank_full)
        copy_out("up3T", up3T[:], bank4)
        copy_out("gate3T", gate3T[:], lambda i: PS[:, i, 0:E0])
        head_rstd(128, "q_ss", "q_rstd")
        for c in range(2):
            copy_out(f"q2T.{c}", half(qT, c), bank4, scale=gb2[:, 0:1], bias=gb2[:, 1:2])
        attention_scalar(at2)

        for c in range(2):
            copy_out(f"x2T.{c}", half(xT, c), bank4)
        dring.wait_copied(act, "logits8")
        A_(g8[:], g8[:], ACT.Exp).then_inc(event("gate3_exp"), 1)
        for c in range(2):
            for t in range(4):
                copy_out(f"hid.{t}.{c}", hid[:, t, c * 512:(c + 1) * 512], bank_full, ACT.Gelu, bias=downb3[:, t:t + 1])

        for c in range(2):
            copy_out(f"xnT.{c}", half(xT, c), bank4, scale=lnwb4[:, 0:1], bias=lnwb4[:, 1:2])
        for c in range(2):
            copy_out(f"router.{c}", half(hrT, c), lambda i: bank4(i, D // 2), ACT.Gelu_apprx_tanh, bias=rb1[:])
        for c in range(2):
            copy_out(f"srow.{c}", half(Srow, c), bank4, bias=rb2[:])
        for c in range(2):
            copy_out(f"permT.{c}", half(PermT, c), bank4)
        for c in range(2):
            copy_out(f"xpT.{c}", xpT[:, c * HB:(c + 1) * HB, DC - 1:], bank4, scale=lnwb4[:, 0:1], bias=lnwb4[:, 1:2])
        W384 = HB * TS
        for dst, name in ((xc, "conv"), (zs, "z")):
            for h in range(NH):
                for c in range(2):
                    kw = {"bias": convb[:, h:h + 1]} if name == "conv" else {}
                    copy_out(f"{name}.{h}.{c}", dst[:, h, c * W384:(c + 1) * W384], lambda i: PS[:, i, 0:W384],
                             ACT.Silu, **kw)
        copy_out("qa", qTa, lambda i: PS[:, i, 0:B * KSEL].rearrange("p (b k) -> p b k", b=B), bias=bqk4[:, 0:1])
        act.wait_ge(event("small4"), 1)
        masked("ka", lambda j: kMa[:, j, :, :], lambda i: PS[:, i, 0:B * KSEL].rearrange("p (b k) -> p b k", b=B),
                    headmask, mb4)
        for c in range(2):
            copy_out(f"dt.{c}", dtp[:, c * W384:(c + 1) * W384], lambda i: PS[0:DTR, i, 0:W384])
        for h in range(NH):
            for c in range(2):
                i = aring.take(act, f"delta.{h}.{c}")
                w = slice(c * W384, (c + 1) * W384)
                A_(sp_abs[:, h, w], PS[:, i, 0:W384], ACT.Abs, bias=dtb[:, h:h + 1])
                A_(sp_relu[:, h, w], PS[:, i, 0:W384], ACT.Relu, bias=dtb[:, h:h + 1]).then_inc(aring.copied, 1)
        act.wait_ge(aring.copied, aring.emptied)
        step(A_(sp_exp, sp_abs, ACT.Exp, scale=-1.0))
        A_(sp_log, sp_exp, ACT.Ln, bias=1.0).then_inc(event("softplus_parts"), 1)
        loaded(act, "ssm")
        A_(Aneg[:], Alog[:], ACT.Exp).then_inc(event("a_exp"), 1)
        act.wait_ge(event("pa_shifted"), 1)
        A_(Pa, Pa, ACT.Exp, scale=1 / math.sqrt(HD)).then_inc(event("pa_exp"), 1)
        copy_out("oaT", oaT, lambda i: PS[:, i, 0:256].rearrange("p (b t) -> p b t", b=2))

        def decay(n):
            s, h = n // NH, n % NH
            if n >= NDA:
                act.wait_ge(event("h_ready"), n - NDA + 1)
            A_(dA[n % NDA].rearrange("p (b t) -> p b t", b=B)[:, :, 1:TS],
               delta[:, h, :].rearrange("p (b t) -> p b t", b=B)[:, :, 1:TS],
               ACT.Exp, scale=Aneg[:, h, s:s + 1]).then_inc(event("dA_ready"), 1)

        act.wait_ge(event("delta_ready"), 1)
        for s in range(DS):
            act.wait_ge(event("bc_ready"), s + 1)
            if s >= 2:
                act.wait_ge(event("dBu_ready"), NH * (s - 1))
            A_(Bsb[s % 2].rearrange("p (c n) -> p c n", c=2), PS[:, 4:6, 0:W384], ACT.Copy)\
                .then_inc(event("b_copied"), 1)
            if s >= 2:
                act.wait_ge(event("hC_ready"), NH * (s - 1))
            A_(Csb[s % 2].rearrange("p (c n) -> p c n", c=2), PS[:, 6:8, 0:W384], ACT.Copy)\
                .then_inc(event("c_copied"), 1)
            for h in range(NH):
                decay(NH * s + h)

        for c in range(2):
            copy_out(f"x4T.{c}", half(xT, c), bank4)
        for c in range(2):
            copy_out(f"q5.{c}", half(qT, c), bank4)
        attention_scalar(at5)

        for c in range(2):
            copy_out(f"x5T.{c}", half(xT, c), bank4)
        dring.wait_copied(act, "logits6")
        A_(aff[:], aff[:], ACT.Exp).then_inc(event("aff_exp"), 1)
        for k in range(E1 * NI * 2):
            act.wait_ge(event("gate_ready"), k + 1)
            if k >= 4:
                act.wait_ge(event("hidden_ready"), k - 3)
            A_(silu6[k % 4], PS[:, k % 2, :], ACT.Silu).then_inc(event("silu_ready"), 1)

    @block.vector
    def _(dve):
        V_ = nc.vector

        def step(ins):
            dve.wait_ge(dve_step.sem, dve_step.then(ins))

        def take(name):
            return dring.take(dve, name)

        def bank_full(i, p=128, n=512):
            return PS[0:p, i, 0:n]

        def half(t, c):
            return t[:, c * HB:(c + 1) * HB, :]

        var_sent = Count(ln_var)

        def norm_halves(src, dst, done, halves=(0, 1)):
            for c in halves:
                for b in range(c * HB, (c + 1) * HB):
                    ins = V_.bn_stats(st[:, b, :], src[:, b, :])
                step(ins)
                for b in range(c * HB, (c + 1) * HB):
                    ins = V_.bn_aggr(mv[:, b, :], st[:, b, :])
                step(ins)
                var_sent.then(V_.tensor_scalar(ve[:, c * HB:(c + 1) * HB], mv[:, c * HB:(c + 1) * HB, 1], EPS, None, ALU.add))
            for c in halves:
                dve.wait_ge(ln_rstd, var_sent.n - len(halves) + halves.index(c) + 1)
                for b in range(c * HB, (c + 1) * HB):
                    ins = V_.tensor_scalar(dst[:, b, :], src[:, b, :], mv[:, b, 0:1], rstd[:, b:b + 1],
                                           ALU.subtract, ALU.mult)
                ins.then_inc(event(done), 1)

        def centre(W, k):
            w = W.rearrange("p (h d) -> p h d", h=H)
            step(V_.tensor_reduce(wmean[:, k, :], w, axis=AX.X, op=ALU.add))
            step(V_.tensor_scalar(wmean[:, k, :], wmean[:, k, :], 1.0 / HD, None, ALU.mult))
            return V_.tensor_tensor(w, w, wmean[:, k, :].rearrange("p (h o) -> p h o", o=1).to_broadcast([128, H, HD]),
                                    ALU.subtract)

        def head_sums(rows, squares, sums):
            dve.wait_ge(event(squares), 1)
            V_.tensor_reduce(hss[0:rows], sq[0:rows].rearrange("p b (h d) -> p (b h) d", d=HD), axis=AX.X,
                             op=ALU.add).then_inc(event(sums), 1)
            dve.wait_ge(event(sums), 1)
            step(V_.tensor_scalar(hvar[0:rows], hss[0:rows], 1.0 / HD, EPS, ALU.mult, ALU.add))

        def head_scale(rows, first, done):
            dve.wait_ge(event(first), 1)
            step(V_.tensor_tensor(hr1[0:rows], hr0[0:rows], hr0[0:rows], ALU.mult))
            step(V_.tensor_tensor(hr1[0:rows], hr1[0:rows], hvar[0:rows], ALU.mult))
            step(V_.tensor_scalar(hr1[0:rows], hr1[0:rows], -0.5, 1.5, ALU.mult, ALU.add))
            step(V_.tensor_tensor(hr1[0:rows], hr1[0:rows], hr0[0:rows], ALU.mult))
            V_.tensor_tensor(sq[0:rows].rearrange("p b (h d) -> p (b h) d", d=HD),
                             qc[0:rows].rearrange("p b (h d) -> p (b h) d", d=HD),
                             hr1[0:rows].rearrange("p (n o) -> p n o", o=1).to_broadcast([rows, B * H, HD]),
                             ALU.mult).then_inc(event(done), 1)

        def attention_vector(at):
            nk = at.nk

            def scores(u):
                return PS[:, u % 3, 0:J * nk].rearrange("p (j k) -> p j k", j=J)

            for s in range(-1, NU + 20):
                if s + 1 < NU:
                    u = s + 1
                    dve.wait_ge(at.scores_ready, u + 1)
                    if u >= 3:
                        dve.wait_ge(at.shifted, u - 2)
                    V_.tensor_reduce(mx[:, u % 3, :], scores(u), axis=AX.X, op=ALU.max).then_inc(at.max_ready, 1)
                if 0 <= s < NU:
                    dve.wait_ge(at.max_ready, s + 1)
                    if s >= 3:
                        dve.wait_ge(at.probsT_ready, s - 2)
                    V_.tensor_tensor(Eb[:, s % 3, :, 0:nk], scores(s),
                                     mx[:, s % 3, :].rearrange("p (j o) -> p j o", o=1).to_broadcast([128, J, nk]),
                                     ALU.subtract).then_inc(at.shifted, 1)

                def row_of(lag):
                    b = (s - lag) // G
                    return b if s >= lag and (s - lag) % G == 0 and b < B else None

                if (b := row_of(7)) is not None:
                    dve.wait_ge(at.out_ready, b + 1)
                    if b >= 2:
                        dve.wait_ge(at.normed, b - 1)
                    o = PS[:, 5 + b % 2, :].rearrange("p (h w) -> p h w", h=H)
                    ins = V_.reciprocal(rs[:, b % 2, :].rearrange("p (h o) -> p h o", o=1), o[:, :, HD:HD + 1])
                    if at.masked:
                        step(ins)
                        ins = V_.tensor_scalar(rs[:, b % 2, :], rs[:, b % 2, :], anykey[:], None, ALU.mult)
                    ins.then_inc(at.recip_ready, 1)
                if (b := row_of(8)) is not None:
                    dve.wait_ge(at.recip_ready, b + 1)
                    if b >= 2:
                        dve.wait_ge(at.normedT_ready, b - 1)
                    o = PS[:, 5 + b % 2, :].rearrange("p (h w) -> p h w", h=H)
                    V_.tensor_tensor(oN[:, b % 2, :].rearrange("p (h d) -> p h d", h=H), o[:, :, 0:HD],
                                     rs[:, b % 2, :].rearrange("p (h o) -> p h o", o=1).to_broadcast([128, H, HD]),
                                     ALU.mult).then_inc(at.normed, 1)
                if (b := row_of(14)) is not None:
                    dve.wait_ge(at.proj_ready, b + 1)
                    if b == 0 and not at.masked:
                        dve.wait_ge(at.xb_ready, 1)
                    V_.tensor_tensor(R[:, b, :], at.XB[:, b, :], PS[:, 7, 128:256], ALU.add)\
                        .then_inc(at.residual_ready, 1)
                if (b := row_of(15)) is not None:
                    dve.wait_ge(at.residual_ready, b + 1)
                    V_.bn_stats(st[:, b, :], R[:, b, :]).then_inc(at.stats_ready, 1)
                if (b := row_of(16)) is not None:
                    dve.wait_ge(at.stats_ready, b + 1)
                    V_.bn_aggr(mv[:, b, :], st[:, b, :]).then_inc(at.var_ready, 1)
                if (b := row_of(17)) is not None:
                    dve.wait_ge(at.var_ready, b + 1)
                    V_.tensor_scalar(ve[:, b:b + 1], mv[:, b, 1:2], EPS, None, ALU.add).then_inc(at.eps_ready, 1)
                if (b := row_of(19)) is not None:
                    dve.wait_ge(at.rstd_ready, b + 1)
                    V_.tensor_scalar(at.Xout[:, b, :], R[:, b, :], mv[:, b, 0:1], rstd[:, b:b + 1],
                                     ALU.subtract, ALU.mult).then_inc(at.x_ready, 1)

        def wide(v, shape):
            return v.rearrange("p (b o) -> p b o", o=1).to_broadcast(shape)

        dve.wait_ge(const_ready, 1)
        step(V_.tensor_reduce(headmask[:], ident[:].rearrange("p (g j d) -> p j g d", g=G, j=J), axis=AX.XY, op=ALU.add))
        V_.tensor_reduce(groupmask[:], ident[:].rearrange("p (g c) -> p g c", g=G), axis=AX.X, op=ALU.add)\
            .then_inc(event("groupmask"), 1)
        loaded(dve, "x0")
        norm_halves(X[0], XH, "xh1", (0,))
        loaded(dve, "a1")
        V_.tensor_scalar(mb1[:], headmask[:], bqk1[:, 1:2], None, ALU.mult).then_inc(event("small1"), 1)
        loaded(dve, "l2")
        centre(Wkv2[:, 0:D], 0).then_inc(event("w2_centred"), 1)
        loaded(dve, "x1")
        norm_halves(X[0], XH, "xh1", (1,))
        centre(Wq2[:], 1).then_inc(event("w2_centred"), 1)
        for p in range(4):
            kv = PS[0:NC, take(f"kv.{p}"), :].rearrange("p (b n) -> p b n", b=2)
            V_.tensor_copy(qc[0:NC, 2 * p:2 * p + 2, :], kv[:, :, 0:D])
            V_.tensor_copy(V2[:, 2 * p:2 * p + 2, :, 0:HD], kv[:, :, D:2 * D].rearrange("p b (h d) -> p b h d", h=H))\
                .then_inc(dring.copied, 1)
        for c in range(2):
            V_.tensor_copy(V5[:, c * HB:(c + 1) * HB, :, 0:HD],
                           bank4(take(f"v5.{c}"), NC).rearrange("p b (h d) -> p b h d", h=H)).then_inc(dring.copied, 1)
        step(V_.tensor_reduce(dmask[:], ident[:].rearrange("p (h d) -> p d h", d=HD), axis=AX.X, op=ALU.add))
        step(V_.tensor_tensor(gbpick[:], gbrow2[:], dmask[:].rearrange("p (o d) -> p o d", o=1).to_broadcast([128, 2, HD]),
                              ALU.mult))
        step(V_.tensor_reduce(gb2[:], gbpick[:], axis=AX.X, op=ALU.add))
        V_.tensor_scalar(sc2[:], headmask[:], gb2[:, 0:1], None, ALU.mult)
        V_.tensor_scalar(sh2[:], headmask[:], gb2[:, 1:2], None, ALU.mult).then_inc(event("small2"), 1)
        for c in range(2):
            i = take(f"v1.{c}")
            V_.tensor_tensor(V1[:, c * HB:(c + 1) * HB, :, 0:HD],
                             bank4(i).rearrange("p b (h d) -> p b h d", h=H),
                             bv1[:].rearrange("p (o h d) -> p o h d", o=1, h=H).to_broadcast([128, HB, H, HD]),
                             ALU.add).then_inc(dring.copied, 1)
        loaded(dve, "l5")
        V_.tensor_scalar(maskneg[:], mask8[:], MASKED, None, ALU.mult)
        step(V_.tensor_reduce(nmasked[:], mask8[:], axis=AX.X, op=ALU.add))
        step(V_.tensor_scalar(anykey[:], nmasked[:], float(NC), None, ALU.is_lt))
        head_sums(NC, "k_sq", "k_ss")
        attention_vector(at1)

        head_scale(NC, "k_rstd", "kn_ready")
        dve.wait_ge(event("kn_ready"), 1)
        for c in range(2):
            V_.tensor_copy(half(qc, c), bank4(take(f"q2.{c}"))).then_inc(dring.copied, 1)
        dring.wait_copied(dve, "q2.1")
        dve.wait_ge(aring.full, aring.index["k2.1"] + 1)
        step(V_.tensor_tensor(half(sq, 1), half(qc, 1), half(qc, 1), ALU.mult))
        head_sums(128, "q_sq", "q_ss")
        head_scale(128, "q_rstd", "qn_ready")
        attention_vector(at2)

        aring.wait_copied(dve, "x2T.1")
        step(V_.tensor_reduce(pooledT[:], xT[:], axis=AX.X, op=ALU.add))
        V_.tensor_scalar(pooledT[:], pooledT[:], 1.0 / T, None, ALU.mult).then_inc(event("pooled"), 1)
        i = take("logits8")
        step(V_.tensor_reduce(m8[:], PS[0:8, i, 0:8], axis=AX.X, op=ALU.max))
        V_.tensor_scalar(g8[:], PS[0:8, i, 0:8], m8[:], None, ALU.subtract).then_inc(dring.copied, 1)
        dve.wait_ge(event("gate3_exp"), 1)
        step(V_.tensor_reduce(m8[:], g8[:], axis=AX.X, op=ALU.add))
        step(V_.reciprocal(m8[:], m8[:]))
        step(V_.tensor_scalar(g8[:], g8[:], m8[:], None, ALU.mult))
        other = g8[:].rearrange("p (o f) -> p o f", o=1).to_broadcast([8, 8, 8])
        own = g8[:].rearrange("p (e o) -> p e o", o=1).to_broadcast([8, 8, 8])
        V_.tensor_tensor(t64[:], other, own, ALU.is_gt)
        step(V_.tensor_tensor(e64[:], other, own, ALU.is_equal))
        step(V_.tensor_tensor(e64[:], e64[:], earlier[:], ALU.mult))
        step(V_.tensor_tensor(t64[:], t64[:], e64[:], ALU.add))
        step(V_.tensor_reduce(r8[:], t64[:], axis=AX.X, op=ALU.add))
        step(V_.tensor_scalar(r8[:], r8[:], 2.0, None, ALU.is_lt))
        step(V_.tensor_tensor(c8[:], r8[:], g8[:], ALU.mult))
        step(V_.tensor_reduce(m8[:], c8[:], axis=AX.X, op=ALU.add))
        step(V_.tensor_scalar(m8[:], m8[:], 1e-8, None, ALU.add))
        step(V_.reciprocal(m8[:], m8[:]))
        V_.tensor_scalar(c8[:], c8[:], m8[:], None, ALU.mult).then_inc(event("c8_ready"), 1)
        V_.tensor_copy(cT[:], PS[0:8, take("cT"), 0:8]).then_inc(dring.copied, 1)
        V_.tensor_copy(cexp[:], PS[:, take("cexp"), 0:4 * B].rearrange("p (t b) -> p t b", t=4)).then_inc(dring.copied, 1)
        dve.wait_ge(dring.copied, dring.emptied)
        for c in range(2):
            for t in range(4):
                aring.wait_copied(dve, f"hid.{t}.{c}")
                v = hid[:, t, c * 512:(c + 1) * 512].rearrange("p (b n) -> p b n", b=HB)
                V_.tensor_tensor(v, v, wide(cexp[:, t, c * HB:(c + 1) * HB], [128, HB, T]), ALU.mult)\
                    .then_inc(event("hid_scaled"), 1)
        for c in range(2):
            V_.tensor_tensor(half(R, c), half(X[0], c), bank4(take(f"up.{c}")), ALU.add).then_inc(dring.copied, 1)
        dve.wait_ge(dring.copied, dring.emptied)
        norm_halves(R, X[1], "x3")

        dve.wait_ge(event("x3"), 2)
        norm_halves(X[1], XH, "xh4")
        aring.wait_copied(dve, "srow.1")
        step(V_.tensor_tensor(gt, Srow, ident[:].rearrange("p (o t) -> p o t", o=1).to_broadcast([128, B, T]), ALU.mult))
        step(V_.tensor_reduce(scol[:], gt, axis=AX.X, op=ALU.add))
        V_.tensor_tensor(gt, Srow, wide(scol[:], [128, B, T]), ALU.is_gt)
        step(V_.tensor_tensor(eq, Srow, wide(scol[:], [128, B, T]), ALU.is_equal))
        step(V_.tensor_tensor(eq, eq, before[:].rearrange("p (o t) -> p o t", o=1).to_broadcast([128, B, T]), ALU.mult))
        step(V_.tensor_tensor(gt, gt, eq, ALU.add))
        step(V_.tensor_reduce(rank[:], gt, axis=AX.X, op=ALU.add))
        step(V_.tensor_scalar(sel[:], rank[:], float(KSEL), None, ALU.is_lt))
        V_.tensor_scalar(unsel[:], sel[:], -1.0, 1.0, ALU.mult, ALU.add).then_inc(event("unsel"), 1)
        V_.tensor_copy(cumU[:], PS[:, take("cumU"), 0:B]).then_inc(dring.copied, 1)
        dve.wait_ge(dring.copied, dring.emptied)
        step(V_.tensor_scalar(posa[:], cumU[:], -1.0, slot_base[:], ALU.mult, ALU.add))
        step(V_.tensor_tensor(posa[:], posa[:], sel[:], ALU.mult))
        step(V_.tensor_tensor(pos[:], cumU[:], unsel[:], ALU.mult))
        step(V_.tensor_tensor(pos[:], pos[:], posa[:], ALU.add))
        V_.tensor_tensor(Perm, colnum[:].rearrange("p (o t) -> p o t", o=1).to_broadcast([128, B, T]),
                         wide(pos[:], [128, B, T]), ALU.is_equal).then_inc(event("perm"), 1)
        loaded(dve, "l4", "ssm")
        V_.tensor_scalar(mb4[:], headmask[:], bqk4[:, 1:2], None, ALU.mult).then_inc(event("small4"), 1)
        V_.tensor_tensor(va, PS[:, take("va"), 0:256].rearrange("p (b n) -> p b n", b=2),
                         bv4[:].rearrange("p (o n) -> p o n", o=1).to_broadcast([128, 2, D]), ALU.add)\
            .then_inc(dring.copied, 1)
        W384 = HB * TS
        for c in range(2):
            V_.tensor_copy(BC[:, c * W384:(c + 1) * W384], PS[0:96, take(f"BC.{c}"), 0:W384]).then_inc(dring.copied, 1)
        dve.wait_ge(dring.copied, dring.emptied)
        step(V_.tensor_copy(BCh, BC))
        V_.tensor_copy(BC3[0:32], BCh[0:32])
        step(V_.tensor_tensor(BC, BC, BCh, ALU.subtract))
        step(V_.tensor_copy(BCm, BC))
        V_.tensor_copy(BC3[32:64], BCm[32:64])
        V_.tensor_tensor(BC3[64:96], BC[64:96], BCm[64:96], ALU.subtract).then_inc(event("bc_parts"), 1)
        dve.wait_ge(event("sa_ready"), 1)
        Sa = PS[:, 0:4, 0:256].rearrange("p g (n k) -> p g n k", k=KSEL)
        step(V_.tensor_reduce(mxa[:].rearrange("p (g n) -> p g n", g=G), Sa, axis=AX.X, op=ALU.max))
        for g in range(G):
            ins = V_.tensor_tensor(Pa[:, 8 * g:8 * g + 8, :], Sa[:, g], wide(mxa[:, 8 * g:8 * g + 8], [128, 8, KSEL]),
                                   ALU.subtract)
        ins.then_inc(event("pa_shifted"), 1)
        dve.wait_ge(event("softplus_parts"), 1)
        step(V_.tensor_scalar(sp_abs, sp_exp, 1.0, -1.0, ALU.add, ALU.add))
        step(V_.tensor_tensor(sp_abs, sp_exp, sp_abs, ALU.subtract))
        step(V_.tensor_tensor(sp_abs, sp_abs, sp_log, ALU.add))
        step(V_.tensor_tensor(delta, sp_abs, sp_relu, ALU.add))
        dve.wait_ge(event("a_exp"), 1)
        V_.tensor_scalar(Aneg[:], Aneg[:], -1.0, None, ALU.mult)
        for i in range(NDA):
            V_.memset(dA[i].rearrange("p (b t) -> p b t", b=B)[:, :, 0:1], 0.0)
        V_.tensor_tensor(du, delta, xc, ALU.mult).then_inc(event("delta_ready"), 1)
        dve.wait_ge(event("delta_ready"), 1)
        dve.wait_ge(event("pa_exp"), 1)
        step(V_.tensor_reduce(sma[:], Pa, axis=AX.X, op=ALU.add))
        step(V_.reciprocal(sma[:], sma[:]))
        step(V_.tensor_tensor(Pa, Pa, wide(sma[:], [128, 2 * H, KSEL]), ALU.mult))
        V_.transpose(PaT.rearrange("p n k -> p (n k)"), Pa.rearrange("p n k -> p (n k)")).then_inc(event("paT"), 1)
        dve.wait_ge(event("oa_ready"), 1)
        for c in range(4):
            ins = V_.tensor_copy(oa[32 * c:32 * c + 32, :, :],
                                 PS[32 * c:32 * c + 32, 4 + c, 0:256].rearrange("p (b n) -> p b n", b=2))
        ins.then_inc(event("oa_copied"), 1)
        loaded(dve, "bc4")
        for c in range(2):
            V_.tensor_tensor(dpos[TS:T, c * HB:(c + 1) * HB, :],
                             PS[TS:T, take(f"dposA.{c}"), :].rearrange("p (b n) -> p b n", b=HB),
                             posbias[TS:T, :].rearrange("p (o n) -> p o n", o=1).to_broadcast([KSEL, HB, D]),
                             ALU.add).then_inc(dring.copied, 1)
        def scan(m):
            dve.wait_ge(event("dBu_ready"), m + 1)
            dve.wait_ge(event("dA_ready"), m + 1)
            if m >= NHS:
                dve.wait_ge(event("hC_ready"), m - NHS + 1)
            V_.tensor_tensor_scan(hst[m % NHS], dA[m % NDA], dBu[m % NDB], 0.0, ALU.mult, ALU.add)\
                .then_inc(event("h_ready"), 1)

        for n in range(NH * DS):
            s, h = n // NH, n % NH
            dve.wait_ge(event("b_copied"), s + 1)
            if n >= NDB:
                dve.wait_ge(event("h_ready"), n - NDB + 1)
            V_.tensor_tensor(dBu[n % NDB], du[:, h, :], Bsb[s % 2], ALU.mult).then_inc(event("dBu_ready"), 1)
            if n >= 1:
                scan(n - 1)
        scan(NH * DS - 1)
        dve.wait_ge(event("hC_used"), NH * DS)
        for h in range(NH):
            ins = V_.tensor_tensor(xc[:, h, :].rearrange("p (c n) -> p c n", c=2), PS[:, 2 * h:2 * h + 2, 0:W384],
                                   zs[:, h, :].rearrange("p (c n) -> p c n", c=2), ALU.mult)
        ins.then_inc(event("y_gated"), 1)
        for c in range(2):
            V_.tensor_copy(dpos[0:TS, c * HB:(c + 1) * HB, :],
                           PS[0:TS, take(f"dposS.{c}"), :].rearrange("p (b n) -> p b n", b=HB)).then_inc(dring.copied, 1)
        for c in range(2):
            i = take(f"dl.{c}")
            V_.scalar_tensor_tensor(half(R, c), half(X[1], c), 2.0, bank4(i), ALU.mult, ALU.add).then_inc(dring.copied, 1)
        dve.wait_ge(dring.copied, dring.emptied)
        norm_halves(R, X[0], "x4")
        dve.wait_ge(event("x4"), 2)
        attention_vector(at5)

        i = take("logits6")
        lg = PS[:, i, 0:B * E1].rearrange("p (b e) -> p b e", b=B)
        step(V_.tensor_reduce(am[:], lg, axis=AX.X, op=ALU.max))
        V_.tensor_tensor(aff[:], lg, wide(am[:], [128, B, E1]), ALU.subtract).then_inc(dring.copied, 1)
        dve.wait_ge(dring.copied, dring.emptied)
        dve.wait_ge(event("aff_exp"), 1)
        step(V_.tensor_reduce(am[:], aff[:], axis=AX.X, op=ALU.add))
        step(V_.reciprocal(am[:], am[:]))
        step(V_.tensor_tensor(aff[:], aff[:], wide(am[:], [128, B, E1]), ALU.mult))
        dve.wait_ge(at5.x_ready, B)
        for e in range(E1 + 1):
            if e < E1:
                for k in range(NI * 2):
                    n = e * NI * 2 + k
                    i, c = k // 2, k % 2
                    dve.wait_ge(event("up_ready"), n + 1)
                    dve.wait_ge(event("silu_ready"), n + 1)
                    if e >= 2:
                        dve.wait_ge(event("down_ready"), 2 * (e - 1))
                    V_.tensor_tensor(hidE[e % 2][:, i, c * 512:(c + 1) * 512], silu6[n % 4], PS[:, 2 + n % 2, :],
                                     ALU.mult).then_inc(event("hidden_ready"), 1)
            if e >= 1:
                p = e - 1
                for c in range(2):
                    dve.wait_ge(event("down_ready"), 2 * p + c + 1)
                    for b4 in range(HB):
                        b = c * HB + b4
                        if p >= 1:
                            dve.wait_ge(event("summed"), B * (p - 1) + b + 1)
                        V_.scalar_tensor_tensor(R[:, b, :], PS[:, 4 + (2 * p + c) % 4, b4 * D:(b4 + 1) * D],
                                                aff[:, b, p:p + 1], (R if p else X[1])[:, b, :],
                                                ALU.mult, ALU.add).then_inc(event("summed"), 1)
        dve.wait_ge(event("summed"), B * E1)
        norm_halves(R, X[0], "out_ready")

    @block.tensor
    def _(pe):
        M_ = nc.tensor.matmul

        def fill(ring, name):
            return ring.fill(pe, name)

        def half(t, c):
            return t[:, c * HB:(c + 1) * HB, :]

        def flat(ap):
            return ap.rearrange("p b t -> p (b t)")

        def transposes(name, srcs, rows, cols):
            i = fill(aring, name)
            for k, src in enumerate(srcs):
                ins = nc.tensor.transpose(PS[0:cols, i, k * rows:(k + 1) * rows], src, ident[0:rows, 0:rows])
            ins.then_inc(aring.full, 1)

        def product(ring, name, lhsT, rhs, rows=128, cols=512):
            i = fill(ring, name)
            M_(PS[0:rows, i, 0:cols], lhsT, rhs, start=True, stop=True).then_inc(ring.full, 1)

        def row_products(ring, name, lhsTs, rhs, rows=128, width=D):
            i = fill(ring, name)
            for k, lhsT in enumerate(lhsTs):
                ins = M_(PS[0:rows, i, k * width:(k + 1) * width], lhsT, rhs, start=True, stop=True)
            ins.then_inc(ring.full, 1)

        def x_transposed(stage, X_, ready, per_half):
            for c in range(2):
                pe.wait_ge(ready, per_half * (c + 1))
                transposes(f"{stage}.{c}", [X_[:, b, :] for b in range(c * HB, (c + 1) * HB)], 128, 128)

        def attention_tensor(at):
            nk = at.nk
            aring.drain(pe)
            dring.drain(pe)
            for s in range(-2, NU + 15):
                if s + 2 < NU:
                    u = s + 2
                    b, g = u // G, u % G
                    if u >= 3:
                        pe.wait_ge(at.shifted, u - 2)
                    if g == 0:
                        pe.wait_ge(at.queries_ready, b + 1)
                    dst = PS[:, u % 3, 0:J * nk].rearrange("p (j k) -> p j k", j=J)
                    ins = M_(dst, qG[:, b % 2, g, :], at.kM[:, :, b, :], start=True, stop=not at.masked)
                    if at.masked:
                        ins = M_(dst, identb[:], maskneg[:].rearrange("p (o k) -> p o k", o=1).to_broadcast([128, J, nk]),
                                 start=False, stop=True)
                    ins.then_inc(at.scores_ready, 1)
                def row_of(lag):
                    b = (s - lag) // G
                    return b if s >= lag and (s - lag) % G == 0 and b < B else None

                if (b := row_of(6)) is not None:
                    pe.wait_ge(at.outT_copied, b + 1)
                    for g in range(G):
                        ins = nc.tensor.transpose(PS[:, 5 + b % 2, 128 * g:128 * g + 128], outT[:, g, :], ident[:])
                    ins.then_inc(at.out_ready, 1)
                if (b := row_of(10)) is not None:
                    pe.wait_ge(at.normed, b + 1)
                    if b:
                        pe.wait_ge(at.residual_ready, b)
                    nc.tensor.transpose(PS[:, 7, 0:128], oN[:, b % 2, :], ident[:]).then_inc(at.normedT_ready, 1)
                if (b := row_of(12)) is not None:
                    pe.wait_ge(at.normedT_copied, b + 1)
                    M_(PS[:, 7, 128:256], oNT[:, b % 2, :], at.Wo, start=True, stop=True).then_inc(at.proj_ready, 1)
                if 0 <= s < NU:
                    pe.wait_ge(at.exp_ready, s + 1)
                    if s >= 2:
                        pe.wait_ge(at.probsT_copied, s - 1)
                    for j in range(J):
                        ins = nc.tensor.transpose(PS[0:nk, 3 + s % 2, 128 * j:128 * j + 128], Eb[:, s % 3, j, 0:nk], ident[:])
                    ins.then_inc(at.probsT_ready, 1)
                if 1 <= s <= NU:
                    u = s - 1
                    b, g = u // G, u % G
                    pe.wait_ge(at.probsT_copied, u + 1)
                    if g == 0 and b >= 2:
                        pe.wait_ge(at.normed, b - 1)
                    for j in range(J):
                        ins = M_(PS[32 * j:32 * j + 32, 5 + b % 2, 128 * g:128 * g + 128], at.V[0:nk, b, J * g + j, :],
                                 PT[0:nk, u % 3, j, :], start=True, stop=True)
                    ins.then_inc(at.pv_done, 1)
            pe.wait_ge(at.residual_ready, B)

        pe.wait_ge(const_ready, 1)
        loaded(pe, "ctx")
        for c in range(2):
            transposes(f"ctxT.{c}", [ctxN[0:NC, b, :] for b in range(c * HB, (c + 1) * HB)], NC, 128)
        loaded(pe, "l5", "l2")
        transposes("W5T", [W5[:, k, :] for k in range(4)], 128, 128)
        aring.wait_copied(pe, "ctxT.1")
        pe.wait_ge(event("w2_centred"), 1)
        for p in range(4):
            row_products(dring, f"kv.{p}", [ctxT[:, b, :] for b in (2 * p, 2 * p + 1)], Wkv2[:], NC, 2 * D)
        aring.wait_copied(pe, "W5T")
        for c in range(2):
            product(aring, f"k5.{c}", W5T[:, 1, :], half(ctxT, c), cols=HB * NC)
        for c in range(2):
            row_products(dring, f"v5.{c}", [ctxT[:, b, :] for b in range(c * HB, (c + 1) * HB)], W5T[:, 2, :], NC)
        loaded(pe, "a1")
        for c in range(2):
            pe.wait_ge(event("xh1"), c + 1)
            transposes(f"x0T.{c}", [XH[:, b, :] for b in range(c * HB, (c + 1) * HB)], 128, 128)
        for c in range(2):
            aring.wait_copied(pe, f"x0T.{c}")
            product(aring, f"q1.{c}", Wqkv1[:, 0:D], half(xT, c))
            product(aring, f"k1.{c}", Wqkv1[:, D:2 * D], half(xT, c))
            row_products(dring, f"v1.{c}", [xT[:, b, :] for b in range(c * HB, (c + 1) * HB)], Wqkv1[:, 2 * D:3 * D])
        pe.wait_ge(event("v_ones"), 1)
        attention_tensor(at1)

        x_transposed("x1T", X[1], at1.x_ready, HB)
        pe.wait_ge(event("kn_ready"), 1)
        for c in range(2):
            transposes(f"k2.{c}", [sq[0:NC, b, :] for b in range(c * HB, (c + 1) * HB)], NC, 128)
        pe.wait_ge(event("w2_centred"), 2)
        for c in range(2):
            aring.wait_copied(pe, f"x1T.{c}")
            row_products(dring, f"q2.{c}", [xT[:, b, :] for b in range(c * HB, (c + 1) * HB)], Wq2[:])
        loaded(pe, "l3")
        transposes("down3T", [down3[:, k, :] for k in range(4)], 128, 128)
        transposes("up3T", [up3[:, 2 * k:2 * k + 2, :].rearrange("p e c -> p (e c)") for k in range(4)], 128, 128)
        transposes("gate3T", [gate3[:]], E0, 128)
        pe.wait_ge(event("v_ones"), 2)
        pe.wait_ge(event("qn_ready"), 1)
        for c in range(2):
            transposes(f"q2T.{c}", [sq[:, b, :] for b in range(c * HB, (c + 1) * HB)], 128, 128)
        attention_tensor(at2)

        x_transposed("x2T", X[0], at2.x_ready, HB)
        pe.wait_ge(event("pooled"), 1)
        product(dring, "logits8", pooledT[:], gate3T[:], 8, 8)
        for c in range(2):
            for t in range(4):
                product(aring, f"hid.{t}.{c}", down3T[:, t * 128:(t + 1) * 128], half(xT, c))
        pe.wait_ge(event("c8_ready"), 1)
        i = fill(dring, "cT")
        nc.tensor.transpose(PS[0:8, i, 0:8], c8[:], ident[0:8, 0:8]).then_inc(dring.full, 1)
        dring.wait_copied(pe, "cT")
        i = fill(dring, "cexp")
        for t in range(4):
            ins = M_(PS[:, i, t * B:(t + 1) * B], spread8[:, t * 128:(t + 1) * 128], cT[:], start=True, stop=True)
        ins.then_inc(dring.full, 1)
        for c in range(2):
            pe.wait_ge(event("hid_scaled"), 4 * (c + 1))
            i = fill(dring, f"up.{c}")
            for b4 in range(HB):
                b = c * HB + b4
                dst = PS[:, i, b4 * D:(b4 + 1) * D]
                for t in range(4):
                    M_(dst, hid[:, t, b * T:(b + 1) * T], up3T[:, t, :], start=(t == 0), stop=False)
                ins = M_(dst, cT[:, b:b + 1].to_broadcast([8, 128]), upb3[:], start=False, stop=True)
            ins.then_inc(dring.full, 1)

        loaded(pe, "l4")
        x_transposed("xnT", XH, event("xh4"), 1)
        for c in range(2):
            aring.wait_copied(pe, f"xnT.{c}")
            product(aring, f"router.{c}", rw1[:], half(xT, c), rows=D // 2)
        for c in range(2):
            aring.wait_copied(pe, f"router.{c}")
            product(aring, f"srow.{c}", rw2[:].to_broadcast([D // 2, 128]), half(hrT, c))
        pe.wait_ge(event("unsel"), 1)
        product(dring, "cumU", after[:], unsel[:], cols=B)
        pe.wait_ge(event("perm"), 1)
        for c in range(2):
            transposes(f"permT.{c}", [Perm[:, b, :] for b in range(c * HB, (c + 1) * HB)], 128, 128)
        for c in range(2):
            i = fill(aring, f"xpT.{c}")
            for b4 in range(HB):
                ins = M_(PS[:, i, b4 * T:(b4 + 1) * T], XH[:, c * HB + b4, :], Perm[:, c * HB + b4, :], start=True, stop=True)
            ins.then_inc(aring.full, 1)
        loaded(pe, "ssm")
        pe.wait_ge(event("ssm_weights"), 1)
        aring.wait_copied(pe, "xpT.1")
        W384 = HB * TS
        for h in range(NH):
            for c in range(2):
                i = fill(aring, f"conv.{h}.{c}")
                for j in range(DC):
                    ins = M_(PS[:, i, 0:W384], convin[:, j, 128 * h:128 * h + 128],
                             xpT[:, c * HB:(c + 1) * HB, j:j + TS], start=(j == 0), stop=(j == DC - 1))
                ins.then_inc(aring.full, 1)
        for h in range(NH):
            for c in range(2):
                product(aring, f"z.{h}.{c}", inw4[:, DIN + 128 * h:DIN + 128 * h + 128],
                        xpT[:, c * HB:(c + 1) * HB, DC - 1:DC - 1 + TS], cols=W384)
        chosen = xpT[:, :, DC - 1 + TS:]
        product(aring, "qa", Wqkvo4[:, 0, :], chosen, cols=B * KSEL)
        product(aring, "ka", Wqkvo4[:, 1, :], chosen, cols=B * KSEL)
        i = fill(dring, "va")
        for b in range(B):
            n, c = b // 4, b % 4
            ins = M_(PS[32 * c:32 * c + 32, i, n * D:(n + 1) * D], chosen[:, b, :], Wqkvo4[:, 2, :], start=True, stop=True)
        ins.then_inc(dring.full, 1)
        aring.wait_copied(pe, "conv.1.1")
        for c in range(2):
            w = slice(c * W384, (c + 1) * W384)
            i = fill(aring, f"dt.{c}")
            for h in range(NH):
                ins = M_(PS[0:DTR, i, 0:W384], xproj[:, h, 0:DTR], xc[:, h, w], start=(h == 0), stop=(h == NH - 1))
            ins.then_inc(aring.full, 1)
        for c in range(2):
            w = slice(c * W384, (c + 1) * W384)
            i = fill(dring, f"BC.{c}")
            for h in range(NH):
                ins = M_(PS[0:96, i, 0:W384], xprojBC[:, h, :], xc[:, h, w], start=(h == 0), stop=(h == NH - 1))
            ins.then_inc(dring.full, 1)
        aring.wait_copied(pe, "dt.1")
        for h in range(NH):
            for c in range(2):
                product(aring, f"delta.{h}.{c}", dtw[:, 128 * h:128 * h + 128], dtp[:, c * W384:(c + 1) * W384], cols=W384)
        aring.drain(pe)
        for g in range(G):
            for b in range(B):
                n, c = b // 4, b % 4
                ins = M_(PS[32 * c:32 * c + 32, g, n * 128:(n + 1) * 128].rearrange("p (j k) -> p j k", j=J),
                         qTa[32 * g:32 * g + 32, b, :], kMa[32 * g:32 * g + 32, :, b, :], start=True, stop=True)
        ins.then_inc(event("sa_ready"), 1)
        pe.wait_ge(event("paT"), 1)
        dring.drain(pe)
        for c in range(4):
            r = slice(32 * c, 32 * c + 32)
            for n in range(2):
                for hh in range(H):
                    g, j = hh // J, hh % J
                    ins = M_(PS[r, 4 + c, n * D + hh * HD:n * D + (hh + 1) * HD], PaT[r, 8 * g + 4 * n + j, :],
                             va[r, n, hh * HD:(hh + 1) * HD], start=True, stop=True)
        ins.then_inc(event("oa_ready"), 1)
        pe.wait_ge(event("oa_copied"), 1)
        transposes("oaT", [oa[:, n, :] for n in range(2)], 128, 128)
        aring.wait_copied(pe, "oaT")
        for c in range(2):
            i = fill(dring, f"dposA.{c}")
            for b4 in range(HB):
                ins = M_(PS[TS:T, i, b4 * D:(b4 + 1) * D], oaT[:, c, 32 * b4:32 * b4 + 32], Wqkvo4[:, 3, :],
                         start=True, stop=True)
            ins.then_inc(dring.full, 1)
        aring.drain(pe)
        for h in range(NH):
            for c in range(2):
                M_(PS[:, 2 * h + c, 0:W384], diagD[:, h, :], xc[:, h, c * W384:(c + 1) * W384], start=True, stop=False)
        dring.drain(pe)
        pe.wait_ge(event("bc_parts"), 1)

        def spread(s):
            if s:
                pe.wait_ge(event("b_copied"), s)
                pe.wait_ge(event("c_copied"), s)
            for k in range(2):
                for c in range(2):
                    ins = M_(PS[:, 4 + 2 * k + c, 0:W384], part_pick[:, DS * k + s:DS * k + s + 1].to_broadcast([96, 128]),
                             BC3[:, c * W384:(c + 1) * W384], start=True, stop=True)
            ins.then_inc(event("bc_ready"), 1)

        def accumulate(s):
            for h in range(NH):
                n = NH * s + h
                pe.wait_ge(event("hC_ready"), n + 1)
                for c in range(2):
                    ins = M_(PS[:, 2 * h + c, 0:W384], ident[:], hC[n % NHC][:, c * W384:(c + 1) * W384], start=False,
                             stop=(s == DS - 1))
                ins.then_inc(event("hC_used"), 1)

        for s in range(DS):
            spread(s)
            if s >= 2:
                accumulate(s - 2)
        accumulate(DS - 2)
        accumulate(DS - 1)
        pe.wait_ge(event("y_gated"), 1)
        for c in range(2):
            i = fill(dring, f"dposS.{c}")
            for b4 in range(HB):
                b = c * HB + b4
                for h in range(NH):
                    ins = M_(PS[0:TS, i, b4 * D:(b4 + 1) * D], xc[:, h, b * TS:(b + 1) * TS], outw4[:, h, :],
                             start=(h == 0), stop=(h == NH - 1))
            ins.then_inc(dring.full, 1)
        for c in range(2):
            dring.wait_copied(pe, f"dposS.{c}")
            i = fill(dring, f"dl.{c}")
            for b4 in range(HB):
                b = c * HB + b4
                ins = M_(PS[:, i, b4 * D:(b4 + 1) * D], PermT[:, b, :], dpos[:, b, :], start=True, stop=True)
            ins.then_inc(dring.full, 1)

        x_transposed("x4T", X[0], event("x4"), 1)
        for c in range(2):
            aring.wait_copied(pe, f"x4T.{c}")
            product(aring, f"q5.{c}", W5T[:, 0, :], half(xT, c))
        attention_tensor(at5)

        loaded(pe, "g6")
        x_transposed("x5T", X[1], at5.x_ready, HB)
        aring.wait_copied(pe, "x5T.1")
        row_products(dring, "logits6", [xT[:, b, :] for b in range(B)], gate6[:], width=E1)
        dring.drain(pe)

        def down(e):
            for c in range(2):
                if 2 * e + c >= 4:
                    pe.wait_ge(event("summed"), B * (e - 2) + HB * (c + 1))
                pe.wait_ge(event("hidden_ready"), NI * 2 * (e + 1))
                for b4 in range(HB):
                    b = c * HB + b4
                    for i in range(NI):
                        ins = M_(PS[:, 4 + (2 * e + c) % 4, b4 * D:(b4 + 1) * D], hidE[e % 2][:, i, b * T:(b + 1) * T],
                                 Wd6[:, NI * e + i, :], start=(i == 0), stop=(i == NI - 1))
                ins.then_inc(event("down_ready"), 1)

        pe.wait_ge(experts_loaded, 3 * 16)
        for e in range(E1):
            for i in range(NI):
                for c in range(2):
                    n = e * NI * 2 + 2 * i + c
                    if n >= 2:
                        pe.wait_ge(event("silu_ready"), n - 1)
                    M_(PS[:, n % 2, :], Wg6[:, e, i * 128:(i + 1) * 128], half(xT, c), start=True, stop=True)\
                        .then_inc(event("gate_ready"), 1)
                    if n >= 2:
                        pe.wait_ge(event("hidden_ready"), n - 1)
                    M_(PS[:, 2 + n % 2, :], Wu6[:, e, i * 128:(i + 1) * 128], half(xT, c), start=True, stop=True)\
                        .then_inc(event("up_ready"), 1)
            if e:
                down(e - 1)
        down(E1 - 1)


_INS = [
    'x', 'ctx_1024', 'mask_1x1xSxS2_bk1', 'L0_attn_ln_gamma', 'L0_attn_ln_beta', 'L0_attn_w_qkv', 'L0_attn_b_qkv',
    'L0_attn_w_out', 'L0_attn_b_out', 'L0_xattn_Wq', 'L0_xattn_Wkv', 'L0_xattn_Wp', 'L0_xattn_bp',
    'L0_xattn_ln_g', 'L0_xattn_ln_b', 'L0_ffn_gate_w', 'L0_ffn_down_w', 'L0_ffn_down_b', 'L0_ffn_up_w',
    'L0_ffn_up_b', 'L1_attn_ln_w', 'L1_attn_ln_b', 'L1_attn_r_w1', 'L1_attn_r_b1', 'L1_attn_r_w2', 'L1_attn_r_b2',
    'L1_attn_Wq', 'L1_attn_bq', 'L1_attn_Wk', 'L1_attn_bk', 'L1_attn_Wv', 'L1_attn_bv', 'L1_attn_Wo',
    'L1_attn_bo', 'L1_attn_in_w', 'L1_attn_conv_w', 'L1_attn_conv_b', 'L1_attn_xproj_w', 'L1_attn_dt_w',
    'L1_attn_dt_b', 'L1_attn_A_log', 'L1_attn_Dp', 'L1_attn_out_w', 'L1_xattn_W_q', 'L1_xattn_W_k',
    'L1_xattn_W_v', 'L1_xattn_W_o', 'L1_ffn_gate_w', 'L1_ffn_Wg', 'L1_ffn_Wu', 'L1_ffn_Wd',
]
_SHAPE = (B, T, D)


def kernel(**inputs):
    import concourse.bacc as _bacc
    from concourse.bass_utils import run_bass_kernel_spmd as _run

    nc = _bacc.Bacc("TRN2", target_bir_lowering=False, num_devices=1)
    arrays, args = {}, {}
    for name in _INS:
        x = np.ascontiguousarray(inputs[name])
        if x.dtype.kind == "b":
            x = x.reshape(-1).view(np.int32)
        arrays[f"in_{name}"] = x
        args[name] = nc.dram_tensor(f"in_{name}", x.shape, mybir.dt.from_np(x.dtype), kind="ExternalInput").ap()
    out = nc.dram_tensor("out_x", _SHAPE, F32, kind="ExternalOutput").ap()
    build(nc, args, out)
    return _run(nc, [arrays], core_ids=[0]).results[0]["out_x"]
```

```python
from contextlib import ExitStack
import math

import numpy as np

import concourse.bass as bass
from concourse import mybir

F32 = mybir.dt.float32
BF16 = mybir.dt.bfloat16
U8 = mybir.dt.uint8
ALU = mybir.AluOpType
ACT = mybir.ActivationFunctionType
AX = mybir.AxisListType

B, T, D = 8, 128, 128
H, HD = 16, 8
G = 4
J = H // G
NU = B * G
NC = 77
VW = 32
HB = B // 2
E0, BN = 8, 64
KSEL = T // 4
TS = T - KSEL
DC, DS, DTR = 4, 16, 8
DIN = 2 * D
NH = DIN // 128
E1, IW = 8, 256
NI = IW // 128
EPS = 1e-5
MASKED = -1e30
K_PARTS = [(0, 32), (32, 64), (64, 96)] + [(n, n + 8) for n in range(96, B * H, 8)]


class Ring:

    def __init__(self, banks, full, copied, jobs):
        self.banks, self.full, self.copied, self.jobs = banks, full, copied, jobs
        self.index = {name: n for n, name in enumerate(jobs)}
        self.filled = self.emptied = 0

    def fill(self, pe, name):
        n, size = self.filled, len(self.banks)
        assert self.jobs[n] == name, (self.jobs[n], name)
        if n >= size:
            pe.wait_ge(self.copied, n - size + 1)
        self.filled += 1
        return self.banks[n % size]

    def take(self, reader, name):
        n = self.emptied
        assert self.jobs[n] == name, (self.jobs[n], name)
        reader.wait_ge(self.full, n + 1)
        self.emptied += 1
        return self.banks[n % len(self.banks)]

    def wait_copied(self, eng, *names):
        eng.wait_ge(self.copied, max(self.index[n] for n in names) + 1)

    def drain(self, pe):
        if self.filled:
            pe.wait_ge(self.copied, self.filled)


class Count:

    def __init__(self, sem):
        self.sem, self.n = sem, 0

    def then(self, ins):
        ins.then_inc(self.sem, 1)
        self.n += 1
        return self.n


class Attention:

    def __init__(self, sem, name, nk, scale, kM, V, Wo, XB, Xout, masked=False):
        self.nk, self.scale, self.kM, self.V = nk, scale, kM, V
        self.Wo, self.XB, self.Xout, self.masked = Wo, XB, Xout, masked
        self.queries_ready = sem(f"{name}_queries_ready")
        self.scores_ready = sem(f"{name}_scores_ready")
        self.max_ready = sem(f"{name}_max_ready")
        self.shifted = sem(f"{name}_shifted")
        self.exp_ready = sem(f"{name}_exp_ready")
        self.probsT_ready = sem(f"{name}_probsT_ready")
        self.probsT_copied = sem(f"{name}_probsT_copied")
        self.pv_done = sem(f"{name}_pv_done")
        self.outT_copied = sem(f"{name}_outT_copied")
        self.out_ready = sem(f"{name}_out_ready")
        self.recip_ready = sem(f"{name}_recip_ready")
        self.normed = sem(f"{name}_normed")
        self.normedT_ready = sem(f"{name}_normedT_ready")
        self.normedT_copied = sem(f"{name}_normedT_copied")
        self.proj_ready = sem(f"{name}_proj_ready")
        self.residual_ready = sem(f"{name}_residual_ready")
        self.stats_ready = sem(f"{name}_stats_ready")
        self.var_ready = sem(f"{name}_var_ready")
        self.eps_ready = sem(f"{name}_eps_ready")
        self.rstd_ready = sem(f"{name}_rstd_ready")
        self.x_ready = sem(f"{name}_x_ready")
        self.xb_ready = sem(f"{name}_xb_ready")


ACT_JOBS = (["ctxT.0", "ctxT.1", "x0T.0", "x0T.1", "q1.0", "k1.0", "q1.1", "k1.1"]
            + ["x1T.0", "down3T", "up3T", "gate3T", "x1T.1", "k2.0", "k2.1", "q2T.0", "q2T.1"]
            + ["x2T.0"] + [f"hid.{t}.{c}" for c in range(2) for t in range(4)]
            + ["xnT.0", "xnT.1", "router.0", "router.1", "srow.0", "srow.1", "W5T", "xprojT", "Wdt.0", "Wdt.1", "k5.0", "k5.1", "v5.0", "v5.1", "xpT.0", "xpT.1"]
            + ["qa", "ka", "permT.0", "permT.1"] + [f"conv.{h}.{c}" for h in range(2) for c in range(2)]
            + [f"delta.{h}.{c}" for h in range(2) for c in range(2)] + [f"z.{h}.{c}" for h in range(2) for c in range(2)]
            + ["x4T.0", "x4T.1", "q5.0", "q5.1", "x5T.0"])
DVE_JOBS = (["kv.0", "kv.1", "kv.2", "kv.3", "v1.0", "v1.1", "q2.0", "q2.1"]
            + ["x2T.1", "logits8", "cT", "cexp", "up.0", "up.1", "scol"]
            + ["cumU", "va", "BC.0", "BC.1", "dposA.0", "dposA.1", "dposS.0", "dposS.1", "dl.0", "dl.1", "x5T.1", "logits6"])


def build(nc, a, out):
    ctx = ExitStack()
    with ctx:
        _build(nc, ctx, a, out)


def _build(nc, ctx, a, out):
    def sb(name, shape, dt=F32):
        return ctx.enter_context(nc.sbuf_tensor(name, shape, dt))

    def sem(name):
        return ctx.enter_context(nc.semaphore(name))

    PS = ctx.enter_context(nc.psum_tensor("PS", [128, 8, 512], F32))

    ident = sb("ident", [128, 128])
    identb = sb("identb", [128, 128], BF16)
    before = sb("before", [128, 128])
    after = sb("after", [128, 128])
    colnum = sb("colnum", [128, 128])
    slot_base = sb("slot_base", [128, 1])
    groupmask = sb("groupmask", [128, G])
    headmask = sb("headmask", [128, J])
    part_pick = sb("part_pick", [96, 32], BF16)
    spread8 = sb("spread8", [E0, E0 * BN])
    xprojBC = sb("xprojBC", [128, NH, 3 * 2 * DS])
    earlier = sb("earlier", [8, 8, 8])
    neg_half = sb("neg_half", [128, HB])
    eps_col = sb("eps_col", [128, 1])
    table_out = sb("table_out", [128, 8])

    gamma1 = sb("gamma1", [128, 1]); beta1 = sb("beta1", [128, 1])
    Wqkv1 = sb("Wqkv1", [128, 3 * D]); bqk1 = sb("bqk1", [128, 2]); bv1 = sb("bv1", [128, D])
    Wo1 = sb("Wo1", [128, D]); bo1 = sb("bo1", [128, D])
    Wq2 = sb("Wq2", [128, D]); Wkv2 = sb("Wkv2", [128, 2 * D]); Wp2 = sb("Wp2", [128, D]); bp2 = sb("bp2", [128, D])
    gbrow2 = sb("gbrow2", [128, 2, HD])
    dmask = sb("dmask", [128, HD])
    gbpick = sb("gbpick", [128, 2, HD])
    gb2 = sb("gb2", [128, 2])
    ctxN = sb("ctxN", [128, B, D])
    untransposed = sb("untransposed", [128, 12 * D])
    W5 = untransposed[:, 0:4 * D].rearrange("p (i n) -> p i n", i=4)
    W5T = sb("W5T", [128, 4, D])
    mask8 = sb("mask8", [128, NC], U8); maskneg = sb("maskneg", [128, NC], BF16)
    maskf = sb("maskf", [128, NC]); nmasked = sb("nmasked", [128, 1]); anykey = sb("anykey", [128, 1])
    gate3 = sb("gate3", [E0, D]); gate3T = sb("gate3T", [128, E0])
    down3 = untransposed[:, 4 * D:8 * D].rearrange("p (i n) -> p i n", i=4)
    down3T = sb("down3T", [128, 4 * 128]); downb3 = sb("downb3", [128, 4])
    up3 = untransposed[:, 8 * D:12 * D].rearrange("p (e c) -> p e c", e=E0)
    up3T = sb("up3T", [128, 4, D]); upb3 = sb("upb3", [128, D])
    lnwb4 = sb("lnwb4", [128, 2])
    rw1 = sb("rw1", [128, D // 2]); rb1 = sb("rb1", [D // 2, 1]); rw2 = sb("rw2", [D // 2, 1]); rb2 = sb("rb2", [128, 1])
    Wqkvo4 = sb("Wqkvo4", [128, 4, D]); bqk4 = sb("bqk4", [128, 2]); bv4 = sb("bv4", [128, D])
    posbias = sb("posbias", [128, D])
    inw4 = sb("inw4", [128, 2 * DIN]); convw = sb("convw", [128, DIN, DC]); convb = sb("convb", [128, NH])
    convin = sb("convin", [128, DC, DIN])
    xprojT = sb("xprojT", [DTR, NH, 128])
    Wdt = sb("Wdt", [128, NH, DIN])
    xproj = sb("xproj", [128, NH, DTR + 2 * DS]); dtw = sb("dtw", [DTR, DIN]); dtb = sb("dtb", [128, NH])
    Alog = sb("Alog", [128, NH, DS]); Aneg = sb("Aneg", [128, NH, DS]); Dp = sb("Dp", [128, NH])
    outw4 = sb("outw4", [128, NH, D]); diagD = sb("diagD", [128, NH, 128])
    gate6 = sb("gate6", [128, E1])

    X = [sb(f"X{i}", [128, B, D]) for i in range(2)]
    XH = sb("XH", [128, B, D])
    XB = sb("XB", [128, B, D])
    xT = sb("xT", [128, B, T])
    ctxT = sb("ctxT", [128, B, NC])
    qT = sb("qT", [128, B, T])
    qG = sb("qG", [128, 2, G, T])
    big = sb("big", [128, J * B * T + B * H * VW])
    kM1 = big[:, 0:J * B * T].rearrange("p (j b t) -> p j b t", j=J, b=B)
    V1 = big[:, J * B * T:].rearrange("p (b h w) -> p b h w", b=B, h=H)
    kM2 = sb("kM2", [128, J, B, NC]); V2full = sb("V2", [128, B * H * VW]); V2 = V2full[0:NC].rearrange("p (b h w) -> p b h w", b=B, h=H)
    kM5 = sb("kM5", [128, J, B, NC]); V5 = sb("V5", [NC, B, H, VW])
    mb1 = sb("mb1", [128, J]); sc2 = sb("sc2", [128, J]); sh2 = sb("sh2", [128, J]); mb4 = sb("mb4", [128, J])
    qc = sb("qc", [128, B, D]); sq = sb("sq", [128, B, D])
    half_bh = sb("half_bh", [128, 32])
    hss = sb("hss", [128, B * H]); hvar = sb("hvar", [128, B * H]); hr0 = sb("hr0", [128, B * H]); hr1 = sb("hr1", [128, B * H])
    wmean = sb("wmean", [128, 2, H])
    Eb = sb("Eb", [128, 3, J, 128]); PT = sb("PT", [128, 3, J, 128]); mx = sb("mx", [128, 3, J])
    outT = sb("outT", [128, G, 128]); rs = sb("rs", [128, 2, H]); oN = sb("oN", [128, 2, D]); oNT = sb("oNT", [128, 2, D])
    R = sb("R", [128, B, D]); st = sb("st", [128, B, 6]); mv = sb("mv", [128, B, 2]); ve = sb("ve", [128, B]); rstd = sb("rstd", [128, B])
    ve4 = sb("ve4", [128, B]); rstd4 = sb("rstd4", [128, B])

    ld = {k: sem(f"loaded_{k}") for k in ("x0", "x1", "ln1", "a1", "ctx", "kv2", "l2", "l5", "l3", "l4", "ssm", "g6", "bc4")}
    experts_loaded = sem("experts_loaded")
    stored = sem("stored")
    const_ready = sem("const_ready")
    aring = Ring([0, 1, 2, 3], sem("act_bank_full"), sem("act_bank_copied"), ACT_JOBS)
    dring = Ring([4, 5, 6, 7], sem("dve_bank_full"), sem("dve_bank_copied"), DVE_JOBS)
    dve_step, act_step, pool_step = Count(sem("dve_step")), Count(sem("act_step")), Count(sem("pool_step"))
    ln_var, ln_rstd = sem("ln_var"), sem("ln_rstd")
    ev = {}

    def event(name):
        if name not in ev:
            ev[name] = sem(name)
        return ev[name]

    at1 = Attention(sem, "at1", T, 1 / math.sqrt(HD), kM1, V1, Wo1[:], XB, X[1])
    at2 = Attention(sem, "at2", NC, math.sqrt(HD), kM2, V2, Wp2[:], XB, X[0])
    at5 = Attention(sem, "at5", NC, 1 / math.sqrt(HD), kM5, V5, W5T[:, 3, :], X[0], X[1], masked=True)

    def bank4(i, p=128):
        return PS[0:p, i, :].rearrange("p (b t) -> p b t", b=4)

    x_src = a["x"].rearrange("b t d -> t b d")

    def col(ap):
        return ap.rearrange("(p o) -> p o", o=1)

    def row(ap, p=128):
        return ap.rearrange("(o n) -> o n", o=1).to_broadcast([p, ap.shape[0]])

    loads = {
        "x0": [(X[0][:, 0:HB, :], x_src[:, 0:HB, :])],
        "x1": [(X[0][:, HB:B, :], x_src[:, HB:B, :])],
        "ln1": [(gamma1[:], col(a["L0_attn_ln_gamma"])), (beta1[:], col(a["L0_attn_ln_beta"]))],
        "a1": [(Wqkv1[:], a["L0_attn_w_qkv"]),
               (bqk1[:], a["L0_attn_b_qkv"][0:2 * D].rearrange("(c p) -> p c", c=2)),
               (bv1[:], row(a["L0_attn_b_qkv"][2 * D:3 * D])),
               (Wo1[:], a["L0_attn_w_out"]), (bo1[:], row(a["L0_attn_b_out"]))],
        "ctx": [(ctxN[0:NC], a["ctx_1024"].rearrange("b t d -> t b d"))],
        "kv2": [(Wkv2[:], a["L0_xattn_Wkv"])],
        "l2": [(Wq2[:], a["L0_xattn_Wq"]), (Wp2[:], a["L0_xattn_Wp"]),
               (bp2[:], row(a["L0_xattn_bp"]))]
              + [(gbrow2[:, c, :], row(a[n])) for c, n in enumerate(("L0_xattn_ln_g", "L0_xattn_ln_b"))],
        "l5": [(W5[:, i, :], a[f"L1_xattn_W_{n}"]) for i, n in enumerate("qkvo")]
              + [(mask8[:], a["mask_1x1xSxS2_bk1"].bitcast(U8).rearrange("(q k) -> q k", k=NC))],
        "l3": [(gate3[:], a["L0_ffn_gate_w"]),
               (down3, a["L0_ffn_down_w"].rearrange("(t e) c d -> (e c) t d", e=2)),
               (downb3[:], a["L0_ffn_down_b"].rearrange("(t e) c -> (e c) t", e=2)),
               (up3, a["L0_ffn_up_w"].rearrange("e d c -> d e c")), (upb3[0:E0], a["L0_ffn_up_b"])],
        "l4": [(lnwb4[:, 0:1], col(a["L1_attn_ln_w"])), (lnwb4[:, 1:2], col(a["L1_attn_ln_b"])),
               (rw1[:], a["L1_attn_r_w1"]), (rb1[:], col(a["L1_attn_r_b1"])), (rw2[:], a["L1_attn_r_w2"]),
               (rb2[:], row(a["L1_attn_r_b2"])),
               (bqk4[:, 0:1], col(a["L1_attn_bq"])), (bqk4[:, 1:2], col(a["L1_attn_bk"])),
               (bv4[:], row(a["L1_attn_bv"]))]
              + [(Wqkvo4[:, i, :], a[f"L1_attn_W{n}"]) for i, n in enumerate("qkvo")],
        "bc4": [(posbias[TS:T, :], row(a["L1_attn_bo"], KSEL))],
        "ssm": [(inw4[:], a["L1_attn_in_w"]),
                (convw[:], a["L1_attn_conv_w"].rearrange("(o n) c -> o n c", o=1).to_broadcast([128, DIN, DC])),
                (convb[:], a["L1_attn_conv_b"].rearrange("(h p) -> p h", p=128)),
                (xproj[:], a["L1_attn_xproj_w"].rearrange("(h p) n -> p h n", p=128)),
                (dtw[:], a["L1_attn_dt_w"]), (dtb[:], a["L1_attn_dt_b"].rearrange("(h p) -> p h", p=128)),
                (Alog[:], a["L1_attn_A_log"].rearrange("(h p) n -> p h n", p=128)),
                (Dp[:], a["L1_attn_Dp"].rearrange("(h p) -> p h", p=128)),
                (outw4[:], a["L1_attn_out_w"].rearrange("(h p) n -> p h n", p=128))],
        "g6": [(gate6[:], a["L1_ffn_gate_w"])],
    }
    need = {k: 16 * len(v) for k, v in loads.items()}

    def loaded(eng, *keys):
        for k in keys:
            eng.wait_ge(ld[k], need[k])

    def load(eng, *keys):
        for k in keys:
            for dst, src in loads[k]:
                eng.dma_start(dst, src, allow_slow_non_contiguous=True).then_inc(ld[k], 16)

    W768 = B * TS
    du = untransposed[:].rearrange("p (h n) -> p h n", h=NH)
    xc = V2full[:, 0:NH * W768].rearrange("p (h n) -> p h n", h=NH)
    zs = V2full[:, NH * W768:2 * NH * W768].rearrange("p (h n) -> p h n", h=NH)
    delta = big[:, 0:2 * W768].rearrange("p (h n) -> p h n", h=NH)

    def spare(t):
        return t[:].rearrange("p b d -> p (b d)")[:, 0:W768]

    dA = [big[:, (2 + i) * W768:(3 + i) * W768] for i in range(2)] + [spare(X[0])]
    dBu = [big[:, (4 + i) * W768:(5 + i) * W768] for i in range(2)] + [spare(xT)]
    hst = [big[:, (6 + i) * W768:(7 + i) * W768] for i in range(2)] + [spare(sq)]
    hC = [big[:, (8 + i) * W768:(9 + i) * W768] for i in range(2)] + [spare(XB), spare(ctxN)]
    NDA, NDB, NHS, NHC = len(dA), len(dBu), len(hst), len(hC)
    kM2flat = kM2[:].rearrange("p j b n -> p (j b n)")
    Bsb = [kM2flat[:, i * W768:(i + 1) * W768] for i in range(2)]
    Csb = [kM2flat[:, 2 * W768:3 * W768], spare(XH)]
    sp_abs = big[:, 2 * W768:4 * W768].rearrange("p (h n) -> p h n", h=NH)
    sp_exp = big[:, 4 * W768:6 * W768].rearrange("p (h n) -> p h n", h=NH)
    sp_log = big[:, 6 * W768:8 * W768].rearrange("p (h n) -> p h n", h=NH)
    sp_relu = big[:, 8 * W768:10 * W768].rearrange("p (h n) -> p h n", h=NH)
    PADT = DC - 1 + T
    xpT = sb("xpT", [128, B, PADT])
    hrT = big[0:D // 2, 2 * B * T:3 * B * T].rearrange("p (b t) -> p b t", b=B)
    Srow = big[:, 0:B * T].rearrange("p (b t) -> p b t", b=B)
    scol = sb("scol", [128, B]); gt = big[:, B * T:2 * B * T].rearrange("p (b t) -> p b t", b=B); eq = V2full[:, 2 * NH * W768:2 * NH * W768 + B * T].rearrange("p (b t) -> p b t", b=B)
    rank = sb("rank", [128, B]); ties = sb("ties", [128, B]); sel = sb("sel", [128, B]); unsel = sb("unsel", [128, B]); cumU = sb("cumU", [128, B])
    pos = sb("pos", [128, B]); posa = sb("posa", [128, B])
    Perm = gt; PermT = eq
    qTa = ctxT[:].rearrange("p b t -> p (b t)")[:, 0:B * KSEL].rearrange("p (b k) -> p b k", b=B); kMa = PT[:].rearrange("p a j t -> p (a j t)")[:, 0:J * B * KSEL].rearrange("p (j b k) -> p j b k", j=J, b=B); va = R[:, 0:2, :]
    Pa = convw[:].rearrange("p n c -> p (n c)").rearrange("p (n k) -> p n k", k=KSEL)
    PaT = XB[:].rearrange("p b d -> p (b d)").rearrange("p (n k) -> p n k", k=KSEL)
    mxa = sb("mxa", [128, 2 * H]); sma = sb("sma", [128, 2 * H])
    oaT = R[:, 4:6, :]
    oa_heads = Pa
    qGa = qG[:].rearrange("p i g t -> p (i g t)").rearrange("p (g b k) -> p g b k", g=G, b=B)
    Ebflat = Eb[0:96].rearrange("p a j t -> p (a j t)")
    sqb = sq[0:96].rearrange("p b d -> p (b d)").bitcast(BF16)
    BC, BC3 = Ebflat[:, 0:W768], Ebflat[:, W768:].bitcast(BF16)[:, 0:W768]
    BCh, BCm = sqb[:, 0:W768], sqb[:, W768:2 * W768]
    dpos = qc
    hid = big[:, 0:4 * B * T].rearrange("p (t n) -> p t n", t=4)
    pooledT = sb("pooledT", [128, B])
    g8 = sb("g8", [8, 8]); m8 = sb("m8", [8, 1]); c8 = sb("c8", [8, 8]); t64 = sb("t64", [8, 8, 8]); e64 = sb("e64", [8, 8, 8])
    r8 = sb("r8", [8, 8]); cT = sb("cT", [128, 8]); cexp = sb("cexp", [128, 4, B])
    aff = sb("aff", [128, B, E1]); am = sb("am", [128, B])
    hidE = [big[:, i * NI * B * T:(i + 1) * NI * B * T].rearrange("p (i n) -> p i n", i=NI) for i in range(2)]
    Wg6 = V2full[:, 0:E1 * IW].rearrange("p (e n) -> p e n", e=E1)
    Wu6 = V2full[:, E1 * IW:2 * E1 * IW].rearrange("p (e n) -> p e n", e=E1)
    Wd6 = big[:, 2 * NI * B * T:2 * NI * B * T + E1 * NI * D].rearrange("p (e n) -> p e n", e=E1 * NI)
    silu6 = [kM2flat[:, i * 512:(i + 1) * 512] for i in range(4)]

    block = ctx.enter_context(nc.Block())

    @block.sync
    def _(sp):
        load(sp, "x0", "ln1", "a1")
        sp.wait_ge(event("upb_zero"), 1)
        load(sp, "l2", "l3", "l4", "l5", "ssm", "bc4", "g6")
        sp.wait_ge(dring.full, dring.index["dl.1"] + 1)
        sp.dma_start(Wg6, a["L1_ffn_Wg"].rearrange("e d n -> d e n")).then_inc(experts_loaded, 16)
        sp.dma_start(Wu6, a["L1_ffn_Wu"].rearrange("e d n -> d e n")).then_inc(experts_loaded, 16)
        sp.dma_start(Wd6, a["L1_ffn_Wd"].rearrange("e (i p) d -> p (e i) d", p=128)).then_inc(experts_loaded, 16)
        for c in range(2):
            sp.wait_ge(event("out_ready"), c + 1)
            sp.dma_start(out.rearrange("b t d -> t b d")[:, c * HB:(c + 1) * HB, :],
                         X[0][:, c * HB:(c + 1) * HB, :]).then_inc(stored, 16)
        sp.wait_ge(stored, 32)

    @block.gpsimd
    def _(pool):
        P_ = nc.gpsimd

        def step(ins):
            pool.wait_ge(pool_step.sem, pool_step.then(ins))

        def affine(t, op, pattern, multiplier=1):
            return P_.affine_select(out=t, in_=t, compare_op=op, fill=1.0, base=0, pattern=pattern,
                                    channel_multiplier=multiplier)

        P_.memset(ident[:], 0.0)
        P_.memset(neg_half[:], -0.5)
        P_.memset(half_bh[:], -0.5)
        P_.memset(upb3[:], 0.0).then_inc(event("upb_zero"), 1)
        step(P_.memset(eps_col[:], EPS))
        affine(ident[:], ALU.not_equal, [[-1, 128]]).then_inc(const_ready, 1)
        pool.wait_ge(const_ready, 1)
        P_.memset(identb[:], 0.0)
        P_.memset(before[:], 0.0)
        P_.memset(after[:], 0.0)
        P_.memset(part_pick[:], 0.0)
        P_.memset(earlier[:], 0.0)
        step(P_.memset(spread8[:], 1.0))
        affine(identb[:], ALU.not_equal, [[-1, 128]])
        affine(before[:], ALU.is_ge, [[1, 128]], -1)
        affine(after[:], ALU.is_ge, [[-1, 128]])
        affine(earlier[:], ALU.is_ge, [[-1, 8], [1, 8]], 0)
        def value_ones(*values):
            for v in values:
                ins = P_.memset(v[:, :, :, HD:VW], 0.0)
            step(ins)
            for v in values:
                ins = P_.memset(v[:, :, :, HD:HD + 1], 1.0)
            ins.then_inc(event("v_ones"), 1)

        powers = Count(ln_rstd)

        def rstds():
            for c in range(2):
                pool.wait_ge(ln_var, powers.n + 1)
                h = slice(c * HB, (c + 1) * HB)
                powers.then(P_.tensor_tensor(out=rstd[:, h], in0=ve[:, h], in1=neg_half[:], op=ALU.pow))

        def attention_pool(at, query_jobs, meanwhile={}, later=None):
            def queries(b):
                aring.wait_copied(pool, query_jobs[b // HB])
                if b >= 2:
                    pool.wait_ge(at.scores_ready, G * (b - 1))
                P_.tensor_tensor(out=qG[:, b % 2], in0=qT[:, b, :].rearrange("p (o t) -> p o t", o=1).to_broadcast([128, G, T]),
                                 in1=groupmask[:].rearrange("p (g o) -> p g o", o=1).to_broadcast([128, G, T]), op=ALU.mult)\
                    .then_inc(at.queries_ready, 1)

            ahead = 6
            for b in range(ahead):
                queries(b)
                if b in meanwhile:
                    meanwhile[b]()
            for b in range(B):
                pool.wait_ge(at.eps_ready, b + 1)
                P_.tensor_tensor(out=rstd[:, b:b + 1], in0=ve[:, b:b + 1], in1=neg_half[:, 0:1], op=ALU.pow)\
                    .then_inc(at.rstd_ready, 1)
                if b + ahead < B:
                    queries(b + ahead)
                if later:
                    later()

        def wide(bias):
            return bias[:].rearrange("p (o n) -> p o n", o=1).to_broadcast([128, B, D])

        rstds()
        P_.iota(colnum[:], pattern=[[1, 128]], base=0, channel_multiplier=0, allow_small_or_imprecise_dtypes=True)
        P_.iota(slot_base[:], pattern=[[0, 1]], base=TS, channel_multiplier=1, allow_small_or_imprecise_dtypes=True)
        P_.memset(xpT[:, :, 0:DC - 1], 0.0)
        P_.memset(cT[:], 0.0)
        P_.tensor_tensor(out=spread8[:].rearrange("p (e c) -> p e c", e=E0), in0=spread8[:].rearrange("p (e c) -> p e c", e=E0),
                         in1=ident[0:E0, 0:E0].rearrange("p (e o) -> p e o", o=1).to_broadcast([E0, E0, BN]), op=ALU.mult)
        for k in range(3):
            step(affine(part_pick[32 * k:32 * k + 32, :], ALU.not_equal, [[-1, 32]]))
        value_ones(V1)
        value_ones(V2)

        def key_squares():
            dring.wait_copied(pool, "kv.3")
            P_.tensor_tensor(out=sq[0:NC], in0=qc[0:NC], in1=qc[0:NC], op=ALU.mult).then_inc(event("k_sq"), 1)

        k_parts = iter(K_PARTS)

        def key_rstds():
            if (part := next(k_parts, None)) is None:
                return
            n = slice(*part)
            pool.wait_ge(event("k_ss"), 2)
            P_.tensor_tensor(out=hr1[0:NC, n], in0=hvar[0:NC, n], in1=half_bh[0:NC, 0:n.stop - n.start], op=ALU.pow)\
                .then_inc(event("k_rstd"), 1)

        def residual1():
            loaded(pool, "x0", "x1", "a1")
            step(P_.tensor_tensor(out=XB[:], in0=X[0][:], in1=X[0][:], op=ALU.add))
            P_.tensor_tensor(out=XB[:], in0=XB[:], in1=wide(bo1), op=ALU.add).then_inc(at1.xb_ready, 1)

        def residual2():
            loaded(pool, "l2")
            P_.tensor_tensor(out=XB[:], in0=X[1][:], in1=wide(bp2), op=ALU.add).then_inc(at2.xb_ready, 1)

        pool.wait_ge(event("groupmask"), 1)
        attention_pool(at1, ("q1.0", "q1.1"), {1: key_squares, 2: residual1, 3: key_rstds, 4: key_rstds, 5: key_rstds},
                       key_rstds)
        dring.wait_copied(pool, "q2.0")
        pool.wait_ge(aring.full, aring.index["k2.1"] + 1)
        P_.tensor_tensor(out=sq[:, 0:HB], in0=qc[:, 0:HB], in1=qc[:, 0:HB], op=ALU.mult).then_inc(event("q_sq"), 1)
        pool.wait_ge(at1.x_ready, B)
        attention_pool(at2, ("q2T.0", "q2T.1"), {1: residual2})
        loaded(pool, "ssm")
        for j in range(DC):
            P_.tensor_tensor(out=convin[:, j, :], in0=inw4[:, 0:DIN], in1=convw[:, :, j], op=ALU.mult)
        for k in range(3):
            P_.tensor_copy(xprojBC[:, :, 2 * DS * k:2 * DS * (k + 1)], xproj[:, :, DTR:])
        for h in range(NH):
            ins = P_.tensor_scalar(out=diagD[:, h, :], in0=ident[:], scalar1=Dp[:, h:h + 1], scalar2=None,
                                   op0=ALU.mult)
        ins.then_inc(event("ssm_weights"), 1)
        for c in range(2):
            h = slice(c * HB, (c + 1) * HB)
            pool.wait_ge(event("ve4_ready"), c + 1)
            P_.tensor_tensor(out=rstd4[:, h], in0=ve4[:, h], in1=neg_half[:], op=ALU.pow).then_inc(event("rstd4_ready"), 1)
        for c in range(2):
            h = slice(c * HB, (c + 1) * HB)
            P_.tensor_tensor(out=rstd[:, h], in0=ve[:, h], in1=neg_half[:], op=ALU.pow).then_inc(event("rstd3_ready"), 1)
        pool.wait_ge(event("equal_scores"), 1)
        P_.tensor_tensor(out=eq, in0=eq, in1=before[:].rearrange("p (o t) -> p o t", o=1).to_broadcast([128, B, T]),
                         op=ALU.mult).then_inc(event("equal_earlier"), 1)
        value_ones(V5[:])
        aring.wait_copied(pool, "qa")
        P_.tensor_tensor(out=qGa, in0=qTa.rearrange("p (o b) k -> p o b k", o=1).to_broadcast([128, G, B, KSEL]),
                         in1=groupmask[:].rearrange("p (g o q) -> p g o q", o=1, q=1).to_broadcast([128, G, B, KSEL]),
                         op=ALU.mult).then_inc(event("qa_copies"), 1)
        for n in range(NH * DS - 1):
            s = n // NH
            pool.wait_ge(event("c_copied"), s + 1)
            pool.wait_ge(event("h_ready"), n + 1)
            if n >= NHC:
                pool.wait_ge(event("hC_used"), n - NHC + 1)
            P_.tensor_tensor(out=hC[n % NHC], in0=hst[n % NHS], in1=Csb[s % 2], op=ALU.mult)\
                .then_inc(event("hC_ready"), 1)
        rstds()
        attention_pool(at5, ("q5.0", "q5.1"))
        rstds()

    @block.scalar
    def _(act):
        A_ = nc.scalar.activation

        def step(ins):
            act.wait_ge(act_step.sem, act_step.then(ins))

        def copy_out(name, dst, view, func=ACT.Identity, **kw):
            A_(dst, view(aring.take(act, name)), func, **kw).then_inc(aring.copied, 1)

        def masked(name, dst, view, scale, shift):
            i = aring.take(act, name)
            for j in range(J):
                ins = A_(dst(j), view(i), ACT.Identity, scale=scale[:, j:j + 1],
                         **({"bias": shift[:, j:j + 1]} if shift is not None else {}))
            ins.then_inc(aring.copied, 1)

        def bank_full(i):
            return PS[:, i, :]

        def bank_ctx(i):
            return PS[:, i, 0:HB * NC].rearrange("p (b n) -> p b n", b=HB)

        def half(t, c):
            return t[:, c * HB:(c + 1) * HB, :]

        def attention_scalar(at, between):
            nk = at.nk
            for s in range(-1, NU + 16):
                if 1 <= s <= NU:
                    u = s - 1
                    act.wait_ge(at.probsT_ready, u + 1)
                    if u >= 3:
                        act.wait_ge(at.pv_done, u - 2)
                    A_(PT[0:nk, u % 3, :, :], bank4(3 + u % 2, nk), ACT.Copy).then_inc(at.probsT_copied, 1)
                if s + 1 < NU:
                    u = s + 1
                    act.wait_ge(at.shifted, u + 1)
                    A_(Eb[:, u % 3, :, 0:nk], Eb[:, u % 3, :, 0:nk], ACT.Exp, scale=at.scale).then_inc(at.exp_ready, 1)
                if s >= 6 and (s - 6) % G == 0 and (s - 6) // G < B:
                    b = (s - 6) // G
                    act.wait_ge(at.pv_done, G * b + G)
                    if b:
                        act.wait_ge(at.out_ready, b)
                    A_(outT[:], bank4(5 + b % 2), ACT.Copy).then_inc(at.outT_copied, 1)
                if s >= 12 and (s - 12) % G == 0 and (s - 12) // G < B:
                    b = (s - 12) // G
                    act.wait_ge(at.normedT_ready, b + 1)
                    if b >= 2:
                        act.wait_ge(at.proj_ready, b - 1)
                    A_(oNT[:, b % 2, :], PS[:, 7, 0:128], ACT.Copy).then_inc(at.normedT_copied, 1)
                if s in between:
                    between[s]()

        tables = iter(range(8))

        def table(func):
            k = next(tables)
            A_(table_out[:, k:k + 1], eps_col[:], func)

        load(act, "x1", "ctx", "kv2")
        for c in range(2):
            copy_out(f"ctxT.{c}", half(ctxT, c), bank_ctx)
        loaded(act, "ln1")
        for c in range(2):
            copy_out(f"x0T.{c}", half(xT, c), bank4, scale=gamma1[:], bias=beta1[:])
        loaded(act, "a1")
        act.wait_ge(event("small1"), 1)
        for c in range(2):
            copy_out(f"q1.{c}", half(qT, c), bank4, bias=bqk1[:, 0:1])
            masked(f"k1.{c}", lambda j: kM1[:, j, c * HB:(c + 1) * HB, :], bank4, headmask, mb1)
        table(ACT.Exp)

        def x1_half():
            copy_out("x1T.0", half(xT, 0), bank4)
            copy_out("down3T", down3T[:], bank_full)

        def mixture_weights():
            copy_out("up3T", up3T[:], bank4)
            copy_out("gate3T", gate3T[:], lambda i: PS[:, i, 0:E0])

        attention_scalar(at1, {NU + 5: x1_half, NU + 8: mixture_weights})

        copy_out("x1T.1", half(xT, 1), bank4)
        act.wait_ge(event("small2"), 1)
        def key2_copies(c):
            masked(f"k2.{c}", lambda j: kM2[:, j, c * HB:(c + 1) * HB, :], bank_ctx, sc2, sh2)

        key2_copies(0)
        table(ACT.Sqrt)
        act.wait_ge(event("q_ss"), 1)
        A_(hr0[:], hss[:], ACT.Sqrt, scale=1.0 / HD, bias=eps_col[:]).then_inc(event("q_std"), 1)
        table(ACT.Exp)
        key2_copies(1)
        for c in range(2):
            copy_out(f"q2T.{c}", half(qT, c), bank4, scale=gb2[:, 0:1], bias=gb2[:, 1:2])
        attention_scalar(at2, {NU + 5: lambda: copy_out("x2T.0", half(xT, 0), bank4)})

        dring.wait_copied(act, "logits8")
        A_(g8[:], g8[:], ACT.Exp).then_inc(event("gate3_exp"), 1)
        for c in range(2):
            for t in range(4):
                copy_out(f"hid.{t}.{c}", hid[:, t, c * 512:(c + 1) * 512], bank_full, ACT.Gelu, bias=downb3[:, t:t + 1])

        for c in range(2):
            copy_out(f"xnT.{c}", half(xT, c), bank4, scale=lnwb4[:, 0:1], bias=lnwb4[:, 1:2])
        for c in range(2):
            copy_out(f"router.{c}", half(hrT, c), lambda i: bank4(i, D // 2), ACT.Gelu_apprx_tanh, bias=rb1[:])
        for c in range(2):
            copy_out(f"srow.{c}", half(Srow, c), bank4, bias=rb2[:])
        copy_out("W5T", W5T[:], bank4)
        copy_out("xprojT", xprojT[:], lambda i: PS[0:DTR, i, 0:NH * 128].rearrange("p (h n) -> p h n", h=NH))
        for h in range(NH):
            copy_out(f"Wdt.{h}", Wdt[:, h, :], lambda i: PS[:, i, 0:DIN])
        for c in range(2):
            masked(f"k5.{c}", lambda j: kM5[:, j, c * HB:(c + 1) * HB, :], bank_ctx, headmask, None)
        for c in range(2):
            copy_out(f"v5.{c}", V5[:, c * HB:(c + 1) * HB, :, 0:HD],
                     lambda i: bank4(i, NC).rearrange("p b (h d) -> p b h d", h=H))
        for c in range(2):
            copy_out(f"xpT.{c}", xpT[:, c * HB:(c + 1) * HB, DC - 1:], bank4, scale=lnwb4[:, 0:1], bias=lnwb4[:, 1:2])
        copy_out("qa", qTa, lambda i: PS[:, i, 0:B * KSEL].rearrange("p (b k) -> p b k", b=B), bias=bqk4[:, 0:1])
        act.wait_ge(event("small4"), 1)
        masked("ka", lambda j: kMa[:, j, :, :], lambda i: PS[:, i, 0:B * KSEL].rearrange("p (b k) -> p b k", b=B),
               headmask, mb4)
        for c in range(2):
            copy_out(f"permT.{c}", half(PermT, c), bank4)
        W384 = HB * TS

        def conv_silu(h, c):
            copy_out(f"conv.{h}.{c}", xc[:, h, c * W384:(c + 1) * W384], lambda i: PS[:, i, 0:W384], ACT.Silu,
                     bias=convb[:, h:h + 1])

        conv_silu(0, 0)
        act.wait_ge(event("pa_shifted"), 1)
        A_(Pa, Pa, ACT.Exp, scale=1 / math.sqrt(HD)).then_inc(event("pa_exp"), 1)
        loaded(act, "ssm")
        A_(Aneg[:], Alog[:], ACT.Exp).then_inc(event("a_exp"), 1)
        conv_silu(0, 1)
        for c in range(2):
            conv_silu(1, c)
        for h in range(NH):
            for c in range(2):
                i = aring.take(act, f"delta.{h}.{c}")
                w = slice(c * W384, (c + 1) * W384)
                A_(sp_abs[:, h, w], PS[:, i, 0:W384], ACT.Abs, bias=dtb[:, h:h + 1])
                A_(sp_relu[:, h, w], PS[:, i, 0:W384], ACT.Relu, bias=dtb[:, h:h + 1]).then_inc(aring.copied, 1)
            act.wait_ge(aring.copied, aring.emptied)
            A_(sp_exp[:, h, :], sp_abs[:, h, :], ACT.Exp, scale=-1.0).then_inc(event("sp_exp"), 1)
        for h in range(NH):
            act.wait_ge(event("sp_exp"), h + 1)
            A_(sp_log[:, h, :], sp_exp[:, h, :], ACT.Ln, bias=1.0).then_inc(event("sp_log"), 1)
        table(ACT.Exp)
        for h in range(NH):
            for c in range(2):
                copy_out(f"z.{h}.{c}", zs[:, h, c * W384:(c + 1) * W384], lambda i: PS[:, i, 0:W384], ACT.Copy)

        def decay(n):
            s, h = n // NH, n % NH
            if n < NH:
                act.wait_ge(event("delta_ready"), n + 1)
            if n >= NDA:
                act.wait_ge(event("h_ready"), n - NDA + 1)
            A_(dA[n % NDA].rearrange("p (b t) -> p b t", b=B)[:, :, 1:TS],
               delta[:, h, :].rearrange("p (b t) -> p b t", b=B)[:, :, 1:TS],
               ACT.Exp, scale=Aneg[:, h, s:s + 1]).then_inc(event("dA_ready"), 1)

        def copy_spread(s, ready, copied, bank, dst):
            act.wait_ge(event(ready), s + 1)
            A_(dst[s % 2].rearrange("p (c n) -> p c n", c=2), PS[:, bank:bank + 2, 0:W384], ACT.Copy)\
                .then_inc(event(copied), 1)

        for s in range(DS):
            if s >= 2:
                act.wait_ge(event("dBu_ready"), NH * (s - 1))
            copy_spread(s, "b_ready", "b_copied", 4, Bsb)
            if s == 0:
                for h in range(NH):
                    decay(h)
            if s >= 2:
                act.wait_ge(event("hC_ready"), NH * (s - 1))
            copy_spread(s, "c_ready", "c_copied", 6, Csb)
            if s:
                for h in range(NH):
                    decay(NH * s + h)
        A_(zs[:], zs[:], ACT.Silu).then_inc(event("z_ready"), 1)

        for c in range(2):
            copy_out(f"x4T.{c}", half(xT, c), bank4)
        for c in range(2):
            copy_out(f"q5.{c}", half(qT, c), bank4)
        attention_scalar(at5, {NU + 5: lambda: copy_out("x5T.0", half(xT, 0), bank4)})

        for k in range(E1 * NI * 2):
            if k == NI * 2:
                dring.wait_copied(act, "logits6")
                A_(aff[:], aff[:], ACT.Exp).then_inc(event("aff_exp"), 1)
            act.wait_ge(event("gate_ready"), k + 1)
            if k >= 4:
                act.wait_ge(event("hidden_ready"), k - 3)
            A_(silu6[k % 4], PS[:, k % 2, :], ACT.Silu).then_inc(event("silu_ready"), 1)

    @block.vector
    def _(dve):
        V_ = nc.vector

        def step(ins):
            dve.wait_ge(dve_step.sem, dve_step.then(ins))

        def take(name):
            return dring.take(dve, name)

        def bank_full(i, p=128, n=512):
            return PS[0:p, i, 0:n]

        def half(t, c):
            return t[:, c * HB:(c + 1) * HB, :]

        var_sent = Count(ln_var)

        def norm_stats(src, c):
            for b in range(c * HB, (c + 1) * HB):
                ins = V_.bn_stats(st[:, b, :], src[:, b, :])
            step(ins)
            for b in range(c * HB, (c + 1) * HB):
                ins = V_.bn_aggr(mv[:, b, :], st[:, b, :])
            step(ins)
            var_sent.then(V_.tensor_scalar(ve[:, c * HB:(c + 1) * HB], mv[:, c * HB:(c + 1) * HB, 1], EPS, None, ALU.add))

        def norm_apply(src, dst, done, c):
            norm_apply.taken += 1
            dve.wait_ge(ln_rstd, norm_apply.taken)
            for b in range(c * HB, (c + 1) * HB):
                ins = V_.tensor_scalar(dst[:, b, :], src[:, b, :], mv[:, b, 0:1], rstd[:, b:b + 1],
                                       ALU.subtract, ALU.mult)
            ins.then_inc(event(done), 1)

        norm_apply.taken = 0

        def centre(W, k):
            w = W.rearrange("p (h d) -> p h d", h=H)
            step(V_.tensor_reduce(wmean[:, k, :], w, axis=AX.X, op=ALU.add))
            step(V_.tensor_scalar(wmean[:, k, :], wmean[:, k, :], 1.0 / HD, None, ALU.mult))
            return V_.tensor_tensor(w, w, wmean[:, k, :].rearrange("p (h o) -> p h o", o=1).to_broadcast([128, H, HD]),
                                    ALU.subtract)

        def head_sums(rows, squares, sums):
            dve.wait_ge(event(squares), 1)
            V_.tensor_reduce(hss[0:rows], sq[0:rows].rearrange("p b (h d) -> p (b h) d", d=HD), axis=AX.X,
                             op=ALU.add).then_inc(event(sums), 1)
            dve.wait_ge(event(sums), 1)
            V_.tensor_scalar(hvar[0:rows], hss[0:rows], 1.0 / HD, EPS, ALU.mult, ALU.add).then_inc(event(sums), 1)
            dve.wait_ge(event(sums), 2)

        def head_scale(rows, rstds, done):
            V_.tensor_tensor(sq[0:rows].rearrange("p b (h d) -> p (b h) d", d=HD),
                             qc[0:rows].rearrange("p b (h d) -> p (b h) d", d=HD),
                             rstds[0:rows].rearrange("p (n o) -> p n o", o=1).to_broadcast([rows, B * H, HD]),
                             ALU.mult).then_inc(event(done), 1)

        def attention_vector(at, between):
            nk = at.nk

            def scores(u):
                return PS[:, u % 3, 0:J * nk].rearrange("p (j k) -> p j k", j=J)

            for s in range(-1, NU + 21):
                if s + 1 < NU:
                    u = s + 1
                    dve.wait_ge(at.scores_ready, u + 1)
                    if u >= 3:
                        dve.wait_ge(at.shifted, u - 2)
                    V_.tensor_reduce(mx[:, u % 3, :], scores(u), axis=AX.X, op=ALU.max).then_inc(at.max_ready, 1)

                def row_of(lag):
                    b = (s - lag) // G
                    return b if s >= lag and (s - lag) % G == 0 and b < B else None

                if (b := row_of(8)) is not None:
                    dve.wait_ge(at.out_ready, b + 1)
                    if b >= 2:
                        dve.wait_ge(at.normed, b - 1)
                    o = PS[:, 5 + b % 2, :].rearrange("p (h w) -> p h w", h=H)
                    ins = V_.reciprocal(rs[:, b % 2, :].rearrange("p (h o) -> p h o", o=1), o[:, :, HD:HD + 1])
                    if at.masked:
                        step(ins)
                        ins = V_.tensor_scalar(rs[:, b % 2, :], rs[:, b % 2, :], anykey[:], None, ALU.mult)
                    ins.then_inc(at.recip_ready, 1)
                if (b := row_of(9)) is not None:
                    dve.wait_ge(at.recip_ready, b + 1)
                    if b >= 2:
                        dve.wait_ge(at.normedT_ready, b - 1)
                    o = PS[:, 5 + b % 2, :].rearrange("p (h w) -> p h w", h=H)
                    V_.tensor_tensor(oN[:, b % 2, :].rearrange("p (h d) -> p h d", h=H), o[:, :, 0:HD],
                                     rs[:, b % 2, :].rearrange("p (h o) -> p h o", o=1).to_broadcast([128, H, HD]),
                                     ALU.mult).then_inc(at.normed, 1)
                if (b := row_of(15)) is not None:
                    dve.wait_ge(at.proj_ready, b + 1)
                    if b == 0 and not at.masked:
                        dve.wait_ge(at.xb_ready, 1)
                    V_.tensor_tensor(R[:, b, :], at.XB[:, b, :], PS[:, 7, 128:256], ALU.add)\
                        .then_inc(at.residual_ready, 1)
                if (b := row_of(16)) is not None:
                    dve.wait_ge(at.residual_ready, b + 1)
                    V_.bn_stats(st[:, b, :], R[:, b, :]).then_inc(at.stats_ready, 1)
                if (b := row_of(17)) is not None:
                    dve.wait_ge(at.stats_ready, b + 1)
                    V_.bn_aggr(mv[:, b, :], st[:, b, :]).then_inc(at.var_ready, 1)
                if (b := row_of(18)) is not None:
                    dve.wait_ge(at.var_ready, b + 1)
                    V_.tensor_scalar(ve[:, b:b + 1], mv[:, b, 1:2], EPS, None, ALU.add).then_inc(at.eps_ready, 1)
                if (b := row_of(20)) is not None:
                    dve.wait_ge(at.rstd_ready, b + 1)
                    V_.tensor_scalar(at.Xout[:, b, :], R[:, b, :], mv[:, b, 0:1], rstd[:, b:b + 1],
                                     ALU.subtract, ALU.mult).then_inc(at.x_ready, 1)
                if s in between:
                    between[s]()
                if s + 1 < NU:
                    u = s + 1
                    dve.wait_ge(at.max_ready, u + 1)
                    if u >= 3:
                        dve.wait_ge(at.probsT_ready, u - 2)
                    V_.tensor_tensor(Eb[:, u % 3, :, 0:nk], scores(u),
                                     mx[:, u % 3, :].rearrange("p (j o) -> p j o", o=1).to_broadcast([128, J, nk]),
                                     ALU.subtract).then_inc(at.shifted, 1)

        def wide(v, shape):
            return v.rearrange("p (b o) -> p b o", o=1).to_broadcast(shape)

        dve.wait_ge(const_ready, 1)
        step(V_.tensor_reduce(headmask[:], ident[:].rearrange("p (g j d) -> p j g d", g=G, j=J), axis=AX.XY, op=ALU.add))
        V_.tensor_reduce(groupmask[:], ident[:].rearrange("p (g c) -> p g c", g=G), axis=AX.X, op=ALU.add)\
            .then_inc(event("groupmask"), 1)
        loaded(dve, "x0")
        norm_stats(X[0], 0)
        loaded(dve, "kv2")
        centre(Wkv2[:, 0:D], 0).then_inc(event("w2_centred"), 1)
        loaded(dve, "x1")
        norm_stats(X[0], 1)
        for c in range(2):
            norm_apply(X[0], XH, "xh1", c)
        loaded(dve, "a1")
        V_.tensor_scalar(mb1[:], headmask[:], bqk1[:, 1:2], None, ALU.mult).then_inc(event("small1"), 1)
        for p in range(4):
            kv = PS[0:NC, take(f"kv.{p}"), :].rearrange("p (b n) -> p b n", b=2)
            V_.tensor_copy(qc[0:NC, 2 * p:2 * p + 2, :], kv[:, :, 0:D])
            V_.tensor_copy(V2[:, 2 * p:2 * p + 2, :, 0:HD], kv[:, :, D:2 * D].rearrange("p b (h d) -> p b h d", h=H))\
                .then_inc(dring.copied, 1)
        for c in range(2):
            i = take(f"v1.{c}")
            V_.tensor_tensor(V1[:, c * HB:(c + 1) * HB, :, 0:HD],
                             bank4(i).rearrange("p b (h d) -> p b h d", h=H),
                             bv1[:].rearrange("p (o h d) -> p o h d", o=1, h=H).to_broadcast([128, HB, H, HD]),
                             ALU.add).then_inc(dring.copied, 1)

        def weights2():
            loaded(dve, "l2")
            centre(Wq2[:], 1).then_inc(event("w2_centred"), 1)
            step(V_.tensor_reduce(dmask[:], ident[:].rearrange("p (h d) -> p d h", d=HD), axis=AX.X, op=ALU.add))
            step(V_.tensor_tensor(gbpick[:], gbrow2[:], dmask[:].rearrange("p (o d) -> p o d", o=1).to_broadcast([128, 2, HD]),
                                  ALU.mult))
            step(V_.tensor_reduce(gb2[:], gbpick[:], axis=AX.X, op=ALU.add))
            V_.tensor_scalar(sc2[:], headmask[:], gb2[:, 0:1], None, ALU.mult)
            V_.tensor_scalar(sh2[:], headmask[:], gb2[:, 1:2], None, ALU.mult).then_inc(event("small2"), 1)

        def weights5():
            loaded(dve, "l5")
            V_.tensor_scalar(maskneg[:], mask8[:], MASKED, None, ALU.mult)
            step(V_.tensor_reduce(nmasked[:], mask8[:], axis=AX.X, op=ALU.add))
            step(V_.tensor_scalar(anykey[:], nmasked[:], float(NC), None, ALU.is_lt))

        def key_variances():
            head_sums(NC, "k_sq", "k_ss")

        attention_vector(at1, {7: key_variances, 11: weights2, 15: weights5})

        dve.wait_ge(event("k_rstd"), len(K_PARTS))
        head_scale(NC, hr1, "kn_ready")
        dve.wait_ge(event("kn_ready"), 1)
        for c in range(2):
            V_.tensor_copy(half(qc, c), bank4(take(f"q2.{c}"))).then_inc(dring.copied, 1)
        dring.wait_copied(dve, "q2.1")
        dve.wait_ge(aring.full, aring.index["k2.1"] + 1)
        step(V_.tensor_tensor(half(sq, 1), half(qc, 1), half(qc, 1), ALU.mult))
        head_sums(128, "q_sq", "q_ss")
        dve.wait_ge(event("q_std"), 1)
        step(V_.reciprocal(hr0[:], hr0[:]))
        step(V_.tensor_tensor(hr1[:], hr0[:], hr0[:], ALU.mult))
        step(V_.tensor_tensor(hr1[:], hr1[:], hvar[:], ALU.mult))
        step(V_.tensor_scalar(hr1[:], hr1[:], -0.5, 1.5, ALU.mult, ALU.add))
        step(V_.tensor_tensor(hr1[:], hr1[:], hr0[:], ALU.mult))
        head_scale(128, hr1, "qn_ready")
        attention_vector(at2, {})

        for c in range(2):
            if c:
                V_.tensor_copy(half(xT, 1), bank4(take("x2T.1"))).then_inc(dring.copied, 1)
                dve.wait_ge(dring.copied, dring.emptied)
            else:
                aring.wait_copied(dve, "x2T.0")
            V_.tensor_reduce(pooledT[:, c * HB:(c + 1) * HB], half(xT, c), axis=AX.X, op=ALU.add)\
                .then_inc(event("pooled"), 1)
        i = take("logits8")
        step(V_.tensor_reduce(m8[:], PS[0:8, i, 0:8], axis=AX.X, op=ALU.max))
        V_.tensor_scalar(g8[:], PS[0:8, i, 0:8], m8[:], 1.0 / T, ALU.subtract, ALU.mult).then_inc(dring.copied, 1)
        dve.wait_ge(event("gate3_exp"), 1)
        step(V_.tensor_reduce(m8[:], g8[:], axis=AX.X, op=ALU.add))
        step(V_.reciprocal(m8[:], m8[:]))
        step(V_.tensor_scalar(g8[:], g8[:], m8[:], None, ALU.mult))
        other = g8[:].rearrange("p (o f) -> p o f", o=1).to_broadcast([8, 8, 8])
        own = g8[:].rearrange("p (e o) -> p e o", o=1).to_broadcast([8, 8, 8])
        V_.tensor_tensor(t64[:], other, own, ALU.is_gt)
        step(V_.tensor_tensor(e64[:], other, own, ALU.is_equal))
        step(V_.tensor_tensor(e64[:], e64[:], earlier[:], ALU.mult))
        step(V_.tensor_tensor(t64[:], t64[:], e64[:], ALU.add))
        step(V_.tensor_reduce(r8[:], t64[:], axis=AX.X, op=ALU.add))
        step(V_.tensor_scalar(r8[:], r8[:], 2.0, None, ALU.is_lt))
        step(V_.tensor_tensor(c8[:], r8[:], g8[:], ALU.mult))
        step(V_.tensor_reduce(m8[:], c8[:], axis=AX.X, op=ALU.add))
        step(V_.tensor_scalar(m8[:], m8[:], 1e-8, None, ALU.add))
        step(V_.reciprocal(m8[:], m8[:]))
        V_.tensor_scalar(c8[:], c8[:], m8[:], None, ALU.mult).then_inc(event("c8_ready"), 1)
        V_.tensor_copy(cT[0:E0], PS[0:8, take("cT"), 0:8]).then_inc(dring.copied, 1)
        V_.tensor_copy(cexp[:], PS[:, take("cexp"), 0:4 * B].rearrange("p (t b) -> p t b", t=4)).then_inc(dring.copied, 1)
        dve.wait_ge(dring.copied, dring.emptied)
        for c in range(2):
            for t in range(4):
                aring.wait_copied(dve, f"hid.{t}.{c}")
                v = hid[:, t, c * 512:(c + 1) * 512].rearrange("p (b n) -> p b n", b=HB)
                V_.tensor_tensor(v, v, wide(cexp[:, t, c * HB:(c + 1) * HB], [128, HB, T]), ALU.mult)\
                    .then_inc(event("hid_scaled"), 1)
        for c in range(2):
            h = slice(c * HB, (c + 1) * HB)
            V_.tensor_tensor(half(R, c), half(X[0], c), bank4(take(f"up.{c}")), ALU.add).then_inc(dring.copied, 1)
            dve.wait_ge(dring.copied, dring.emptied)
            for b in range(c * HB, (c + 1) * HB):
                ins = V_.bn_stats(st[:, b, :], R[:, b, :])
            step(ins)
            for b in range(c * HB, (c + 1) * HB):
                ins = V_.bn_aggr(mv[:, b, :], st[:, b, :])
            step(ins)
            step(V_.tensor_scalar(ve[:, h], mv[:, h, 1], EPS, None, ALU.add))
            V_.scalar_tensor_tensor(ve4[:, h], ve[:, h], EPS, mv[:, h, 1], ALU.mult, ALU.add).then_inc(event("ve4_ready"), 1)
        for c in range(2):
            dve.wait_ge(event("rstd4_ready"), c + 1)
            for b in range(c * HB, (c + 1) * HB):
                ins = V_.tensor_scalar(XH[:, b, :], R[:, b, :], mv[:, b, 0:1], rstd4[:, b:b + 1], ALU.subtract, ALU.mult)
            ins.then_inc(event("xh4"), 1)
        for c in range(2):
            dve.wait_ge(event("rstd3_ready"), c + 1)
            for b in range(c * HB, (c + 1) * HB):
                V_.tensor_scalar(X[1][:, b, :], R[:, b, :], mv[:, b, 0:1], rstd[:, b:b + 1], ALU.subtract, ALU.mult)

        aring.wait_copied(dve, "srow.1")
        V_.tensor_copy(scol[:], PS[:, take("scol"), 0:B]).then_inc(dring.copied, 1)
        dve.wait_ge(dring.copied, dring.emptied)
        V_.tensor_tensor(eq, Srow, wide(scol[:], [128, B, T]), ALU.is_equal).then_inc(event("equal_scores"), 1)
        step(V_.tensor_tensor(gt, Srow, wide(scol[:], [128, B, T]), ALU.is_gt))
        step(V_.tensor_reduce(rank[:], gt, axis=AX.X, op=ALU.add))
        dve.wait_ge(event("equal_earlier"), 1)
        step(V_.tensor_reduce(ties[:], eq, axis=AX.X, op=ALU.add))
        step(V_.tensor_tensor(rank[:], rank[:], ties[:], ALU.add))
        V_.tensor_scalar(unsel[:], rank[:], float(KSEL), None, ALU.is_ge).then_inc(event("unsel"), 1)
        V_.tensor_scalar(sel[:], rank[:], float(KSEL), None, ALU.is_lt)
        i = take("cumU")
        V_.tensor_copy(cumU[:], PS[:, i, 0:B])
        V_.tensor_scalar(posa[:], PS[:, i, 0:B], -2.0, slot_base[:], ALU.mult, ALU.add).then_inc(dring.copied, 1)
        dve.wait_ge(dring.copied, dring.emptied)
        step(V_.tensor_tensor(posa[:], posa[:], sel[:], ALU.mult))
        step(V_.tensor_tensor(pos[:], cumU[:], posa[:], ALU.add))
        V_.tensor_tensor(Perm, colnum[:].rearrange("p (o t) -> p o t", o=1).to_broadcast([128, B, T]),
                         wide(pos[:], [128, B, T]), ALU.is_equal).then_inc(event("perm"), 1)
        loaded(dve, "l4", "ssm")
        V_.tensor_scalar(mb4[:], headmask[:], bqk4[:, 1:2], None, ALU.mult).then_inc(event("small4"), 1)
        V_.tensor_tensor(va, PS[:, take("va"), 0:256].rearrange("p (b n) -> p b n", b=2),
                         bv4[:].rearrange("p (o n) -> p o n", o=1).to_broadcast([128, 2, D]), ALU.add)\
            .then_inc(dring.copied, 1)
        dve.wait_ge(event("sa_ready"), 1)
        Sa = PS[:, 4:8, 0:256].rearrange("p g (n k) -> p g n k", k=KSEL)
        step(V_.tensor_reduce(mxa[:].rearrange("p (g n) -> p g n", g=G), Sa, axis=AX.X, op=ALU.max))
        for g in range(G):
            ins = V_.tensor_tensor(Pa[:, 8 * g:8 * g + 8, :], Sa[:, g], wide(mxa[:, 8 * g:8 * g + 8], [128, 8, KSEL]),
                                   ALU.subtract)
        ins.then_inc(event("pa_shifted"), 1)
        dve.wait_ge(event("pa_exp"), 1)
        step(V_.tensor_reduce(sma[:], Pa, axis=AX.X, op=ALU.add))
        step(V_.reciprocal(sma[:], sma[:]))
        step(V_.tensor_tensor(Pa, Pa, wide(sma[:], [128, 2 * H, KSEL]), ALU.mult))
        V_.transpose(PaT.rearrange("p n k -> p (n k)"), Pa.rearrange("p n k -> p (n k)")).then_inc(event("paT"), 1)
        W384 = HB * TS
        for c in range(2):
            V_.tensor_copy(BC[:, c * W384:(c + 1) * W384], PS[0:96, take(f"BC.{c}"), 0:W384]).then_inc(dring.copied, 1)
        dve.wait_ge(dring.copied, dring.emptied)
        step(V_.tensor_copy(BCh, BC))
        V_.tensor_copy(BC3[0:32], BCh[0:32])
        step(V_.tensor_tensor(BC, BC, BCh, ALU.subtract))
        step(V_.tensor_copy(BCm, BC))
        V_.tensor_copy(BC3[32:64], BCm[32:64])
        V_.tensor_tensor(BC3[64:96], BC[64:96], BCm[64:96], ALU.subtract).then_inc(event("bc_parts"), 1)
        dve.wait_ge(event("a_exp"), 1)
        V_.tensor_scalar(Aneg[:], Aneg[:], -1.0, None, ALU.mult)
        for h in range(NH):
            dve.wait_ge(event("sp_exp"), h + 1)
            step(V_.tensor_scalar(sp_abs[:, h, :], sp_exp[:, h, :], 1.0, -1.0, ALU.add, ALU.add))
            step(V_.tensor_tensor(sp_abs[:, h, :], sp_exp[:, h, :], sp_abs[:, h, :], ALU.subtract))
            step(V_.tensor_tensor(sp_relu[:, h, :], sp_abs[:, h, :], sp_relu[:, h, :], ALU.add))
            if h == 0:
                dve.wait_ge(event("oa_ready"), 1)
                for n in range(2):
                    ins = V_.tensor_tensor(oa_heads[:, 16 * n:16 * n + 16, :].rearrange("p (c j) q -> p c j q", c=4),
                                           PS[:, 4:8, n * 128:(n + 1) * 128].rearrange("p c (j q) -> p c j q", j=J),
                                           headmask[:].rearrange("p (a j b) -> p a j b", a=1, b=1).to_broadcast([128, 4, J, KSEL]),
                                           ALU.mult)
                ins.then_inc(event("oa_masked"), 1)
        for i in range(NDA):
            V_.memset(dA[i].rearrange("p (b t) -> p b t", b=B)[:, :, 0:1], 0.0)
        for h in range(NH):
            dve.wait_ge(event("sp_log"), h + 1)
            V_.tensor_tensor(delta[:, h, :], sp_log[:, h, :], sp_relu[:, h, :], ALU.add).then_inc(event("delta_ready"), 1)
        for h in range(NH):
            dve.wait_ge(event("delta_ready"), h + 1)
            V_.tensor_tensor(du[:, h, :], delta[:, h, :], xc[:, h, :], ALU.mult).then_inc(event("du_ready"), 1)
        def scan(m):
            dve.wait_ge(event("dBu_ready"), m + 1)
            dve.wait_ge(event("dA_ready"), m + 1)
            if m >= NHS:
                dve.wait_ge(event("hC_ready"), m - NHS + 1)
            V_.tensor_tensor_scan(hst[m % NHS], dA[m % NDA], dBu[m % NDB], 0.0, ALU.mult, ALU.add)\
                .then_inc(event("h_ready"), 1)

        for n in range(NH * DS):
            s, h = n // NH, n % NH
            dve.wait_ge(event("b_copied"), s + 1)
            if n < NH:
                dve.wait_ge(event("du_ready"), n + 1)
            if n >= NDB:
                dve.wait_ge(event("h_ready"), n - NDB + 1)
            V_.tensor_tensor(dBu[n % NDB], du[:, h, :], Bsb[s % 2], ALU.mult).then_inc(event("dBu_ready"), 1)
            if n >= 1:
                scan(n - 1)
        scan(NH * DS - 1)
        n = NH * DS - 1
        dve.wait_ge(event("c_copied"), DS)
        dve.wait_ge(event("h_ready"), n + 1)
        dve.wait_ge(event("hC_used"), n - NHC + 1)
        V_.tensor_tensor(hC[n % NHC], hst[n % NHS], Csb[(DS - 1) % 2], ALU.mult).then_inc(event("last_hC_ready"), 1)
        V_.tensor_reduce(oaT.rearrange("p n (c q) -> p (n c) q", c=4), oa_heads.rearrange("p (b j) q -> p b q j", j=J),
                         axis=AX.X, op=ALU.add).then_inc(event("oaT_ready"), 1)
        dve.wait_ge(event("z_ready"), 1)
        for h in range(NH):
            dve.wait_ge(event("hC_used"), NH * (DS - 1) + h + 1)
            V_.tensor_tensor(xc[:, h, :].rearrange("p (c n) -> p c n", c=2), PS[:, 2 * h:2 * h + 2, 0:W384],
                             zs[:, h, :].rearrange("p (c n) -> p c n", c=2), ALU.mult).then_inc(event("y_gated"), 1)
        loaded(dve, "bc4")
        for c in range(2):
            V_.tensor_tensor(dpos[TS:T, c * HB:(c + 1) * HB, :],
                             PS[TS:T, take(f"dposA.{c}"), :].rearrange("p (b n) -> p b n", b=HB),
                             posbias[TS:T, :].rearrange("p (o n) -> p o n", o=1).to_broadcast([KSEL, HB, D]),
                             ALU.add).then_inc(dring.copied, 1)
        for c in range(2):
            V_.tensor_copy(dpos[0:TS, c * HB:(c + 1) * HB, :],
                           PS[0:TS, take(f"dposS.{c}"), :].rearrange("p (b n) -> p b n", b=HB)).then_inc(dring.copied, 1)
        for c in range(2):
            i = take(f"dl.{c}")
            V_.scalar_tensor_tensor(half(R, c), half(X[1], c), 2.0, bank4(i), ALU.mult, ALU.add).then_inc(dring.copied, 1)
            dve.wait_ge(dring.copied, dring.emptied)
            norm_stats(R, c)
        for c in range(2):
            norm_apply(R, X[0], "x4", c)
        dve.wait_ge(event("x4"), 2)
        attention_vector(at5, {})

        V_.tensor_copy(half(xT, 1), bank4(take("x5T.1"))).then_inc(dring.copied, 1)
        dve.wait_ge(at5.x_ready, B)
        for e in range(E1 + 1):
            if e < E1:
                for k in range(NI * 2):
                    n = e * NI * 2 + k
                    c, i = k // NI, k % NI
                    dve.wait_ge(event("up_ready"), n + 1)
                    dve.wait_ge(event("silu_ready"), n + 1)
                    if e >= 2:
                        dve.wait_ge(event("down_ready"), 2 * (e - 1))
                    V_.tensor_tensor(hidE[e % 2][:, i, c * 512:(c + 1) * 512], silu6[n % 4], PS[:, 2 + n % 2, :],
                                     ALU.mult).then_inc(event("hidden_ready"), 1)
            if e == 0:
                i = take("logits6")
                lg = PS[:, i, 0:B * E1].rearrange("p (b e) -> p b e", b=B)
                step(V_.tensor_reduce(am[:], lg, axis=AX.X, op=ALU.max))
                V_.tensor_tensor(aff[:], lg, wide(am[:], [128, B, E1]), ALU.subtract).then_inc(dring.copied, 1)
                dve.wait_ge(dring.copied, dring.emptied)
                dve.wait_ge(event("aff_exp"), 1)
                step(V_.tensor_reduce(am[:], aff[:], axis=AX.X, op=ALU.add))
                step(V_.reciprocal(am[:], am[:]))
                step(V_.tensor_tensor(aff[:], aff[:], wide(am[:], [128, B, E1]), ALU.mult))
            if e >= 1:
                p = e - 1
                for c in range(2):
                    dve.wait_ge(event("down_ready"), 2 * p + c + 1)
                    for b4 in range(HB):
                        b = c * HB + b4
                        if p >= 1:
                            dve.wait_ge(event("summed"), B * (p - 1) + b + 1)
                        V_.scalar_tensor_tensor(R[:, b, :], PS[:, 4 + (2 * p + c) % 4, b4 * D:(b4 + 1) * D],
                                                aff[:, b, p:p + 1], (R if p else X[1])[:, b, :],
                                                ALU.mult, ALU.add).then_inc(event("summed"), 1)
                    if p == E1 - 1:
                        dve.wait_ge(event("summed"), B * p + HB * (c + 1))
                        norm_stats(R, c)
        for c in range(2):
            norm_apply(R, X[0], "out_ready", c)

    @block.tensor
    def _(pe):
        M_ = nc.tensor.matmul

        def fill(ring, name):
            return ring.fill(pe, name)

        def half(t, c):
            return t[:, c * HB:(c + 1) * HB, :]

        def flat(ap):
            return ap.rearrange("p b t -> p (b t)")

        def transposes(name, srcs, rows, cols, ring=aring):
            i = fill(ring, name)
            for k, src in enumerate(srcs):
                ins = nc.tensor.transpose(PS[0:cols, i, k * rows:(k + 1) * rows], src, ident[0:rows, 0:rows])
            ins.then_inc(ring.full, 1)

        def product(ring, name, lhsT, rhs, rows=128, cols=512):
            i = fill(ring, name)
            M_(PS[0:rows, i, 0:cols], lhsT, rhs, start=True, stop=True).then_inc(ring.full, 1)

        def row_products(ring, name, lhsTs, rhs, rows=128, width=D):
            i = fill(ring, name)
            for k, lhsT in enumerate(lhsTs):
                ins = M_(PS[0:rows, i, k * width:(k + 1) * width], lhsT, rhs, start=True, stop=True)
            ins.then_inc(ring.full, 1)

        def transposed_half(stage, c, X_, ready, per_half, ring=aring):
            pe.wait_ge(ready, per_half * (c + 1))
            transposes(f"{stage}.{c}", [X_[:, b, :] for b in range(c * HB, (c + 1) * HB)], 128, 128, ring)

        def x_transposed(stage, X_, ready, per_half):
            for c in range(2):
                transposed_half(stage, c, X_, ready, per_half)

        def attention_tensor(at, between):
            nk = at.nk
            aring.drain(pe)
            dring.drain(pe)
            for s in range(-2, NU + 16):
                if s + 2 < NU:
                    u = s + 2
                    b, g = u // G, u % G
                    if u >= 3:
                        pe.wait_ge(at.shifted, u - 2)
                    if g == 0:
                        pe.wait_ge(at.queries_ready, b + 1)
                    dst = PS[:, u % 3, 0:J * nk].rearrange("p (j k) -> p j k", j=J)
                    ins = M_(dst, qG[:, b % 2, g, :], at.kM[:, :, b, :], start=True, stop=not at.masked)
                    if at.masked:
                        ins = M_(dst, identb[:], maskneg[:].rearrange("p (o k) -> p o k", o=1).to_broadcast([128, J, nk]),
                                 start=False, stop=True)
                    ins.then_inc(at.scores_ready, 1)
                def row_of(lag):
                    b = (s - lag) // G
                    return b if s >= lag and (s - lag) % G == 0 and b < B else None

                if (b := row_of(7)) is not None:
                    pe.wait_ge(at.outT_copied, b + 1)
                    for g in range(G):
                        ins = nc.tensor.transpose(PS[:, 5 + b % 2, 128 * g:128 * g + 128], outT[:, g, :], ident[:])
                    ins.then_inc(at.out_ready, 1)
                if (b := row_of(11)) is not None:
                    pe.wait_ge(at.normed, b + 1)
                    if b:
                        pe.wait_ge(at.residual_ready, b)
                    nc.tensor.transpose(PS[:, 7, 0:128], oN[:, b % 2, :], ident[:]).then_inc(at.normedT_ready, 1)
                if (b := row_of(13)) is not None:
                    pe.wait_ge(at.normedT_copied, b + 1)
                    M_(PS[:, 7, 128:256], oNT[:, b % 2, :], at.Wo, start=True, stop=True).then_inc(at.proj_ready, 1)
                if 2 <= s < NU + 2:
                    u = s - 2
                    b, g = u // G, u % G
                    pe.wait_ge(at.probsT_copied, u + 1)
                    if g == 0 and b >= 2:
                        pe.wait_ge(at.normed, b - 1)
                    for j in range(J):
                        ins = M_(PS[32 * j:32 * j + 32, 5 + b % 2, 128 * g:128 * g + 128], at.V[0:nk, b, J * g + j, :],
                                 PT[0:nk, u % 3, j, :], start=True, stop=True)
                    ins.then_inc(at.pv_done, 1)
                if 0 <= s < NU:
                    pe.wait_ge(at.exp_ready, s + 1)
                    if s >= 2:
                        pe.wait_ge(at.probsT_copied, s - 1)
                    for j in range(J):
                        ins = nc.tensor.transpose(PS[0:nk, 3 + s % 2, 128 * j:128 * j + 128], Eb[:, s % 3, j, 0:nk], ident[:])
                    ins.then_inc(at.probsT_ready, 1)
                if s in between:
                    pe.wait_ge(at.shifted, NU)
                    pe.wait_ge(at.probsT_copied, NU)
                    between[s]()
            pe.wait_ge(at.residual_ready, B)

        pe.wait_ge(const_ready, 1)
        loaded(pe, "ctx")
        for c in range(2):
            transposes(f"ctxT.{c}", [ctxN[0:NC, b, :] for b in range(c * HB, (c + 1) * HB)], NC, 128)
        aring.wait_copied(pe, "ctxT.1")
        pe.wait_ge(event("w2_centred"), 1)
        for p in range(4):
            row_products(dring, f"kv.{p}", [ctxT[:, b, :] for b in (2 * p, 2 * p + 1)], Wkv2[:], NC, 2 * D)
        for c in range(2):
            pe.wait_ge(event("xh1"), c + 1)
            transposes(f"x0T.{c}", [XH[:, b, :] for b in range(c * HB, (c + 1) * HB)], 128, 128)
        loaded(pe, "a1")
        for c in range(2):
            aring.wait_copied(pe, f"x0T.{c}")
            product(aring, f"q1.{c}", Wqkv1[:, 0:D], half(xT, c))
            product(aring, f"k1.{c}", Wqkv1[:, D:2 * D], half(xT, c))
            row_products(dring, f"v1.{c}", [xT[:, b, :] for b in range(c * HB, (c + 1) * HB)], Wqkv1[:, 2 * D:3 * D])
        pe.wait_ge(event("v_ones"), 1)

        def x1_half():
            transposed_half("x1T", 0, X[1], at1.x_ready, HB)
            loaded(pe, "l3")
            transposes("down3T", [down3[:, k, :] for k in range(4)], 128, 128)

        def mixture_weights():
            transposes("up3T", [up3[:, 2 * k:2 * k + 2, :].rearrange("p e c -> p (e c)") for k in range(4)], 128, 128)
            transposes("gate3T", [gate3[:]], E0, 128)

        attention_tensor(at1, {NU + 5: x1_half, NU + 8: mixture_weights})

        transposed_half("x1T", 1, X[1], at1.x_ready, HB)
        pe.wait_ge(event("w2_centred"), 2)
        for c in range(2):
            aring.wait_copied(pe, f"x1T.{c}")
            row_products(dring, f"q2.{c}", [xT[:, b, :] for b in range(c * HB, (c + 1) * HB)], Wq2[:])
        pe.wait_ge(event("kn_ready"), 1)
        for c in range(2):
            transposes(f"k2.{c}", [sq[0:NC, b, :] for b in range(c * HB, (c + 1) * HB)], NC, 128)
        pe.wait_ge(event("v_ones"), 2)
        pe.wait_ge(event("qn_ready"), 1)
        for c in range(2):
            transposes(f"q2T.{c}", [sq[:, b, :] for b in range(c * HB, (c + 1) * HB)], 128, 128)

        def hidden(c, ts):
            if c:
                dring.wait_copied(pe, "x2T.1")
            else:
                aring.wait_copied(pe, "x2T.0")
            for t in ts:
                product(aring, f"hid.{t}.{c}", down3T[:, t * 128:(t + 1) * 128], half(xT, c))

        attention_tensor(at2, {NU + 5: lambda: transposed_half("x2T", 0, X[0], at2.x_ready, HB),
                               NU + 9: lambda: hidden(0, range(4))})

        transposed_half("x2T", 1, X[0], at2.x_ready, HB, dring)
        pe.wait_ge(event("pooled"), 2)
        product(dring, "logits8", pooledT[:], gate3T[:], 8, 8)
        hidden(1, (0, 1))
        pe.wait_ge(event("c8_ready"), 1)
        i = fill(dring, "cT")
        nc.tensor.transpose(PS[0:8, i, 0:8], c8[:], ident[0:8, 0:8]).then_inc(dring.full, 1)
        dring.wait_copied(pe, "cT")
        i = fill(dring, "cexp")
        for t in range(4):
            ins = M_(PS[:, i, t * B:(t + 1) * B], spread8[:, t * 128:(t + 1) * 128], cT[0:E0], start=True, stop=True)
        ins.then_inc(dring.full, 1)
        hidden(1, (2, 3))
        for c in range(2):
            pe.wait_ge(event("hid_scaled"), 4 * (c + 1))
            i = fill(dring, f"up.{c}")
            for b4 in range(HB):
                b = c * HB + b4
                dst = PS[:, i, b4 * D:(b4 + 1) * D]
                for t in range(4):
                    M_(dst, hid[:, t, b * T:(b + 1) * T], up3T[:, t, :], start=(t == 0), stop=False)
                ins = M_(dst, cT[:, b:b + 1].to_broadcast([128, 128]), upb3[:], start=False, stop=True)
            ins.then_inc(dring.full, 1)

        loaded(pe, "l4")
        x_transposed("xnT", XH, event("xh4"), 1)
        for c in range(2):
            aring.wait_copied(pe, f"xnT.{c}")
            product(aring, f"router.{c}", rw1[:], half(xT, c), rows=D // 2)
        for c in range(2):
            aring.wait_copied(pe, f"router.{c}")
            product(aring, f"srow.{c}", rw2[:].to_broadcast([D // 2, 128]), half(hrT, c))
        aring.wait_copied(pe, "srow.1")
        i = fill(dring, "scol")
        for b in range(B):
            ins = nc.tensor.transpose(PS[:, i, b:b + 1], Srow[0:1, b, :], ident[0:1, 0:1])
        ins.then_inc(dring.full, 1)
        loaded(pe, "l5")
        transposes("W5T", [W5[:, k, :] for k in range(4)], 128, 128)
        loaded(pe, "ssm")
        i = fill(aring, "xprojT")
        for h in range(NH):
            ins = nc.tensor.transpose(PS[0:DTR, i, h * 128:(h + 1) * 128], xproj[:, h, 0:DTR], ident[:])
        ins.then_inc(aring.full, 1)
        aring.wait_copied(pe, "xprojT")
        for h in range(NH):
            product(aring, f"Wdt.{h}", xprojT[:, h, :], dtw[:], cols=DIN)
        aring.wait_copied(pe, "W5T")
        for c in range(2):
            product(aring, f"k5.{c}", W5T[:, 1, :], half(ctxT, c), cols=HB * NC)
        pe.wait_ge(event("unsel"), 1)
        product(dring, "cumU", after[:], unsel[:], cols=B)
        for c in range(2):
            row_products(aring, f"v5.{c}", [ctxT[:, b, :] for b in range(c * HB, (c + 1) * HB)], W5T[:, 2, :], NC)
        pe.wait_ge(event("perm"), 1)
        for c in range(2):
            i = fill(aring, f"xpT.{c}")
            for b4 in range(HB):
                ins = M_(PS[:, i, b4 * T:(b4 + 1) * T], XH[:, c * HB + b4, :], Perm[:, c * HB + b4, :], start=True, stop=True)
            ins.then_inc(aring.full, 1)
        loaded(pe, "ssm")
        pe.wait_ge(event("ssm_weights"), 1)
        aring.wait_copied(pe, "xpT.1")
        W384 = HB * TS
        chosen = xpT[:, :, DC - 1 + TS:]
        product(aring, "qa", Wqkvo4[:, 0, :], chosen, cols=B * KSEL)
        product(aring, "ka", Wqkvo4[:, 1, :], chosen, cols=B * KSEL)
        i = fill(dring, "va")
        for b in range(B):
            n, c = b // 4, b % 4
            ins = M_(PS[32 * c:32 * c + 32, i, n * D:(n + 1) * D], chosen[:, b, :], Wqkvo4[:, 2, :], start=True, stop=True)
        ins.then_inc(dring.full, 1)
        for c in range(2):
            transposes(f"permT.{c}", [Perm[:, b, :] for b in range(c * HB, (c + 1) * HB)], 128, 128)

        def conv(h, c):
            i = fill(aring, f"conv.{h}.{c}")
            for j in range(DC):
                ins = M_(PS[:, i, 0:W384], convin[:, j, 128 * h:128 * h + 128],
                         xpT[:, c * HB:(c + 1) * HB, j:j + TS], start=(j == 0), stop=(j == DC - 1))
            ins.then_inc(aring.full, 1)

        conv(0, 0)
        dring.drain(pe)
        aring.wait_copied(pe, "ka")
        pe.wait_ge(event("qa_copies"), 1)
        for g in range(G):
            for b in range(B):
                n, c = b // 4, b % 4
                ins = M_(PS[32 * c:32 * c + 32, 4 + g, n * 128:(n + 1) * 128].rearrange("p (j k) -> p j k", j=J),
                         qGa[:, g, b, :], kMa[:, :, b, :], start=True, stop=True)
        ins.then_inc(event("sa_ready"), 1)
        conv(0, 1)
        for c in range(2):
            conv(1, c)
        aring.wait_copied(pe, "conv.1.1")
        pe.wait_ge(event("pa_shifted"), 1)
        for c in range(2):
            w = slice(c * W384, (c + 1) * W384)
            i = fill(dring, f"BC.{c}")
            for h in range(NH):
                ins = M_(PS[0:96, i, 0:W384], xprojBC[:, h, :], xc[:, h, w], start=(h == 0), stop=(h == NH - 1))
            ins.then_inc(dring.full, 1)
        for h in range(NH):
            for c in range(2):
                i = fill(aring, f"delta.{h}.{c}")
                for k in range(NH):
                    ins = M_(PS[:, i, 0:W384], Wdt[:, k, 128 * h:128 * h + 128], xc[:, k, c * W384:(c + 1) * W384],
                             start=(k == 0), stop=(k == NH - 1))
                ins.then_inc(aring.full, 1)
        pe.wait_ge(event("paT"), 1)
        dring.drain(pe)
        for n in range(2):
            for c in range(4):
                r = slice(32 * c, 32 * c + 32)
                for g in range(G):
                    ins = M_(PS[32 * g:32 * g + 32, 4 + c, n * 128:(n + 1) * 128].rearrange("p (j q) -> p j q", j=J),
                             va[r, n, 32 * g:32 * g + 32], PaT[r, 8 * g + 4 * n:8 * g + 4 * n + 4, :], start=True, stop=True)
        ins.then_inc(event("oa_ready"), 1)
        for h in range(NH):
            for c in range(2):
                product(aring, f"z.{h}.{c}", inw4[:, DIN + 128 * h:DIN + 128 * h + 128],
                        xpT[:, c * HB:(c + 1) * HB, DC - 1:DC - 1 + TS], cols=W384)
        pe.wait_ge(event("oa_masked"), 1)
        pe.wait_ge(event("bc_parts"), 1)

        def y_start():
            aring.drain(pe)
            for h in range(NH):
                for c in range(2):
                    M_(PS[:, 2 * h + c, 0:W384], diagD[:, h, :], xc[:, h, c * W384:(c + 1) * W384], start=True, stop=False)

        def spread(s):
            for k, (copied, ready) in enumerate((("b_copied", "b_ready"), ("c_copied", "c_ready"))):
                if s:
                    pe.wait_ge(event(copied), s)
                for c in range(2):
                    ins = M_(PS[:, 4 + 2 * k + c, 0:W384], part_pick[:, DS * k + s:DS * k + s + 1].to_broadcast([96, 128]),
                             BC3[:, c * W384:(c + 1) * W384], start=True, stop=True)
                ins.then_inc(event(ready), 1)

        def accumulate(s):
            for h in range(NH):
                n = NH * s + h
                if n < NH * DS - 1:
                    pe.wait_ge(event("hC_ready"), n + 1)
                else:
                    pe.wait_ge(event("last_hC_ready"), 1)
                for c in range(2):
                    ins = M_(PS[:, 2 * h + c, 0:W384], ident[:], hC[n % NHC][:, c * W384:(c + 1) * W384], start=False,
                             stop=(s == DS - 1))
                ins.then_inc(event("hC_used"), 1)

        for s in range(DS):
            spread(s)
            if s == 0:
                y_start()
            if s >= 2:
                accumulate(s - 2)
        accumulate(DS - 2)
        accumulate(DS - 1)
        pe.wait_ge(event("b_copied"), DS)
        pe.wait_ge(event("c_copied"), DS)
        pe.wait_ge(event("oaT_ready"), 1)
        for c in range(2):
            i = fill(dring, f"dposA.{c}")
            for b4 in range(HB):
                ins = M_(PS[TS:T, i, b4 * D:(b4 + 1) * D], oaT[:, c, 32 * b4:32 * b4 + 32], Wqkvo4[:, 3, :],
                         start=True, stop=True)
            ins.then_inc(dring.full, 1)
        pe.wait_ge(event("y_gated"), NH)
        for c in range(2):
            i = fill(dring, f"dposS.{c}")
            for b4 in range(HB):
                b = c * HB + b4
                for h in range(NH):
                    ins = M_(PS[0:TS, i, b4 * D:(b4 + 1) * D], xc[:, h, b * TS:(b + 1) * TS], outw4[:, h, :],
                             start=(h == 0), stop=(h == NH - 1))
            ins.then_inc(dring.full, 1)
        for c in range(2):
            dring.wait_copied(pe, f"dposS.{c}")
            i = fill(dring, f"dl.{c}")
            for b4 in range(HB):
                b = c * HB + b4
                ins = M_(PS[:, i, b4 * D:(b4 + 1) * D], PermT[:, b, :], dpos[:, b, :], start=True, stop=True)
            ins.then_inc(dring.full, 1)

        x_transposed("x4T", X[0], event("x4"), 1)
        for c in range(2):
            aring.wait_copied(pe, f"x4T.{c}")
            product(aring, f"q5.{c}", W5T[:, 0, :], half(xT, c))

        def gate_up(e, c):
            for i in range(NI):
                n = e * NI * 2 + NI * c + i
                if n >= 2:
                    pe.wait_ge(event("silu_ready"), n - 1)
                M_(PS[:, n % 2, :], Wg6[:, e, i * 128:(i + 1) * 128], half(xT, c), start=True, stop=True)\
                    .then_inc(event("gate_ready"), 1)
                if n >= 2:
                    pe.wait_ge(event("hidden_ready"), n - 1)
                M_(PS[:, 2 + n % 2, :], Wu6[:, e, i * 128:(i + 1) * 128], half(xT, c), start=True, stop=True)\
                    .then_inc(event("up_ready"), 1)

        def first_expert():
            pe.wait_ge(experts_loaded, 3 * 16)
            aring.drain(pe)
            gate_up(0, 0)

        pe.wait_ge(event("v_ones"), 3)
        attention_tensor(at5, {NU + 5: lambda: transposed_half("x5T", 0, X[1], at5.x_ready, HB), NU + 9: first_expert})

        loaded(pe, "g6")
        transposed_half("x5T", 1, X[1], at5.x_ready, HB, dring)
        dring.wait_copied(pe, "x5T.1")
        gate_up(0, 1)
        row_products(dring, "logits6", [xT[:, b, :] for b in range(B)], gate6[:], width=E1)

        def down(e):
            for c in range(2):
                if 2 * e + c >= 4:
                    pe.wait_ge(event("summed"), B * (e - 2) + HB * (c + 1))
                pe.wait_ge(event("hidden_ready"), NI * 2 * (e + 1))
                for b4 in range(HB):
                    b = c * HB + b4
                    for i in range(NI):
                        ins = M_(PS[:, 4 + (2 * e + c) % 4, b4 * D:(b4 + 1) * D], hidE[e % 2][:, i, b * T:(b + 1) * T],
                                 Wd6[:, NI * e + i, :], start=(i == 0), stop=(i == NI - 1))
                ins.then_inc(event("down_ready"), 1)

        for e in range(1, E1):
            for c in range(2):
                gate_up(e, c)
            if e == 1:
                dring.drain(pe)
            down(e - 1)
        down(E1 - 1)


_INS = [
    'x', 'ctx_1024', 'mask_1x1xSxS2_bk1', 'L0_attn_ln_gamma', 'L0_attn_ln_beta', 'L0_attn_w_qkv', 'L0_attn_b_qkv',
    'L0_attn_w_out', 'L0_attn_b_out', 'L0_xattn_Wq', 'L0_xattn_Wkv', 'L0_xattn_Wp', 'L0_xattn_bp',
    'L0_xattn_ln_g', 'L0_xattn_ln_b', 'L0_ffn_gate_w', 'L0_ffn_down_w', 'L0_ffn_down_b', 'L0_ffn_up_w',
    'L0_ffn_up_b', 'L1_attn_ln_w', 'L1_attn_ln_b', 'L1_attn_r_w1', 'L1_attn_r_b1', 'L1_attn_r_w2', 'L1_attn_r_b2',
    'L1_attn_Wq', 'L1_attn_bq', 'L1_attn_Wk', 'L1_attn_bk', 'L1_attn_Wv', 'L1_attn_bv', 'L1_attn_Wo',
    'L1_attn_bo', 'L1_attn_in_w', 'L1_attn_conv_w', 'L1_attn_conv_b', 'L1_attn_xproj_w', 'L1_attn_dt_w',
    'L1_attn_dt_b', 'L1_attn_A_log', 'L1_attn_Dp', 'L1_attn_out_w', 'L1_xattn_W_q', 'L1_xattn_W_k',
    'L1_xattn_W_v', 'L1_xattn_W_o', 'L1_ffn_gate_w', 'L1_ffn_Wg', 'L1_ffn_Wu', 'L1_ffn_Wd',
]
_SHAPE = (B, T, D)


def kernel(**inputs):
    import concourse.bacc as _bacc
    from concourse.bass_utils import run_bass_kernel_spmd as _run

    nc = _bacc.Bacc("TRN2", target_bir_lowering=False, num_devices=1)
    arrays, args = {}, {}
    for name in _INS:
        x = np.ascontiguousarray(inputs[name])
        if x.dtype.kind == "b":
            x = x.reshape(-1).view(np.int32)
        arrays[f"in_{name}"] = x
        args[name] = nc.dram_tensor(f"in_{name}", x.shape, mybir.dt.from_np(x.dtype), kind="ExternalInput").ap()
    out = nc.dram_tensor("out_x", _SHAPE, F32, kind="ExternalOutput").ap()
    build(nc, args, out)
    return _run(nc, [arrays], core_ids=[0]).results[0]["out_x"]
```
